# Optimizing a Trainium2 kernel written in Bass

```python
import numpy as np
import jax
import jax.numpy as jnp

def _softmax(x, axis=-1):
    return jax.nn.softmax(x, axis=axis)

def _gelu(x):
    return jax.nn.gelu(x, approximate=True)

def _silu(x):
    return jax.nn.silu(x)

def _sigmoid(x):
    return jax.nn.sigmoid(x)

def _layernorm(x, axis=-1, eps=1e-05):
    m = jnp.mean(x, axis=axis, keepdims=True)
    v = jnp.var(x, axis=axis, keepdims=True)
    return (x - m) / jnp.sqrt(v + eps)

def _scatter_add(tgt, idx, src, axis=0):
    return tgt.at[idx].add(src)

def _segment_sum(src, seg, n):
    return jax.ops.segment_sum(src, seg, n)
kernel_name = 'mk_seq_postln_d2_jaxref_r8_070d94'

def setup_inputs(seed: int=0):
    np.random.seed(seed)
    _w = jnp.asarray

    def _L0_attn_setup():
        import jax, jax.numpy as jnp
        import numpy as np
        DIM = 128
        HEADS = 16
        HEAD_DIM = 64
        key = jax.random.key(seed)
        ks = jax.random.split(key, 6)
        inner = HEADS * HEAD_DIM
        s = 0.02
        return {'x': jax.random.normal(ks[0], (2, 256, DIM), dtype=jnp.float32), 'Wq': jax.random.normal(ks[1], (DIM, inner), dtype=jnp.float32) * s, 'Wk': jax.random.normal(ks[2], (DIM, inner), dtype=jnp.float32) * s, 'Wv': jax.random.normal(ks[3], (DIM, inner), dtype=jnp.float32) * s, 'Wo': jax.random.normal(ks[4], (inner, DIM), dtype=jnp.float32) * s, 'bo': jax.random.normal(ks[5], (DIM,), dtype=jnp.float32) * s}
    _L0_attn_in = _L0_attn_setup()

    def _L0_ffn_setup():
        import jax, jax.numpy as jnp
        import numpy as np
        EPS = 1e-05

        def _quantize(W):
            gamma = jnp.mean(jnp.abs(W))
            return jnp.clip(jnp.round(W / (gamma + EPS)), -1.0, 1.0)
        key = jax.random.key(seed)
        k_x, k_w1, k_b1, k_w2, k_b2 = jax.random.split(key, 5)
        n_embd = 128
        d_ff = 4 * n_embd
        B, S = (4, 512)
        bound1 = 1.0 / np.sqrt(n_embd)
        bound2 = 1.0 / np.sqrt(d_ff)
        x = jax.random.normal(k_x, (B, S, n_embd), dtype=jnp.float32)
        W1 = jax.random.uniform(k_w1, (d_ff, n_embd), jnp.float32, -bound1, bound1)
        b1 = jax.random.uniform(k_b1, (d_ff,), jnp.float32, -bound1, bound1)
        W2 = jax.random.uniform(k_w2, (n_embd, d_ff), jnp.float32, -bound2, bound2)
        b2 = jax.random.uniform(k_b2, (n_embd,), jnp.float32, -bound2, bound2)
        return {'x': x, 'W1': W1, 'b1': b1, 'W2': W2, 'b2': b2}
    _L0_ffn_in = _L0_ffn_setup()

    def _L1_attn_setup():
        import jax, jax.numpy as jnp
        import numpy as np
        NUM_HEADS = 16
        DIM = 128
        HEAD_DIM = DIM // 2 // NUM_HEADS
        SCALE = HEAD_DIM ** (-0.5)
        NBITS_W = 4
        NBITS_ATT = 8

        def round_ste(x):
            return x + jax.lax.stop_gradient(jnp.round(x) - x)

        def quant_weight(w, alpha, nbits):
            qn, qp = (-2 ** (nbits - 1), 2 ** (nbits - 1) - 1)
            return round_ste(jnp.clip(w / alpha, qn, qp)) * alpha

        def quant_act(x, alpha, zp, nbits):
            qn, qp = (-2 ** (nbits - 1), 2 ** (nbits - 1) - 1)
            zp_r = round_ste(zp)
            xq = round_ste(jnp.clip(x / alpha + zp_r, qn, qp))
            return (xq - zp_r) * alpha
        key = jax.random.key(seed)
        ks = jax.random.split(key, 9)
        B, N = (8, 128)
        x = jax.random.normal(ks[0], (B, N, DIM), jnp.float32)
        qkv_w = jax.random.normal(ks[1], (DIM // 2 * 3, DIM), jnp.float32) * 0.02
        proj_w = jax.random.normal(ks[2], (DIM, DIM // 2), jnp.float32) * 0.02
        proj_b = jnp.zeros((DIM,), jnp.float32)
        qkv_alpha = 0.05 + 0.1 * jax.random.uniform(ks[3], (DIM // 2 * 3, 1), jnp.float32)
        proj_alpha = 0.05 + 0.1 * jax.random.uniform(ks[4], (DIM, 1), jnp.float32)
        bias_q = jnp.zeros((1, NUM_HEADS, 1, 1), jnp.float32)
        bias_k = jnp.zeros((1, NUM_HEADS, 1, 1), jnp.float32)

        def act_params(k):
            a = 0.05 + 0.1 * jax.random.uniform(k, (1, NUM_HEADS, 1, 1), jnp.float32)
            z = jnp.zeros((1, NUM_HEADS, 1, 1), jnp.float32)
            return (a, z)
        q_alpha, q_zp = act_params(ks[5])
        k_alpha, k_zp = act_params(ks[6])
        v_alpha, v_zp = act_params(ks[7])
        attn_alpha, attn_zp = act_params(ks[8])
        return dict(x=x, qkv_w=qkv_w, qkv_alpha=qkv_alpha, bias_q=bias_q, bias_k=bias_k, q_alpha=q_alpha, q_zp=q_zp, k_alpha=k_alpha, k_zp=k_zp, v_alpha=v_alpha, v_zp=v_zp, attn_alpha=attn_alpha, attn_zp=attn_zp, proj_w=proj_w, proj_b=proj_b, proj_alpha=proj_alpha)
    _L1_attn_in = _L1_attn_setup()

    def _L1_ffn_setup():
        import jax, jax.numpy as jnp
        import numpy as np
        B, S, D, H, E = (8, 256, 128, 512, 16)
        key = jax.random.key(seed)
        ks = jax.random.split(key, 4)
        sd = 1.0 / np.sqrt(D).astype(np.float32)
        sh = 1.0 / np.sqrt(H).astype(np.float32)
        return {'x': jax.random.normal(ks[0], (B, S, D), jnp.float32), 'Wg': jax.random.normal(ks[1], (D, E), jnp.float32) * sd, 'bg': jnp.zeros((E,), jnp.float32), 'W1': jax.random.normal(ks[2], (E, D, H), jnp.float32) * sd, 'b1': jnp.zeros((E, H), jnp.float32), 'W2': jax.random.normal(ks[3], (E, H, D), jnp.float32) * sh, 'b2': jnp.zeros((E, D), jnp.float32)}
    _L1_ffn_in = _L1_ffn_setup()
    _d = {'L0_attn_x': _L0_attn_in['x'], 'L0_attn_Wq': _L0_attn_in['Wq'], 'L0_attn_Wk': _L0_attn_in['Wk'], 'L0_attn_Wv': _L0_attn_in['Wv'], 'L0_attn_Wo': _L0_attn_in['Wo'], 'L0_attn_bo': _L0_attn_in['bo'], 'L0_ffn_W1': _L0_ffn_in['W1'], 'L0_ffn_b1': _L0_ffn_in['b1'], 'L0_ffn_W2': _L0_ffn_in['W2'], 'L0_ffn_b2': _L0_ffn_in['b2'], 'L1_attn_qkv_w': _L1_attn_in['qkv_w'], 'L1_attn_qkv_alpha': _L1_attn_in['qkv_alpha'], 'L1_attn_bias_q': _L1_attn_in['bias_q'], 'L1_attn_bias_k': _L1_attn_in['bias_k'], 'L1_attn_q_alpha': _L1_attn_in['q_alpha'], 'L1_attn_q_zp': _L1_attn_in['q_zp'], 'L1_attn_k_alpha': _L1_attn_in['k_alpha'], 'L1_attn_k_zp': _L1_attn_in['k_zp'], 'L1_attn_v_alpha': _L1_attn_in['v_alpha'], 'L1_attn_v_zp': _L1_attn_in['v_zp'], 'L1_attn_attn_alpha': _L1_attn_in['attn_alpha'], 'L1_attn_attn_zp': _L1_attn_in['attn_zp'], 'L1_attn_proj_w': _L1_attn_in['proj_w'], 'L1_attn_proj_b': _L1_attn_in['proj_b'], 'L1_attn_proj_alpha': _L1_attn_in['proj_alpha'], 'L1_ffn_Wg': _L1_ffn_in['Wg'], 'L1_ffn_bg': _L1_ffn_in['bg'], 'L1_ffn_W1': _L1_ffn_in['W1'], 'L1_ffn_b1': _L1_ffn_in['b1'], 'L1_ffn_W2': _L1_ffn_in['W2'], 'L1_ffn_b2': _L1_ffn_in['b2']}
    _x0 = _d['L0_attn_x']
    _d['L0_attn_x'] = jax.random.normal(jax.random.fold_in(jax.random.key(seed), 1), (1, 2048, 128), dtype=_x0.dtype)
    del _x0
    return _d

def reference(L0_attn_x, L0_attn_Wq, L0_attn_Wk, L0_attn_Wv, L0_attn_Wo, L0_attn_bo, L0_ffn_W1, L0_ffn_b1, L0_ffn_W2, L0_ffn_b2, L1_attn_qkv_w, L1_attn_qkv_alpha, L1_attn_bias_q, L1_attn_bias_k, L1_attn_q_alpha, L1_attn_q_zp, L1_attn_k_alpha, L1_attn_k_zp, L1_attn_v_alpha, L1_attn_v_zp, L1_attn_attn_alpha, L1_attn_attn_zp, L1_attn_proj_w, L1_attn_proj_b, L1_attn_proj_alpha, L1_ffn_Wg, L1_ffn_bg, L1_ffn_W1, L1_ffn_b1, L1_ffn_W2, L1_ffn_b2):

    def _L0_attn_ref(x, Wq, Wk, Wv, Wo, bo):
        import jax, jax.numpy as jnp
        import numpy as np
        DIM = 128
        HEADS = 16
        HEAD_DIM = 64
        N, S, _ = x.shape
        scale = 1.0 / np.sqrt(HEAD_DIM).astype(np.float32)
        q = (x @ Wq).reshape(N, S, HEADS, HEAD_DIM).transpose(0, 2, 1, 3)
        k = (x @ Wk).reshape(N, S, HEADS, HEAD_DIM).transpose(0, 2, 1, 3)
        v = (x @ Wv).reshape(N, S, HEADS, HEAD_DIM).transpose(0, 2, 1, 3)
        logits = jnp.einsum('nhid,nhjd->nhij', q, k) * scale
        causal = 1000000000.0 * (jnp.tril(jnp.ones((S, S), dtype=logits.dtype)) - 1.0)
        logits = logits + causal[None, None, :, :]
        attn = jax.nn.softmax(logits, axis=-1)
        out = jnp.einsum('nhij,nhjd->nhid', attn, v)
        out = out.transpose(0, 2, 1, 3).reshape(N, S, HEADS * HEAD_DIM)
        return out @ Wo + bo

    def _L0_ffn_ref(x, W1, b1, W2, b2):
        import jax, jax.numpy as jnp
        import numpy as np
        EPS = 1e-05

        def _quantize(W):
            gamma = jnp.mean(jnp.abs(W))
            return jnp.clip(jnp.round(W / (gamma + EPS)), -1.0, 1.0)
        Wq1 = _quantize(W1)
        Wq2 = _quantize(W2)
        h = jax.nn.relu(jnp.einsum('bsd,fd->bsf', x, Wq1) + b1)
        out = jnp.einsum('bsf,df->bsd', h, Wq2) + b2
        return out

    def _L1_attn_ref(x, qkv_w, qkv_alpha, bias_q, bias_k, q_alpha, q_zp, k_alpha, k_zp, v_alpha, v_zp, attn_alpha, attn_zp, proj_w, proj_b, proj_alpha):
        import jax, jax.numpy as jnp
        import numpy as np
        NUM_HEADS = 16
        DIM = 128
        HEAD_DIM = DIM // 2 // NUM_HEADS
        SCALE = HEAD_DIM ** (-0.5)
        NBITS_W = 4
        NBITS_ATT = 8

        def round_ste(x):
            return x + jax.lax.stop_gradient(jnp.round(x) - x)

        def quant_weight(w, alpha, nbits):
            qn, qp = (-2 ** (nbits - 1), 2 ** (nbits - 1) - 1)
            return round_ste(jnp.clip(w / alpha, qn, qp)) * alpha

        def quant_act(x, alpha, zp, nbits):
            qn, qp = (-2 ** (nbits - 1), 2 ** (nbits - 1) - 1)
            zp_r = round_ste(zp)
            xq = round_ste(jnp.clip(x / alpha + zp_r, qn, qp))
            return (xq - zp_r) * alpha
        B, N, C2 = x.shape
        C = C2 // 2
        wq = quant_weight(qkv_w, qkv_alpha, NBITS_W)
        qkv = jnp.einsum('bnc,oc->bno', x, wq)
        qkv = qkv.reshape(B, N, 3, NUM_HEADS, C // NUM_HEADS).transpose(2, 0, 3, 1, 4)
        q = qkv[0] + bias_q
        k = qkv[1] + bias_k
        v = qkv[2]
        q = quant_act(q, q_alpha, q_zp, NBITS_W) * SCALE
        k = quant_act(k, k_alpha, k_zp, NBITS_W)
        v = quant_act(v, v_alpha, v_zp, NBITS_W)
        attn = jnp.einsum('bhnd,bhmd->bhnm', q, k)
        attn = jax.nn.softmax(attn, axis=-1)
        attn = quant_act(attn, attn_alpha, attn_zp, NBITS_ATT)
        out = jnp.einsum('bhnm,bhmd->bhnd', attn, v)
        out = out.transpose(0, 2, 1, 3).reshape(B, N, C)
        wp = quant_weight(proj_w, proj_alpha, NBITS_W)
        return jnp.einsum('bnc,oc->bno', out, wp) + proj_b

    def _L1_ffn_ref(x, Wg, bg, W1, b1, W2, b2):
        import jax, jax.numpy as jnp
        import numpy as np
        B, S, D, H, E = (8, 256, 128, 512, 16)
        d = x.shape[-1]
        xf = x.reshape(-1, d)
        n_tok = xf.shape[0]
        n_exp = Wg.shape[1]
        cap = -(-n_tok // n_exp)
        score = jax.nn.softmax(xf @ Wg + bg, axis=-1)
        gate = jnp.max(score, axis=-1)
        idx = jnp.argmax(score, axis=-1)
        onehot = jax.nn.one_hot(idx, n_exp, dtype=jnp.int32)
        pos = jnp.sum((jnp.cumsum(onehot, axis=0) - 1) * onehot, axis=-1)
        keep = pos < cap
        safe_pos = jnp.where(keep, pos, cap - 1)
        buf = jnp.zeros((n_exp, cap, d), x.dtype).at[idx, safe_pos].add(jnp.where(keep[:, None], xf, 0.0))
        h = jax.nn.relu(jnp.einsum('ecd,edh->ech', buf, W1) + b1[:, None, :])
        y = jnp.einsum('ech,ehd->ecd', h, W2) + b2[:, None, :]
        out = y[idx, safe_pos] * gate[:, None]
        out = jnp.where(keep[:, None], out, 0.0)
        return out.reshape(x.shape)
    x = L0_attn_x
    x = _layernorm(x + _L0_attn_ref(x, L0_attn_Wq, L0_attn_Wk, L0_attn_Wv, L0_attn_Wo, L0_attn_bo), axis=-1)
    x = _layernorm(x + _L0_ffn_ref(x, L0_ffn_W1, L0_ffn_b1, L0_ffn_W2, L0_ffn_b2), axis=-1)
    x = _layernorm(x + _L1_attn_ref(x, L1_attn_qkv_w, L1_attn_qkv_alpha, L1_attn_bias_q, L1_attn_bias_k, L1_attn_q_alpha, L1_attn_q_zp, L1_attn_k_alpha, L1_attn_k_zp, L1_attn_v_alpha, L1_attn_v_zp, L1_attn_attn_alpha, L1_attn_attn_zp, L1_attn_proj_w, L1_attn_proj_b, L1_attn_proj_alpha), axis=-1)
    x = _layernorm(x + _L1_ffn_ref(x, L1_ffn_Wg, L1_ffn_bg, L1_ffn_W1, L1_ffn_b1, L1_ffn_W2, L1_ffn_b2), axis=-1)
    return x

_drawn_inputs = setup_inputs


def setup_inputs(seed=0):
    import zlib

    import numpy as np

    out = dict(_drawn_inputs(seed))
    spreads = {'L1_attn_bias_q': (0.0, 0.1),
     'L1_attn_bias_k': (0.0, 0.1),
     'L1_attn_q_zp': (0.0, 0.1),
     'L1_attn_k_zp': (0.0, 0.1),
     'L1_attn_v_zp': (0.0, 0.1),
     'L1_attn_attn_zp': (0.0, 0.1),
     'L1_attn_proj_b': (0.0, 0.1),
     'L1_ffn_bg': (0.0, 0.1),
     'L1_ffn_b1': (0.0, 0.58),
     'L1_ffn_b2': (0.0, 0.408)}
    factors = {'L0_attn_Wq': 8.0,
     'L0_attn_Wk': 8.0,
     'L0_attn_Wv': 3.512,
     'L0_attn_Wo': 3.586,
     'L0_ffn_b1': 4.784,
     'L0_ffn_b2': 51.744}
    for name, (base, spread) in spreads.items():
        noise = np.random.default_rng([zlib.crc32(name.encode()), seed]).standard_normal(out[name].shape)
        drawn = base * np.exp(spread * noise) if base else spread * noise
        out[name] = jnp.asarray(drawn.astype(out[name].dtype))
    for name, factor in factors.items():
        out[name] = (out[name] * factor).astype(out[name].dtype)
    return out
```

```python
from contextlib import ExitStack

import numpy as np
import concourse.bass as bass
from concourse import mybir

F32 = mybir.dt.float32
F16 = mybir.dt.float16
BF16 = mybir.dt.bfloat16
I32 = mybir.dt.int32
U32 = mybir.dt.uint32
ALU = mybir.AluOpType
ACT = mybir.ActivationFunctionType
AX = mybir.AxisListType.X

P = 128
S = 2048
D = 128
TILES = S // P
HEADS = 16
HD = 64
PAIRS = HEADS // 2
GROUPS = TILES // 4
RAW_MASK = -8e9
EXP_SCALE = 1.0 / 8.0
VW = 2 * HD + 1
VSTRIDE = VW + 1
ACC = 256
RING = 4
LEAD = 2


class Unit:

    def __init__(self, group, pair):
        self.group = group
        first = 2 * pair
        self.first = pair == 0
        self.last = pair == 2 * group + 1
        r = [max(0, j - 4 * group) for j in (first, first + 1)]
        second = 512 if r[0] == 0 else (4 - r[0]) * P
        self.keys = [(first, r[0], 0), (first + 1, r[1], second)]
        self.width = second + (4 - r[1]) * P


UNITS = [Unit(g, p) for g in range(GROUPS) for p in range(2 * g + 2)]
NU = len(UNITS)
BODY = 2 * NU


def max_jobs(group):
    return [("max", group, r, c) for c in range(group + 1) for r in range(4)]


def job_plan():
    plan = [[] for _ in range(NU)]

    def put(step, ahead, jobs):
        plan[step] += [(ahead, j) for j in jobs]

    m0, m1, m2, m3 = max_jobs(0), max_jobs(1), max_jobs(2), max_jobs(3)
    put(0, 1, [("kq", 0)])
    put(0, 0, m3[0:1])
    put(1, 0, m3[1:3] + [("shift", 2)])
    put(2, 1, [("kq", 1)])
    put(2, 0, m3[3:5])
    put(3, 0, m3[5:7])
    put(4, 1, [("kq", 2)])
    put(4, 0, m3[7:9])
    put(5, 0, m3[9:11])
    put(6, 1, [("kq", 3)])
    put(6, 0, m3[11:13])
    put(7, 0, m3[13:16])
    put(9, 0, [("shift", 3)])
    put(9, 1, [("v", 0)])
    put(10, 1, [("v", 1)] + m0[0:2])
    put(11, 1, m0[2:4] + m1[0:1])
    put(12, 1, m1[1:4])
    put(13, 1, [("shift", 0)] + m1[4:6])
    put(14, 1, m1[6:8] + m2[0:1])
    put(15, 1, m2[1:3])
    put(16, 1, [("shift", 1)] + m2[3:5])
    put(17, 1, m2[5:7])
    put(18, 1, m2[7:10])
    put(19, 1, m2[10:12])
    return plan


PLAN = job_plan()
LAST_KQ = [(1, ("kq", 3)) in step for step in PLAN].index(True)
FIRST_JOBS = [what for step in PLAN for ahead, what in step if ahead]
JOBS_PER_TRIP = 2 * sum(len(p) for p in PLAN)
assert JOBS_PER_TRIP % 2 == 0


class Job:

    def __init__(self, index, trip, head, what):
        self.bank = index % 2
        self.before = index // 2 + (0 if trip is None else trip * (JOBS_PER_TRIP // 2))
        self.head = head
        self.side = head % 2
        self.kind = what[0]
        self.what = what
        self.trip = trip

    def heads_done(self):
        return self.head if self.trip is None else self.trip * 2 + self.head

    def shifts_done(self, group):
        return self.heads_done() * GROUPS + group


def jobs_of(trip, step):
    if step is None:
        return [Job(i, None, 0, w) for i, w in enumerate(FIRST_JOBS)]
    at = len(FIRST_JOBS)
    for s in range(step):
        at += len(PLAN[s % NU])
    return [Job(at + i, trip, step // NU + ahead, w) for i, (ahead, w) in enumerate(PLAN[step % NU])]


def shift_job(trip, head, group):
    if trip is None:
        return [j for j in jobs_of(None, None) if j.what == ("shift", group)][0], 0
    if group < 2 and head == 0:
        steps, head, back = range(NU, BODY), 2, JOBS_PER_TRIP // 2
    else:
        steps, back = range(BODY), 0
    for s in steps:
        for j in jobs_of(trip, s):
            if j.what == ("shift", group) and j.head == head:
                return j, back


class Memory:

    def __init__(self, nc, kept, ctx):
        def keep(name, shape, dt=F32):
            return kept.enter_context(nc.sbuf_tensor(name, shape, dt))

        def sb(name, shape, dt=F32):
            return ctx.enter_context(nc.sbuf_tensor(name, shape, dt))

        self.psum = kept.enter_context(nc.psum_tensor("psum", [P, 8, 512], F32))
        self.x = keep("x", [P, TILES, D])
        self.heads_out = keep("heads_out", [P, TILES, HEADS * HD])
        self.ident = keep("ident", [P, P])
        self.ident16 = keep("ident16", [P, P], F16)
        self.xt_hi = sb("xt_hi", [P, S], F16)
        self.xt_lo = sb("xt_lo", [P, S], F16)
        self.wkq_hi = sb("wkq_hi", [P, HEADS + 1, 2 * HD], F16)
        self.wkq_lo = sb("wkq_lo", [P, HEADS + 1, 2 * HD], F16)
        self.wv_hi = sb("wv_hi", [P, (HEADS + 1) * HD], F16)
        self.wv_lo = sb("wv_lo", [P, (HEADS + 1) * HD], F16)
        self.identb = sb("identb", [P, P], BF16)
        self.mask_ik = sb("mask_ik", [P, P], BF16)
        self.mask_ki = sb("mask_ki", [P, P], BF16)
        self.kq_hi = sb("kq_hi", [P, S], F16)
        self.kq_lo = sb("kq_lo", [P, S], F16)
        self.k_hh = [sb(f"k_hh{i}", [P, S], F16) for i in range(2)]
        self.q_hl = [sb(f"q_hl{i}", [P, S], F16) for i in range(2)]
        self.k_l1 = [sb(f"k_l1{i}", [HD + 1, S], F16) for i in range(2)]
        self.q_hm = [sb(f"q_hm{i}", [HD + 1, S], F16) for i in range(2)]
        self.v = [sb(f"v{i}", [P, TILES, VSTRIDE], F16) for i in range(2)]
        self.part_max = sb("part_max", [P, 2, 4, 4])
        self.neg_max = sb("neg_max", [P, 2, 4], F16)
        self.prob = [sb(f"prob{i}", [P, 1024]) for i in range(RING)]
        self.prob_hi = [sb(f"prob_hi{i}", [P, 1024], F16) for i in range(RING)]
        self.prob_lo = [sb(f"prob_lo{i}", [P, 1024], F16) for i in range(RING)]
        self.acc_copy = sb("acc_copy", [P, 2, 4, VW])
        self.acc_sum = sb("acc_sum", [P, 2, 4, HD])
        self.inv_sum = sb("inv_sum", [P, 2, 4, 1])
        self.scores = [self.psum[:, 2 * b:2 * b + 2, :].rearrange("p b n -> p (b n)") for b in range(2)]
        self.bank = [self.psum[:, 4 + b, :] for b in range(2)]
        self.acc = [self.psum[:, 6 + b, :] for b in range(2)]


def setup(nc, m, ins, sem):
    wraw = [m.heads_out[:, t, :] for t in range(3)]
    loaded, consts, turned, ready = sem("loaded"), sem("consts"), sem("turned"), sem("ready")
    x_loaded = sem("x_loaded")
    cast, moved = sem("cast"), sem("moved")
    with nc.Block() as block:

        @block.sync
        def _(sp):
            sp.dma_start(m.x[:], ins["L0_attn_x"].rearrange("a (t p) d -> p (a t) d", p=P)).then_inc(x_loaded, 16)
            for t, n in enumerate(("L0_attn_Wk", "L0_attn_Wq", "L0_attn_Wv")):
                sp.dma_start(wraw[t], ins[n]).then_inc(loaded, 16)

        @block.gpsimd
        def _(pool):
            pool.memset(m.ident[:], 0.0).then_inc(consts, 1)
            pool.memset(m.mask_ik[:], 0.0).then_inc(consts, 1)
            pool.memset(m.mask_ki[:], 0.0).then_inc(consts, 1)
            pool.wait_ge(consts, 3)
            pool.affine_select(out=m.ident[:], in_=m.ident[:], compare_op=ALU.not_equal, fill=1.0,
                               base=0, pattern=[[-1, P]], channel_multiplier=1).then_inc(consts, 1)
            pool.affine_select(out=m.mask_ik[:], in_=m.mask_ik[:], compare_op=ALU.is_ge, fill=RAW_MASK,
                               base=0, pattern=[[-1, P]], channel_multiplier=1).then_inc(consts, 1)
            pool.affine_select(out=m.mask_ki[:], in_=m.mask_ki[:], compare_op=ALU.is_ge, fill=RAW_MASK,
                               base=0, pattern=[[1, P]], channel_multiplier=-1).then_inc(consts, 1)
            pool.wait_ge(consts, 4)
            pool.tensor_scalar(m.ident16[:], m.ident[:], 1.0, None, ALU.mult).then_inc(consts, 1)
            pool.tensor_scalar(m.identb[:], m.ident[:], 1.0, None, ALU.mult).then_inc(consts, 1)
            for side in range(2):
                pool.memset(m.v[side][:, :, 2 * HD:VW], 1.0).then_inc(consts, 1)
            for w in (m.wkq_hi[:, HEADS, :], m.wkq_lo[:, HEADS, :], m.wv_hi[:, HEADS * HD:], m.wv_lo[:, HEADS * HD:]):
                pool.memset(w, 0.0).then_inc(consts, 1)

        @block.tensor
        def _(pe):
            pe.wait_ge(consts, 4)
            pe.wait_ge(x_loaded, 16)
            for b in range(4):
                for t in range(4):
                    last = pe.transpose(m.psum[:, b, t * P:(t + 1) * P], m.x[:, 4 * b + t, :], m.ident[:])
                last.then_inc(turned, 1)

        def heads_of(w):
            return w.rearrange("p (h d) -> p h d", d=HD)

        @block.scalar
        def _(act):
            for b in range(4):
                act.wait_ge(turned, b + 1)
                act.activation(m.xt_hi[:, b * 512:(b + 1) * 512], m.psum[:, b, :], ACT.Copy).then_inc(cast, 1)
            act.wait_ge(loaded, 48)
            act.activation(m.wkq_hi[:, 0:HEADS, 0:HD], heads_of(wraw[0]), ACT.Copy).then_inc(cast, 1)
            act.activation(m.wkq_hi[:, 0:HEADS, HD:2 * HD], heads_of(wraw[1]), ACT.Copy).then_inc(cast, 1)
            act.activation(m.wv_hi[:, 0:HEADS * HD], wraw[2], ACT.Copy).then_inc(cast, 1)

        @block.vector
        def _(dve):
            for side in range(2):
                dve.memset(m.k_l1[side][HD:HD + 1, :], 1.0).then_inc(moved, 1)
            for b in range(4):
                dve.wait_ge(cast, b + 1)
                c = slice(b * 512, (b + 1) * 512)
                dve.tensor_tensor(m.xt_lo[:, c], m.psum[:, b, :], m.xt_hi[:, c], ALU.subtract).then_inc(ready, 1)
            dve.wait_ge(loaded, 48)
            for t in range(2):
                dve.wait_ge(cast, 5 + t)
                c = slice(t * HD, (t + 1) * HD)
                dve.tensor_tensor(m.wkq_lo[:, 0:HEADS, c], heads_of(wraw[t]), m.wkq_hi[:, 0:HEADS, c],
                                  ALU.subtract).then_inc(ready, 1)
            dve.wait_ge(cast, 7)
            dve.tensor_tensor(m.wv_lo[:, 0:HEADS * HD], wraw[2], m.wv_hi[:, 0:HEADS * HD],
                              ALU.subtract).then_inc(ready, 1)


def attention(nc, m, sem):
    bank_full = [sem("bank_full0"), sem("bank_full1")]
    bank_free = [sem("bank_free0"), sem("bank_free1")]
    high_done = sem("high_done")
    low_done = sem("low_done")
    kq_spread = sem("kq_spread")
    neg_max_ready = sem("neg_max_ready")
    scores_full = sem("scores_full")
    exp_done = sem("exp_done")
    low_dve = sem("low_dve")
    low_pool = sem("low_pool")
    prob_free = sem("prob_free")
    acc_free = sem("acc_free")
    inv_ready = sem("inv_ready")
    sum_ready = sem("sum_ready")
    norm_done = sem("norm_done")

    def share(u):
        return u.width // 2

    def load_wait(engine, count):
        engine.wait_ge(kq_spread, 96 * count)

    with nc.Block() as block:

        @block.tensor
        def _(pe):
            def run(job):
                full, free = bank_full[job.bank], bank_free[job.bank]
                out = m.bank[job.bank]
                if job.trip is not None or job.before > 0:
                    pe.wait_ge(free, job.before)
                if job.kind == "kq":
                    c = slice(job.what[1] * 512, (job.what[1] + 1) * 512)
                    h = job.heads_done()
                    hi = m.wkq_hi[:, bass.ds(h, 1), :].rearrange("p a n -> p (a n)")
                    lo = m.wkq_lo[:, bass.ds(h, 1), :].rearrange("p a n -> p (a n)")
                    pe.matmul(out, hi, m.xt_hi[:, c], start=True, stop=False)
                    pe.matmul(out, hi, m.xt_lo[:, c], start=False, stop=False)
                    pe.matmul(out, lo, m.xt_hi[:, c], start=False, stop=True).then_inc(full, 1)
                elif job.kind == "v":
                    h = job.heads_done()
                    hi = m.wv_hi[:, bass.ds(h * HD, HD)]
                    lo = m.wv_lo[:, bass.ds(h * HD, HD)]
                    for t in range(8):
                        tok = slice((8 * job.what[1] + t) * P, (8 * job.what[1] + t + 1) * P)
                        o = out[:, t * HD:(t + 1) * HD]
                        pe.matmul(o, m.xt_hi[:, tok], hi, start=True, stop=False)
                        pe.matmul(o, m.xt_hi[:, tok], lo, start=False, stop=False)
                        last = pe.matmul(o, m.xt_lo[:, tok], hi, start=False, stop=True)
                    last.then_inc(full, 1)
                elif job.kind == "max":
                    _, g, r, c = job.what
                    if (g, r, c) == (0, 0, 0):
                        load_wait(pe, job.heads_done() + 1)
                    tile = 4 * g + r
                    q = m.q_hl[job.side][0:HD, tile * P:(tile + 1) * P]
                    width = 512 if c < g else (r + 1) * P
                    k = m.k_hh[job.side][0:HD, c * 512:c * 512 + width]
                    last = pe.matmul(out[:, 0:width], q, k, start=True, stop=(c < g))
                    if c == g:
                        last = pe.matmul(out[:, width - P:width], m.identb[:], m.mask_ik[:],
                                         start=False, stop=True)
                    last.then_inc(full, 1)
                else:
                    g = job.what[1]
                    pe.wait_ge(neg_max_ready, job.shifts_done(g) + 1)
                    for r in range(4):
                        last = pe.matmul(out[0:1, r * P:(r + 1) * P], m.neg_max[:, g % 2, r:r + 1],
                                         m.ident16[:], start=True, stop=True)
                    last.then_inc(full, 1)

            def scores(trip, s):
                u, head = UNITS[s % NU], s // NU
                out = m.scores[s % 2]
                units = s if trip is None else trip * BODY + s
                if trip is not None or s >= 2:
                    pe.wait_ge(exp_done, units - 1)
                if u.first:
                    job, back = shift_job(trip, head, u.group)
                    pe.wait_ge(bank_free[job.bank], job.before - back + 1)
                side = head % 2
                for j, r, col in u.keys:
                    n = (4 - r) * P
                    o = out[:, col:col + n]
                    keys = slice(j * P, (j + 1) * P)
                    queries = slice((4 * u.group + r) * P, (4 * u.group + 4) * P)
                    pe.matmul(o, m.k_hh[side][:, keys], m.q_hl[side][:, queries], start=True, stop=False)
                    if j >= 4 * u.group:
                        pe.matmul(o[:, 0:P], m.identb[:], m.mask_ki[:], start=False, stop=False)
                    last = pe.matmul(o, m.k_l1[side][:, keys], m.q_hm[side][:, queries], start=False, stop=True)
                last.then_inc(scores_full, 1)

            def weigh(trip, s):
                u, side = UNITS[s % NU], s // NU
                pe.wait_ge(low_dve, trip * BODY + s + 1)
                pe.wait_ge(low_pool, trip * BODY + s + 1)
                if u.first:
                    pe.wait_ge(acc_free, trip * 2 * GROUPS + side * GROUPS + u.group + 1)
                for j, first, col in u.keys:
                    for r in range(first, 4):
                        c = slice(col + (r - first) * P, col + (r - first + 1) * P)
                        a = (r % 2) * ACC
                        o = m.acc[r // 2][:, a:a + VW]
                        pe.matmul(o, m.prob_hi[s % RING][:, c], m.v[side][:, j, 0:VW],
                                  start=(j == 0 and r % 2 == 0), stop=False, skip_group_check=True)
                        last = pe.matmul(o[:, HD:VW], m.prob_lo[s % RING][:, c], m.v[side][:, j, HD:VW],
                                         start=False, stop=(j == 4 * u.group + r), skip_group_check=True)
                last.then_inc(prob_free, 1)

            for job in jobs_of(None, None):
                run(job)
            for s in range(LEAD):
                scores(None, s)
            with pe.Fori(0, PAIRS) as trip:
                for s in range(BODY):
                    jobs = jobs_of(trip, s)
                    half = (len(jobs) + 1) // 2
                    for job in jobs[:half]:
                        run(job)
                    scores(trip, s + LEAD)
                    for job in jobs[half:]:
                        run(job)
                    weigh(trip, s)

        @block.scalar
        def _(act):
            def run(job):
                full, free = bank_full[job.bank], bank_free[job.bank]
                src = m.bank[job.bank]
                if job.kind == "max":
                    return
                act.wait_ge(full, job.before + 1)
                if job.kind == "kq":
                    c = slice(job.what[1] * 512, (job.what[1] + 1) * 512)
                    if job.what[1] == 0 and not (job.trip is None):
                        load_wait(act, job.heads_done())
                    act.activation(m.kq_hi[:, c], src, ACT.Copy).then_inc(high_done, 1)
                elif job.kind == "v":
                    v = m.v[job.side][:, 8 * job.what[1]:8 * job.what[1] + 8, HD:2 * HD]
                    act.activation(v, src.rearrange("p (t d) -> p t d", d=HD), ACT.Copy).then_inc(high_done, 1)
                else:
                    g = job.what[1]
                    act.activation(m.q_hm[job.side][HD:HD + 1, g * 512:(g + 1) * 512], src[0:1, :],
                                   ACT.Copy).then_inc(free, 1)

            def exp_high(trip, s):
                u = UNITS[s % NU]
                n = s if trip is None else trip * BODY + s
                act.wait_ge(scores_full, n + 1)
                act.wait_ge(prob_free, n + 1)
                act.activation(m.prob_hi[s % RING][:, 0:u.width], m.scores[s % 2][:, 0:u.width], ACT.Exp,
                               scale=EXP_SCALE)

            def exp_full(s):
                u = UNITS[s % NU]
                act.activation(m.prob[s % RING][:, 0:u.width], m.scores[s % 2][:, 0:u.width], ACT.Exp,
                               scale=EXP_SCALE).then_inc(exp_done, 1)

            def copy_acc(trip, s):
                g = UNITS[s % NU].group
                n = trip * 2 * GROUPS + (s // NU) * GROUPS + g
                act.wait_ge(prob_free, trip * BODY + s + 1 + RING)
                act.wait_ge(norm_done, n + 1)
                for b in range(2):
                    src = m.acc[b].rearrange("p (t n) -> p t n", n=ACC)[:, :, 0:VW]
                    last = act.activation(m.acc_copy[:, g % 2, 2 * b:2 * b + 2, :], src, ACT.Copy)
                last.then_inc(acc_free, 1)

            for job in jobs_of(None, None):
                run(job)
            for s in range(LEAD - 1):
                exp_high(None, s)
                exp_full(s)
            with act.Fori(0, PAIRS) as trip:
                for s in range(BODY):
                    exp_high(trip, s + LEAD - 1)
                    if s > 0 and UNITS[(s - 1) % NU].last:
                        copy_acc(trip, s - 1)
                    for job in jobs_of(trip, s):
                        run(job)
                    exp_full(s + LEAD - 1)
                copy_acc(trip, BODY - 1)

        @block.vector
        def _(dve):
            def run(job):
                full, free = bank_full[job.bank], bank_free[job.bank]
                src = m.bank[job.bank]
                if job.kind == "shift":
                    return
                if job.kind == "max":
                    _, g, r, c = job.what
                    dve.wait_ge(full, job.before + 1)
                    width = 512 if c < g else (r + 1) * P
                    dve.tensor_reduce(m.part_max[:, g % 2, r, c:c + 1], src[:, 0:width], AX, ALU.max).then_inc(free, 1)
                    if (r, c) == (3, g):
                        dve.wait_ge(free, job.before + 1)
                        dve.wait_ge(bank_free[1 - job.bank], job.before + job.bank)
                        dve.tensor_reduce(m.neg_max[:, g % 2, :], m.part_max[:, g % 2, :, 0:g + 1], AX, ALU.max,
                                          negate=True).then_inc(neg_max_ready, 1)
                    return
                k = job.what[1] + (4 if job.kind == "v" else 0)
                dve.wait_ge(high_done, job.heads_done() * 6 + k + 1)
                if job.kind == "kq":
                    c = slice(job.what[1] * 512, (job.what[1] + 1) * 512)
                    dve.tensor_tensor(m.kq_lo[:, c], src, m.kq_hi[:, c], ALU.subtract).then_inc(free, 1)
                else:
                    t = slice(8 * job.what[1], 8 * job.what[1] + 8)
                    dve.tensor_tensor(m.v[job.side][:, t, 0:HD], src.rearrange("p (t d) -> p t d", d=HD),
                                      m.v[job.side][:, t, HD:2 * HD], ALU.subtract).then_inc(free, 1)

            def low(trip, s):
                u = UNITS[s % NU]
                dve.wait_ge(exp_done, trip * BODY + s + 1)
                c = slice(0, share(u))
                b = s % RING
                dve.tensor_tensor(m.prob_lo[b][:, c], m.prob[b][:, c], m.prob_hi[b][:, c],
                                  ALU.subtract).then_inc(low_dve, 1)

            def invert(trip, s):
                g = UNITS[s % NU].group
                n = trip * 2 * GROUPS + (s // NU) * GROUPS + g
                dve.wait_ge(acc_free, n + 2)
                dve.reciprocal(m.inv_sum[:, g % 2, :, :], m.acc_copy[:, g % 2, :, 2 * HD:VW]).then_inc(inv_ready, 1)

            for job in jobs_of(None, None):
                run(job)
            with dve.Fori(0, PAIRS) as trip:
                for s in range(BODY):
                    low(trip, s)
                    for job in jobs_of(trip, s):
                        run(job)
                    if s > 0 and UNITS[(s - 1) % NU].last:
                        invert(trip, s - 1)
                invert(trip, BODY - 1)

        @block.gpsimd
        def _(pool):
            def low(trip, s):
                u = UNITS[s % NU]
                pool.wait_ge(exp_done, trip * BODY + s + 1)
                c = slice(share(u), u.width)
                b = s % RING
                pool.tensor_tensor(m.prob_lo[b][:, c], m.prob[b][:, c], m.prob_hi[b][:, c],
                                   ALU.subtract).then_inc(low_pool, 1)

            def normalise(trip, s):
                u, side = UNITS[s % NU], s // NU
                g = u.group
                n = trip * 2 * GROUPS + side * GROUPS + g
                pool.wait_ge(inv_ready, n + 1)
                a = m.acc_copy[:, g % 2, :, :]
                pool.tensor_tensor(m.acc_sum[:, g % 2, :, :], a[:, :, 0:HD], a[:, :, HD:2 * HD],
                                   ALU.add).then_inc(sum_ready, 1)
                pool.wait_ge(sum_ready, n + 1)
                out = m.heads_out[:, 4 * g:4 * g + 4, bass.ds(trip * 2 * HD + side * HD, HD)]
                pool.tensor_tensor(out, m.acc_sum[:, g % 2, :, :],
                                   m.inv_sum[:, g % 2, :, :].broadcast_to([P, 4, HD]), ALU.mult).then_inc(norm_done, 1)

            pool.sem_inc(prob_free, RING)
            pool.sem_inc(acc_free, 1)
            pool.sem_inc(norm_done, 2)
            with pool.Fori(0, PAIRS) as trip:
                for s in range(BODY):
                    low(trip, s)
                    if s > 1 and UNITS[(s - 2) % NU].last:
                        normalise(trip, s - 2)
                normalise(trip, BODY - 1)

        @block.sync
        def _(sp):
            def spread(heads, side):
                hi, lo = m.kq_hi, m.kq_lo
                for dst, src in ((m.k_hh[side][0:HD, :], hi[0:HD, :]), (m.q_hl[side][0:HD, :], hi[HD:P, :]),
                                 (m.k_hh[side][HD:P, :], hi[0:HD, :]), (m.q_hl[side][HD:P, :], lo[HD:P, :]),
                                 (m.k_l1[side][0:HD, :], lo[0:HD, :]), (m.q_hm[side][0:HD, :], hi[HD:P, :])):
                    sp.dma_start(dst, src).then_inc(kq_spread, 16)

            last = [j for j in jobs_of(None, None) if j.kind == "kq"][-2:]
            for j in last:
                sp.wait_ge(bank_free[j.bank], j.before + 1)
            spread(0, 0)
            with sp.Fori(0, PAIRS) as trip:
                for head in range(2):
                    for j in [j for j in jobs_of(trip, head * NU + LAST_KQ) if j.kind == "kq"]:
                        sp.wait_ge(bank_free[j.bank], j.before + 1)
                    spread(None, (head + 1) % 2)


ROUND = 12582912.0
EPS = 1e-5
FF = 512
FT = FF // P
Q1 = 64
H1 = 4
SCALE1 = H1 ** -0.5
EXPERTS = 16
CAP = S // EXPERTS
G = 512
PARAMS = ["L1_attn_bias_q", "L1_attn_bias_k", "L1_attn_q_alpha", "L1_attn_k_alpha", "L1_attn_v_alpha",
          "L1_attn_q_zp", "L1_attn_k_zp", "L1_attn_v_zp", "L1_attn_attn_alpha", "L1_attn_attn_zp"]
BQ, BK, QA, KA, VA, QZ, KZ, VZ, AA, AZ = range(10)


class Chain:

    def __init__(self, engine, sem, base=0):
        self.engine, self.sem, self.base, self.count = engine, sem, base, 0

    def mark(self, instruction):
        instruction.then_inc(self.sem, 1)
        self.count += 1

    def wait(self):
        self.engine.wait_ge(self.sem, self.base + self.count)

    def step(self, instruction):
        self.mark(instruction)
        self.wait()


def moments(dve, c, stats, mv):
    c.mark(dve.tensor_tensor(mv[:, :, 0:2], stats[:, :, 1:3], stats[:, :, 4:6], ALU.add))
    c.step(dve.tensor_tensor(mv[:, :, 2:3], stats[:, :, 1:2], stats[:, :, 4:5], ALU.subtract))
    c.step(dve.scalar_tensor_tensor(mv[:, :, 3:4], mv[:, :, 2:3], 0.25, mv[:, :, 2:3], ALU.mult, ALU.mult))
    c.mark(dve.tensor_scalar(mv[:, :, 0:1], mv[:, :, 0:1], 0.5, None, ALU.mult))
    c.step(dve.scalar_tensor_tensor(mv[:, :, 1:2], mv[:, :, 1:2], 1.0 / D, mv[:, :, 3:4], ALU.mult, ALU.add))


class Tail:

    def __init__(self, nc, ctx):
        def sb(name, shape, dt=F32):
            return ctx.enter_context(nc.sbuf_tensor(name, shape, dt))

        self.nc = nc
        self.x2 = sb("x2", [P, TILES, D])
        self.x2t = sb("x2t", [P, 2, S], F16)
        self.wkq1 = sb("wkq1", [P, 3 * Q1], F16)
        self.row = sb("row", [1, 10, HEADS])
        self.aw_row = sb("aw_row", [1, 3 * Q1])
        self.bad = sb("bad", [1, 1], I32)
        self.y1 = sb("y1", [P, TILES, D])
        self.ones = sb("ones", [P, P])
        self.bo_b = sb("bo_b", [P, D])
        self.b2_b = sb("b2_b", [P, D])
        self.pb_b = sb("pb_b", [P, D])
        self.bg_b = sb("bg_b", [P, EXPERTS])
        self.pw = sb("pw", [P, Q1])
        self.pa = sb("pa", [P, 1])

    def scope(self, ctx):
        self.sb = lambda name, shape, dt=F32: ctx.enter_context(self.nc.sbuf_tensor(name, shape, dt))


def layer0_rest(nc, m, t, ins, sem):
    sb = t.sb
    wo = sb("wo", [P, PAIRS, D])
    wo_hi = sb("wo_hi", [P, PAIRS, D], F16)
    wo_lo = sb("wo_lo", [P, PAIRS, D], F16)
    w1 = sb("w1", [P, FT, D])
    w2 = sb("w2", [P, FF])
    w1q = sb("w1q", [P, FF], F16)
    w2q = sb("w2q", [P, FF], F16)
    w1t = sb("w1t", [P, FF], F16)
    w2t = sb("w2t", [P, FT, D], F16)
    qkv = sb("qkv", [Q1, 3, D])
    qkv_a = sb("qkv_a", [Q1, 3, 1])
    qkv_ia = sb("qkv_ia", [Q1, 3, 1])
    qkv_q = sb("qkv_q", [Q1, 3, D], F16)
    b1 = sb("b1", [P, FT])
    part = sb("part", [P, 2])
    gamma = sb("gamma", [P, 2])
    inv_gamma = sb("inv_gamma", [P, 2])
    rounded = sb("rounded", [P, FF])
    xb = sb("xb", [P, TILES, D])
    o_hi = sb("o_hi", [P, 4, HEADS * HD], F16)
    o_lo = sb("o_lo", [P, 4, HEADS * HD], F16)
    ot_hi = sb("ot_hi", [P, PAIRS, P], F16)
    ot_lo = sb("ot_lo", [P, PAIRS, P], F16)
    r = sb("r", [P, 4, D])
    stats = sb("stats", [P, 4, 6])
    mv = sb("mv", [P, 4, 4])
    dev = sb("dev", [P, 4])
    rstd = sb("rstd", [P, 4])
    x1 = sb("x1", [P, 4, D])
    x1b = sb("x1b", [P, 4, D])
    x_hi = sb("x_hi", [P, 4, D], F16)
    x_lo = sb("x_lo", [P, 4, D], F16)
    x1t = sb("x1t", [P, 2, G], F16)
    up = sb("up", [P, FT, G])
    up_hi = sb("up_hi", [P, FT, G], F16)
    up_lo = sb("up_lo", [P, FT, G], F16)

    loaded, prep, made, turned = sem("r_loaded"), sem("r_prep"), sem("r_made"), sem("r_turned")
    halves = lambda bank: m.psum[:, bank, :].bitcast(F16)

    with nc.Block() as block:

        @block.sync
        def _(sp):
            loads = [(wo[:], ins["L0_attn_Wo"].rearrange("(a p) n -> p a n", p=P)),
                     (w1[:], ins["L0_ffn_W1"].rearrange("(a p) n -> p a n", p=P)),
                     (w2[:], ins["L0_ffn_W2"]),
                     (b1[:], ins["L0_ffn_b1"].rearrange("(a p) -> p a", p=P)),
                     (qkv[:], ins["L1_attn_qkv_w"].rearrange("(a p) n -> p a n", p=Q1)),
                     (qkv_a[:], ins["L1_attn_qkv_alpha"].rearrange("(a p) n -> p a n", p=Q1)),
                     (t.aw_row[:], ins["L1_attn_qkv_alpha"].rearrange("o a -> a o")),
                     (t.bo_b[:], ins["L0_attn_bo"].partition_broadcast(P)),
                     (t.b2_b[:], ins["L0_ffn_b2"].partition_broadcast(P)),
                     (t.pb_b[:], ins["L1_attn_proj_b"].partition_broadcast(P)),
                     (t.bg_b[:], ins["L1_ffn_bg"].partition_broadcast(P)),
                     (t.pw[:], ins["L1_attn_proj_w"]),
                     (t.pa[:], ins["L1_attn_proj_alpha"])]
            loads += [(t.row[:, i, :], ins[n].rearrange("a h b c -> (a b c) h")) for i, n in enumerate(PARAMS)]
            t.loads = len(loads)
            with nc.allow_non_contiguous_dma("small parameters, once"):
                for dst, src in loads:
                    sp.dma_start(dst, src).then_inc(loaded, 16)

        n_loads = 13 + len(PARAMS)

        @block.vector
        def _(dve):
            c = Chain(dve, prep)
            c.step(dve.memset(t.ones[:], 1.0))
            dve.wait_ge(loaded, 16 * n_loads)
            c.mark(dve.tensor_reduce(part[:, 0:1], w1[:].rearrange("p a n -> p (a n)"), AX, ALU.add,
                                     apply_absolute_value=True))
            c.step(dve.tensor_reduce(part[:, 1:2], w2[:], AX, ALU.add, apply_absolute_value=True))
            c.step(dve.reciprocal(qkv_ia[:], qkv_a[:]))
            dve.wait_ge(turned, 1)
            c.step(dve.tensor_scalar(gamma[:], m.psum[:, 0, 0:2], 1.0 / (FF * D), EPS, ALU.mult, ALU.add))
            c.step(dve.reciprocal(inv_gamma[:], gamma[:]))
            for k, (w, q) in enumerate(((w1[:].rearrange("p a n -> p (a n)"), w1q), (w2[:], w2q))):
                c.step(dve.tensor_scalar(rounded[:], w, inv_gamma[:, k:k + 1], ROUND, ALU.mult, ALU.add))
                c.step(dve.tensor_scalar(rounded[:], rounded[:], -ROUND, 1.0, ALU.add, ALU.min))
                c.step(dve.tensor_scalar(q[:], rounded[:], -1.0, None, ALU.max))
            for k in range(3):
                w = rounded[0:Q1, 0:D]
                c.step(dve.tensor_scalar(w, qkv[:, k, :], qkv_ia[:, k, :], -8.0, ALU.mult, ALU.max))
                c.step(dve.tensor_scalar(w, w, 7.0, ROUND, ALU.min, ALU.add))
                c.step(dve.tensor_scalar(qkv_q[:, k, :], w, -ROUND, None, ALU.add))
            dve.tensor_copy(part[:, 0:1], gamma[:, 0:1]).then_inc(made, 1)
            dve.wait_ge(turned, 2)
            c.mark(dve.tensor_copy(w1t[:], halves(1)[:, 0:FF]))
            c.mark(dve.tensor_copy(w2t[:].rearrange("p a n -> p (a n)"), halves(2)[:, 0:FF]))
            c.mark(dve.tensor_copy(t.wkq1[:], halves(3)[:, 0:3 * Q1]))
            c.step(dve.tensor_copy(wo_hi[:], wo[:]))
            c.step(dve.tensor_tensor(wo_lo[:], wo[:], wo_hi[:], ALU.subtract))

        @block.tensor
        def _(pe):
            pe.wait_ge(prep, 3)
            pe.matmul(m.psum[:, 0, 0:2], t.ones[:], part[:], start=True, stop=True).then_inc(turned, 1)
            pe.wait_ge(made, 1)
            for f in range(FT):
                pe.transpose(halves(1)[:, f * P:(f + 1) * P], w1q[:, f * P:(f + 1) * P], m.ident16[:])
                pe.transpose(halves(2)[:, f * P:(f + 1) * P], w2q[:, f * P:(f + 1) * P], m.ident16[:])
            for k in range(3):
                last = pe.transpose(halves(3)[:, k * Q1:(k + 1) * Q1], qkv_q[:, k, :], m.ident16[0:Q1, 0:Q1])
            last.then_inc(turned, 1)

        @block.gpsimd
        def _(pool):
            pool.wait_ge(loaded, 16 * n_loads)
            pool.tensor_tensor(xb[:], m.x[:], t.bo_b[:].unsqueeze(1).broadcast_to([P, TILES, D]),
                               ALU.add).then_inc(sem("r_xb"), 1)
            pool.memset(t.y1[:], 0.0).then_inc(sem("r_y1"), 1)

    split_hi, split_lo = sem("split_hi"), sem("split_lo")
    o_turned, ot_hi_done, ot_lo_done = sem("o_turned"), sem("ot_hi_done"), sem("ot_lo_done")
    y_done, dev_asked, dev_done = sem("y_done"), sem("dev_asked"), sem("dev_done")
    x_hi_done, x_lo_done, x1b_done = sem("x_hi_done"), sem("x_lo_done"), sem("x1b_done")
    x_ready, x_turned, xt_done = sem("x_ready"), sem("x_turned"), sem("xt_done")
    up_full, up_done = sem("up_full"), sem("up_done")
    up_hi_done, up_lo_done, down_done = sem("up_hi_done"), sem("up_lo_done"), sem("down_done")
    group_done = sem("group_done")
    chain = sem("r_chain")
    PER = 28

    with nc.Block() as block:

        @block.tensor
        def _(pe):
            with pe.Fori(0, GROUPS) as g:
                for k in range(4):
                    pe.wait_ge(split_hi, g * 4 + k + 1)
                    pe.wait_ge(split_lo, g * 4 + k + 1)
                    pe.wait_ge(ot_hi_done, g * 4 + k + 1)
                    pe.wait_ge(ot_lo_done, g * 4 + k + 1)
                    for b, o in ((0, o_hi), (1, o_lo)):
                        for h in range(PAIRS):
                            last = pe.transpose(halves(b)[:, h * P:(h + 1) * P], o[:, k, h * P:(h + 1) * P], m.ident16[:])
                    last.then_inc(o_turned, 1)
                    pe.wait_ge(ot_hi_done, g * 4 + k + 2)
                    pe.wait_ge(ot_lo_done, g * 4 + k + 2)
                    out = m.psum[:, 2, k * P:(k + 1) * P]
                    for h in range(PAIRS):
                        pe.matmul(out, ot_hi[:, h, :], wo_hi[:, h, :], start=(h == 0), stop=False)
                        pe.matmul(out, ot_hi[:, h, :], wo_lo[:, h, :], start=False, stop=False)
                        last = pe.matmul(out, ot_lo[:, h, :], wo_hi[:, h, :], start=False, stop=(h == PAIRS - 1))
                last.then_inc(y_done, 1)

                def turn(n, bank):
                    pe.wait_ge(x_hi_done, g * 2 + n + 1)
                    pe.wait_ge(x_lo_done, g * 2 + n + 1)
                    for a, x in enumerate((x_hi, x_lo)):
                        for k in range(4):
                            last = pe.transpose(halves(bank)[:, a * G + k * P:a * G + (k + 1) * P], x[:, k, :], m.ident16[:])
                    last.then_inc(x_turned, 1)

                turn(0, 3)
                pe.wait_ge(xt_done, g * 2 + 1)
                for f in range(FT):
                    if f >= 2:
                        pe.wait_ge(up_done, g * FT + f - 1)
                    pe.matmul(m.psum[:, 4 + f % 2, :], w1t[:, f * P:(f + 1) * P], x1t[:, 0, :], start=True, stop=False)
                    pe.matmul(m.psum[:, 4 + f % 2, :], w1t[:, f * P:(f + 1) * P], x1t[:, 1, :],
                              start=False, stop=True).then_inc(up_full, 1)
                pe.wait_ge(up_lo_done, (g + 1) * FT)
                for k in range(4):
                    out = m.psum[:, 6, k * P:(k + 1) * P]
                    for f in range(FT):
                        pe.matmul(out, up_hi[:, f, k * P:(k + 1) * P], w2t[:, f, :], start=(f == 0), stop=False)
                        last = pe.matmul(out, up_lo[:, f, k * P:(k + 1) * P], w2t[:, f, :], start=False, stop=(f == FT - 1))
                last.then_inc(down_done, 1)
                turn(1, 7)

        @block.scalar
        def _(act):
            with act.Fori(0, GROUPS) as g:
                act.wait_ge(group_done, g + 1)
                for k in range(4):
                    act.activation(o_hi[:, k, :], m.heads_out[:, bass.ds(g * 4 + k, 1), :].rearrange("p a n -> p (a n)"),
                                   ACT.Copy).then_inc(split_hi, 1)
                    if k:
                        act.wait_ge(o_turned, g * 4 + k)
                        act.activation(ot_hi[:].rearrange("p a n -> p (a n)"), halves(0), ACT.Copy).then_inc(ot_hi_done, 1)
                act.wait_ge(o_turned, g * 4 + 4)
                act.activation(ot_hi[:].rearrange("p a n -> p (a n)"), halves(0), ACT.Copy).then_inc(ot_hi_done, 1)

                def norm(n, bank, dst):
                    act.wait_ge(dev_asked, g * 2 + n + 1)
                    act.activation(dev[:], rstd[:], ACT.Sqrt).then_inc(dev_done, 1)
                    act.wait_ge(x_ready, g * 2 + n + 1)
                    x = x1[:] if n == 0 else t.x2[:, bass.ds(g * 4, 4), :]
                    act.activation(x_hi[:], x, ACT.Copy).then_inc(x_hi_done, 1)
                    act.wait_ge(x_turned, g * 2 + n + 1)
                    act.activation(dst, halves(bank).rearrange("p (a n) -> p a n", a=2), ACT.Copy).then_inc(xt_done, 1)

                norm(0, 3, x1t[:])
                for f in range(FT):
                    act.wait_ge(up_full, g * FT + f + 1)
                    act.activation(up[:, f, :], m.psum[:, 4 + f % 2, :], ACT.Relu, bias=b1[:, f:f + 1]).then_inc(up_done, 1)
                norm(1, 7, t.x2t[:, :, bass.ds(g * G, G)])

        @block.vector
        def _(dve):
            with dve.Fori(0, GROUPS) as g:
                c = Chain(dve, chain, g * PER)
                dve.wait_ge(group_done, g + 1)

                def copy_low(k):
                    dve.wait_ge(o_turned, g * 4 + k + 1)
                    dve.tensor_copy(ot_lo[:].rearrange("p a n -> p (a n)"), halves(1)).then_inc(ot_lo_done, 1)

                for k in range(4):
                    dve.wait_ge(split_hi, g * 4 + k + 1)
                    o = m.heads_out[:, bass.ds(g * 4 + k, 1), :].rearrange("p a n -> p (a n)")
                    dve.tensor_tensor(o_lo[:, k, :], o, o_hi[:, k, :], ALU.subtract).then_inc(split_lo, 1)
                    if k:
                        copy_low(k - 1)
                copy_low(3)

                def norm(n, x):
                    for k in range(4):
                        c.mark(dve.bn_stats(stats[:, k, :], r[:, k, :]))
                    c.wait()
                    moments(dve, c, stats, mv)
                    dve.tensor_scalar(rstd[:], mv[:, :, 1], EPS, None, ALU.add).then_inc(dev_asked, 1)
                    dve.wait_ge(dev_done, g * 2 + n + 1)
                    c.step(dve.reciprocal(rstd[:], dev[:]))
                    for k in range(4):
                        last = dve.tensor_scalar(x[:, k, :], r[:, k, :], mv[:, k, 0:1], rstd[:, k:k + 1],
                                                 ALU.subtract, ALU.mult)
                        if k < 3:
                            c.mark(last)
                    last.then_inc(x_ready, 1)
                    dve.wait_ge(x_hi_done, g * 2 + n + 1)
                    dve.tensor_tensor(x_lo[:], x, x_hi[:], ALU.subtract).then_inc(x_lo_done, 1)

                dve.wait_ge(y_done, g + 1)
                c.step(dve.tensor_tensor(r[:], m.psum[:, 2, :].rearrange("p (a n) -> p a n", n=D),
                                         xb[:, bass.ds(g * 4, 4), :], ALU.add))
                norm(0, x1[:])
                dve.tensor_tensor(x1b[:], x1[:], t.b2_b[:].unsqueeze(1).broadcast_to([P, 4, D]), ALU.add)\
                    .then_inc(x1b_done, 1)
                for f in range(FT):
                    dve.wait_ge(up_done, g * FT + f + 1)
                    dve.tensor_copy(up_hi[:, f, :], up[:, f, :]).then_inc(up_hi_done, 1)
                    dve.wait_ge(up_hi_done, g * FT + f + 1)
                    dve.tensor_tensor(up_lo[:, f, :], up[:, f, :], up_hi[:, f, :], ALU.subtract).then_inc(up_lo_done, 1)
                dve.wait_ge(down_done, g + 1)
                dve.wait_ge(x1b_done, g + 1)
                c.step(dve.tensor_tensor(r[:], m.psum[:, 6, :].rearrange("p (a n) -> p a n", n=D), x1b[:], ALU.add))
                norm(1, t.x2[:, bass.ds(g * 4, 4), :])
                dve.wait_ge(xt_done, g * 2 + 2)
                dve.tensor_copy(part[:, 0:1], gamma[:, 0:1]).then_inc(group_done, 1)
                assert c.count == PER

        @block.gpsimd
        def _(pool):
            pool.sem_inc(group_done, 1)
            pool.sem_inc(ot_hi_done, 1)
            pool.sem_inc(ot_lo_done, 1)


def turn_rows(pe, out, cols, ident):
    return pe.matmul(out, cols, ident, start=True, stop=True)


def attention1_check(nc, m, t, sem):
    sb = t.sb
    ext = sb("ext", [P, 2, 4])
    ext1 = sb("ext1", [P, 2])
    v = sb("v_row", [1, 2, P])
    mag = sb("mag", [1, 3, P])
    small = sb("small", [1, 8, HEADS])
    prm = sb("prm", [1, 8, HEADS])
    full, done, chain, asked, expd = (sem("c_full"), sem("c_done"), sem("c_chain"), sem("c_asked"), sem("c_exp"))
    with nc.Block() as block:

        @block.tensor
        def _(pe):
            for c in range(4):
                cols = slice(c * G, (c + 1) * G)
                pe.matmul(m.psum[:, c, :], t.wkq1[:, 0:P], t.x2t[:, 0, cols], start=True, stop=False)
                pe.matmul(m.psum[:, c, :], t.wkq1[:, 0:P], t.x2t[:, 1, cols], start=False, stop=True).then_inc(full, 1)
            pe.wait_ge(done, 1)
            for k in range(2):
                last = turn_rows(pe, m.psum[0:1, 4, k * P:(k + 1) * P], ext1[:, k:k + 1], m.ident[:])
            last.then_inc(full, 1)

        @block.vector
        def _(dve):
            c = Chain(dve, chain)
            for k in range(4):
                dve.wait_ge(full, k + 1)
                c.mark(dve.tensor_reduce(ext[:, 0, k:k + 1], m.psum[:, k, :], AX, ALU.max))
                c.mark(dve.tensor_reduce(ext[:, 1, k:k + 1], m.psum[:, k, :], AX, ALU.min))
            c.wait()
            c.step(dve.tensor_reduce(ext1[:, 0:1], ext[:, 0, :], AX, ALU.max))
            dve.tensor_reduce(ext1[:, 1:2], ext[:, 1, :], AX, ALU.min).then_inc(done, 1)

            def both(x):
                return x.unsqueeze(3).broadcast_to([1, 2, HEADS, H1])

            c.mark(dve.reciprocal(prm[:, 0:2, :], t.row[:, QA:QA + 2, :]))
            c.step(dve.tensor_scalar(prm[:, 2:4, :], t.row[:, QZ:QZ + 2, :], ROUND, -ROUND, ALU.add, ALU.add))
            dve.wait_ge(full, 5)
            for k in range(2):
                w = v[:, k, :]
                q = w.rearrange("a (b h d) -> a b h d", b=2, d=H1)
                c.step(dve.tensor_tensor(w, m.psum[0:1, 4, k * P:(k + 1) * P], t.aw_row[:, 0:P], ALU.mult))
                c.step(dve.tensor_tensor(q, q, both(t.row[:, BQ:BQ + 2, :]), ALU.add))
                c.step(dve.tensor_tensor(q, q, both(prm[:, 0:2, :]), ALU.mult))
                c.step(dve.tensor_tensor(q, q, both(prm[:, 2:4, :]), ALU.add))
                c.step(dve.tensor_scalar(w, w, -8.0, 7.0, ALU.max, ALU.min))
                c.step(dve.tensor_scalar(w, w, ROUND, -ROUND, ALU.add, ALU.add))
                c.step(dve.tensor_tensor(q, q, both(prm[:, 2:4, :]), ALU.subtract))
                c.step(dve.tensor_tensor(q, q, both(t.row[:, QA:QA + 2, :]), ALU.mult))
            c.step(dve.scalar_tensor_tensor(mag[:, 0:2, :], v[:], -1.0, v[:], ALU.mult, ALU.max))
            c.step(dve.tensor_tensor(mag[:, 0, 0:Q1], mag[:, 0, 0:Q1], mag[:, 1, 0:Q1], ALU.max))
            c.step(dve.tensor_tensor(mag[:, 2, Q1:P], v[:, 0, Q1:P], v[:, 1, Q1:P], ALU.subtract))
            c.step(dve.scalar_tensor_tensor(mag[:, 2, Q1:P], mag[:, 2, Q1:P], -1.0, mag[:, 2, Q1:P], ALU.mult, ALU.max))
            c.step(dve.tensor_tensor(mag[:, 2, 0:Q1], mag[:, 0, 0:Q1], mag[:, 2, Q1:P], ALU.mult))
            c.step(dve.tensor_reduce(small[:, 0, :], mag[:, 2, 0:Q1].rearrange("a (h d) -> a h d", d=H1), AX, ALU.add))
            dve.tensor_scalar(small[:, 1, :], small[:, 0, :], -SCALE1, None, ALU.mult).then_inc(asked, 1)
            dve.wait_ge(expd, 1)
            c.step(dve.tensor_tensor(small[:, 3, :], small[:, 2, :], t.row[:, AA, :], ALU.mult))
            c.step(dve.tensor_scalar(small[:, 3, :], small[:, 3, :], 2.02 / S, None, ALU.is_gt))
            c.step(dve.tensor_scalar(small[:, 4, :], t.row[:, AZ, :], ROUND, -ROUND, ALU.add, ALU.add))
            c.mark(dve.tensor_scalar(small[:, 5, :], small[:, 4, :], -128.0, None, ALU.is_ge))
            c.mark(dve.tensor_scalar(small[:, 6, :], small[:, 4, :], 127.0, None, ALU.is_le))
            c.wait()
            c.step(dve.tensor_tensor(small[:, 3, :], small[:, 3, :], small[:, 5, :], ALU.mult))
            c.step(dve.tensor_tensor(small[:, 3, :], small[:, 3, :], small[:, 6, :], ALU.mult))
            c.step(dve.tensor_reduce(small[:, 7, 0:1], small[:, 3, :], AX, ALU.min))
            c.step(dve.tensor_scalar(t.bad[:], small[:, 7, 0:1], -1.0, 1.0, ALU.mult, ALU.add))

        @block.scalar
        def _(act):
            act.wait_ge(asked, 1)
            act.activation(small[:, 2, :], small[:, 1, :], ACT.Exp).then_inc(expd, 1)


def attention1_general(nc, m, t, sem):
    sb = t.sb
    qt = sb("g_qt", [Q1, 3, S])
    vn = sb("g_vn", [P, TILES, Q1])
    rows = sb("g_rows", [1, 15, Q1])
    cols = sb("g_cols", [Q1, 15])
    arow = sb("g_arow", [1, 3, HEADS])
    acols = sb("g_acols", [P, 3, HEADS])
    sel = sb("g_sel", [Q1, HEADS])
    seln = sb("g_seln", [Q1, HEADS])
    qi = sb("g_qi", [Q1, P])
    hp = sb("g_hp", [P, 3])
    nmax = sb("g_nmax", [P, 1])
    tot = sb("g_tot", [P, 1])
    inv = sb("g_inv", [P, 1])
    e = sb("g_e", [P, S])
    at = sb("g_at", [P, S])
    o1 = sb("g_o1", [P, TILES, Q1])
    ot = sb("g_ot", [Q1, P])
    wp = sb("g_wp", [P, Q1])
    wpt = sb("g_wpt", [Q1, D])
    oi = sb("g_oi", [P, Q1])
    pe_done, dve_done, act_done, pool_done = sem("g_pe"), sem("g_dve"), sem("g_act"), sem("g_pool")
    wp_rounded = sem("g_wp")
    flat = lambda a: m.psum[:, a:a + 4, :].rearrange("p b n -> p (b n)")
    PE0, DVE0 = 7, 35
    PE1, DVE1, ACT1 = 3, 13, 1
    PE2, DVE2 = 2, 3

    with nc.Block() as block:

        @block.gpsimd
        def _(pool):
            taken = pool.value_load(t.bad[0:1, 0:1], min_val=0, max_val=1)
            with pool.If(taken):
                pool.memset(seln[:], 1.0).then_inc(pool_done, 1)
                pool.wait_ge(pool_done, 1)
                pool.affine_select(out=sel[:], in_=seln[:], compare_op=ALU.is_ge, fill=0.0, base=0,
                                   pattern=[[-H1, HEADS]], channel_multiplier=1).then_inc(pool_done, 1)
                pool.wait_ge(pool_done, 2)
                pool.affine_select(out=sel[:], in_=sel[:], compare_op=ALU.is_ge, fill=0.0, base=H1 - 1,
                                   pattern=[[H1, HEADS]], channel_multiplier=-1).then_inc(pool_done, 1)

        @block.tensor
        def _(pe):
            taken = pe.value_load(t.bad[0:1, 0:1], min_val=0, max_val=1)
            with pe.If(taken):
                pe.wait_ge(dve_done, 10)
                for k in range(15):
                    pe.matmul(m.psum[0:Q1, 4, 2 * k:2 * k + 1], rows[:, k, :], t.ones[0:1, 0:1], start=True, stop=True)
                last = pe.matmul(m.psum[:, 5, 0:3 * HEADS], t.ones[0:1, :], arow[:].rearrange("a b h -> a (b h)"),
                                 start=True, stop=True)
                last.then_inc(pe_done, 1)
                for k in range(3):
                    if k:
                        pe.wait_ge(dve_done, 12 + 6 * k)
                    for c in range(4):
                        o = m.psum[0:Q1, c, :]
                        w = t.wkq1[:, k * Q1:(k + 1) * Q1]
                        tok = slice(c * G, (c + 1) * G)
                        pe.matmul(o, w, t.x2t[:, 0, tok], start=True, stop=False)
                        last = pe.matmul(o, w, t.x2t[:, 1, tok], start=False, stop=True)
                    last.then_inc(pe_done, 1)
                pe.wait_ge(dve_done, 30)
                for b in range(2):
                    for k in range(8):
                        last = pe.transpose(m.psum[:, 6 + b, k * Q1:(k + 1) * Q1],
                                            qt[:, 2, (8 * b + k) * P:(8 * b + k + 1) * P], m.ident[0:Q1, 0:Q1])
                    last.then_inc(pe_done, 1)
                pe.wait_ge(dve_done, 34)
                pe.transpose(m.psum[0:Q1, 5, 0:D], wp[:], m.ident[:]).then_inc(pe_done, 1)
                with pe.Fori(0, HEADS) as h:
                    with pe.Fori(0, TILES) as i:
                        p0 = h * (TILES * PE1) + i * PE1 + PE0
                        d0 = h * (TILES * DVE1) + i * DVE1 + DVE0
                        pe.wait_ge(dve_done, d0 + 4)
                        for c in range(4):
                            last = pe.matmul(m.psum[:, c, :], qi[:], qt[:, 1, c * G:(c + 1) * G], start=True, stop=True)
                        last.then_inc(pe_done, 1)
                        pe.wait_ge(dve_done, d0 + 10)
                        for k in range(TILES):
                            last = pe.transpose(flat(4)[:, k * P:(k + 1) * P], e[:, k * P:(k + 1) * P], m.ident[:])
                        last.then_inc(pe_done, 1)
                        pe.wait_ge(dve_done, d0 + 11)
                        for k in range(TILES):
                            last = pe.matmul(m.psum[:, 0, 0:H1], at[:, k * P:(k + 1) * P],
                                             vn[:, k, bass.ds(h * H1, H1)], start=(k == 0), stop=(k == TILES - 1))
                        last.then_inc(pe_done, 1)
                with pe.Fori(0, TILES) as i:
                    d0 = HEADS * TILES * DVE1 + DVE0 + i * DVE2
                    pe.wait_ge(dve_done, d0 + 1)
                    pe.matmul(m.psum[0:Q1, 0, 0:P], oi[:], m.ident[:], start=True, stop=True).then_inc(pe_done, 1)
                    pe.wait_ge(dve_done, d0 + 2)
                    pe.matmul(m.psum[:, 1, 0:D], ot[:], wpt[:], start=True, stop=True).then_inc(pe_done, 1)

        @block.scalar
        def _(act):
            taken = act.value_load(t.bad[0:1, 0:1], min_val=0, max_val=1)
            with act.If(taken):
                with act.Fori(0, HEADS) as h:
                    with act.Fori(0, TILES) as i:
                        act.wait_ge(dve_done, h * (TILES * DVE1) + i * DVE1 + DVE0 + 5)
                        act.activation(e[:], flat(0), ACT.Exp, bias=nmax[:], accum_out=tot[:]).then_inc(act_done, 1)

        @block.vector
        def _(dve):
            taken = dve.value_load(t.bad[0:1, 0:1], min_val=0, max_val=1)
            with dve.If(taken):
                c = Chain(dve, dve_done)

                def spread(x):
                    return x.unsqueeze(3).broadcast_to([1, x.shape[1], HEADS, H1])

                def by_head(k, n):
                    return rows[:, k:k + n, :].rearrange("a b (h d) -> a b h d", d=H1)

                c.step(dve.tensor_copy(rows[:, 0:3, :], t.aw_row[:].rearrange("a (b n) -> a b n", b=3)))
                c.step(dve.memset(rows[:, 5, :], 0.0))
                c.step(dve.tensor_copy(by_head(3, 2), spread(t.row[:, BQ:BQ + 2, :])))
                c.step(dve.tensor_copy(by_head(6, 3), spread(t.row[:, QA:QA + 3, :])))
                c.step(dve.reciprocal(rows[:, 9:12, :], rows[:, 6:9, :]))
                c.step(dve.tensor_copy(by_head(12, 3), spread(t.row[:, QZ:QZ + 3, :])))
                c.step(dve.tensor_scalar(rows[:, 12:15, :], rows[:, 12:15, :], ROUND, -ROUND, ALU.add, ALU.add))
                c.step(dve.tensor_copy(arow[:, 0, :], t.row[:, AA, :]))
                c.step(dve.reciprocal(arow[:, 1, :], t.row[:, AA, :]))
                c.step(dve.tensor_scalar(arow[:, 2, :], t.row[:, AZ, :], ROUND, -ROUND, ALU.add, ALU.add))
                assert c.count == 10
                dve.wait_ge(pe_done, 1)
                c.step(dve.tensor_copy(cols[:], m.psum[0:Q1, 4, 0:30].rearrange("p (a b) -> p a b", b=2)[:, :, 0]))
                c.step(dve.tensor_copy(acols[:], m.psum[:, 5, 0:3 * HEADS].rearrange("p (a b) -> p a b", b=HEADS)))
                for k in range(3):
                    assert c.count == 12 + 6 * k
                    x = qt[:, k, :]
                    col = lambda n: cols[:, n + k:n + k + 1]
                    dve.wait_ge(pe_done, 2 + k)
                    c.step(dve.tensor_scalar(x, flat(0)[0:Q1, :], col(0), col(3), ALU.mult, ALU.add))
                    c.step(dve.tensor_scalar(x, x, col(9), col(12), ALU.mult, ALU.add))
                    c.step(dve.tensor_scalar(x, x, -8.0, 7.0, ALU.max, ALU.min))
                    c.step(dve.tensor_scalar(x, x, ROUND, -ROUND, ALU.add, ALU.add))
                    c.step(dve.tensor_scalar(x, x, col(12), col(6), ALU.subtract, ALU.mult))
                    c.step(dve.tensor_scalar(x, x, SCALE1 if k == 0 else 1.0, None, ALU.mult))
                assert c.count == 30
                dve.wait_ge(pe_done, 6)
                c.mark(dve.tensor_copy(vn[:], m.psum[:, 6:8, :].rearrange("p b (k n) -> p (b k) n", n=Q1)))
                c.step(dve.reciprocal(tot[:], t.pa[:]))
                c.step(dve.tensor_scalar(wp[:], t.pw[:], tot[:], -8.0, ALU.mult, ALU.max))
                dve.tensor_scalar(wp[:], wp[:], 7.0, ROUND, ALU.min, ALU.add).then_inc(wp_rounded, 1)
                dve.wait_ge(wp_rounded, 1)
                c.step(dve.tensor_scalar(wp[:], wp[:], -ROUND, t.pa[:], ALU.add, ALU.mult))
                assert c.count == 34
                dve.wait_ge(pe_done, 7)
                c.step(dve.tensor_copy(wpt[:], m.psum[0:Q1, 5, 0:D]))
                assert c.count == DVE0
                dve.wait_ge(pool_done, 3)
                with dve.Fori(0, HEADS) as h:
                    with dve.Fori(0, TILES) as i:
                        p0 = h * (TILES * PE1) + i * PE1 + PE0
                        c = Chain(dve, dve_done, h * (TILES * DVE1) + i * DVE1 + DVE0)
                        c.step(dve.tensor_copy(hp[:], acols[:, :, bass.ds(h, 1)].rearrange("p a b -> p (a b)")))
                        c.step(dve.tensor_copy(seln[:, 0:1], sel[:, bass.ds(h, 1)]))
                        c.step(dve.tensor_copy(qi[:], qt[:, 0, bass.ds(i * P, P)]))
                        c.step(dve.tensor_scalar(qi[:], qi[:], seln[:, 0:1], None, ALU.mult))
                        dve.wait_ge(pe_done, p0 + 1)
                        c.step(dve.tensor_reduce(nmax[:], flat(0), AX, ALU.max, negate=True))
                        dve.wait_ge(act_done, h * TILES + i + 1)
                        c.step(dve.reciprocal(inv[:], tot[:]))
                        c.step(dve.tensor_scalar(e[:], e[:], inv[:], hp[:, 1:2], ALU.mult, ALU.mult))
                        c.step(dve.tensor_scalar(e[:], e[:], hp[:, 2:3], -128.0, ALU.add, ALU.max))
                        c.step(dve.tensor_scalar(e[:], e[:], 127.0, ROUND, ALU.min, ALU.add))
                        c.step(dve.tensor_scalar(e[:], e[:], -ROUND, hp[:, 2:3], ALU.add, ALU.subtract))
                        dve.wait_ge(pe_done, p0 + 2)
                        c.step(dve.tensor_copy(at[:], flat(4)))
                        dve.wait_ge(pe_done, p0 + 3)
                        c.step(dve.tensor_scalar(oi[:, 0:H1], m.psum[:, 0, 0:H1], hp[:, 0:1], None, ALU.mult))
                        c.step(dve.tensor_copy(o1[:, bass.ds(i, 1), bass.ds(h * H1, H1)].rearrange("p a n -> p (a n)"), oi[:, 0:H1]))
                        assert c.count == DVE1
                with dve.Fori(0, TILES) as i:
                    p0 = HEADS * TILES * PE1 + PE0 + i * PE2
                    c = Chain(dve, dve_done, HEADS * TILES * DVE1 + DVE0 + i * DVE2)
                    c.step(dve.tensor_copy(oi[:], o1[:, bass.ds(i, 1), :].rearrange("p a n -> p (a n)")))
                    dve.wait_ge(pe_done, p0 + 1)
                    c.step(dve.tensor_copy(ot[:], m.psum[0:Q1, 0, 0:P]))
                    dve.wait_ge(pe_done, p0 + 2)
                    c.step(dve.tensor_copy(t.y1[:, bass.ds(i, 1), :].rearrange("p a n -> p (a n)"), m.psum[:, 1, 0:D]))
                    assert c.count == DVE2


def norm_all(dve, c, r, x, stats, mv, var, dev, asked, devd, nth):
    for k in range(TILES):
        c.mark(dve.bn_stats(stats[:, k, :], r[:, k, :]))
    c.wait()
    moments(dve, c, stats, mv)
    dve.tensor_scalar(var[:], mv[:, :, 1], EPS, None, ALU.add).then_inc(asked, 1)
    dve.wait_ge(devd, nth)
    c.step(dve.reciprocal(var[:], dev[:]))
    for k in range(TILES):
        c.mark(dve.tensor_scalar(x[:, k, :], r[:, k, :], mv[:, k, 0:1], var[:, k:k + 1], ALU.subtract, ALU.mult))
    c.wait()


def experts(nc, m, t, ins, out, sem):
    sb = t.sb
    r = sb("e_r", [P, TILES, D])
    x3 = sb("e_x3", [P, TILES, D])
    stats = sb("e_stats", [P, TILES, 6])
    mv = sb("e_mv", [P, TILES, 4])
    var = sb("e_var", [P, TILES])
    dev = sb("e_dev", [P, TILES])
    wg = sb("e_wg", [P, EXPERTS])
    x3t = sb("e_x3t", [P, S])
    logit = sb("e_logit", [P, TILES, EXPERTS])
    lm = sb("e_lm", [P, TILES, EXPERTS])
    ex = sb("e_ex", [P, TILES, EXPERTS])
    top = sb("e_top", [P, TILES, 8])
    topi = sb("e_topi", [P, TILES, 8], U32)
    idx = sb("e_idx", [P, TILES])
    iota = sb("e_iota", [P, EXPERTS])
    hot = sb("e_hot", [P, TILES, EXPERTS], BF16)
    before = sb("e_before", [P, TILES, EXPERTS], BF16)
    tri = sb("e_tri", [P, P], BF16)
    onesb = sb("e_onesb", [P, P], BF16)
    cnt = sb("e_cnt", [P, TILES, EXPERTS])
    pos = sb("e_pos", [P, TILES])
    keep = sb("e_keep", [P, TILES])
    gate = sb("e_gate", [P, TILES])
    slot = sb("e_slot", [P, TILES])
    slotu = sb("e_slotu", [P, TILES], U32)
    zeros = sb("e_zeros", [P, TILES * D])
    xe = sb("e_xe", [P, EXPERTS, D])
    xet = sb("e_xet", [P, EXPERTS * CAP])
    w1 = [sb(f"e_w1{i}", [P, FF]) for i in range(2)]
    w2 = [sb(f"e_w2{i}", [P, FT, D]) for i in range(2)]
    b1 = sb("e_b1", [P, EXPERTS, FT])
    b1r = sb("e_b1r", [EXPERTS, FF])
    b2 = [sb(f"e_b2{i}", [P, D]) for i in range(2)]
    h = [sb(f"e_h{i}", [P, FT, CAP]) for i in range(2)]
    ye = [sb(f"e_ye{i}", [P, D]) for i in range(2)]
    back = sb("e_back", [P, TILES, D])
    rows_in = nc.dram_tensor("expert_rows", (S, D), F32, kind="Internal").ap()
    rows_out = nc.dram_tensor("expert_out", (S, D), F32, kind="Internal").ap()

    chain, asked, devd, pe_done, act_done = sem("e_chain"), sem("e_asked"), sem("e_devd"), sem("e_pe"), sem("e_act")
    loaded, zeroed, consts, slots = sem("e_loaded"), sem("e_zeroed"), sem("e_consts"), sem("e_slots")
    scattered, gathered, turned = sem("e_scattered"), sem("e_gathered"), sem("e_turned")
    xe_loaded, w_loaded, w_used = sem("e_xe"), [sem("e_w0"), sem("e_w1_")], sem("e_wused")
    up_full, up_done, down_full, down_done = sem("e_upf"), sem("e_upd"), sem("e_dnf"), sem("e_dnd")
    y_stored, back_zero, stored, copied = [sem("e_ys0"), sem("e_ys1")], sem("e_bz"), sem("e_stored"), sem("e_copied")

    x3_ready, hot_ready, stored_ready = sem("e_x3r"), sem("e_hotr"), sem("e_storer")

    def tile_rows(a):
        return a.rearrange("(e c) d -> c e d", c=P)

    with nc.Block() as block:

        @block.sync
        def _(sp):
            sp.dma_start(wg[:], ins["L1_ffn_Wg"]).then_inc(loaded, 16)
            sp.dma_start(b1r[:], ins["L1_ffn_b1"]).then_inc(loaded, 16)
            sp.wait_ge(consts, 1)
            sp.dma_start(tile_rows(rows_in), zeros[:].rearrange("p (a n) -> p a n", n=D)).then_inc(zeroed, 16)

            def weights(e, s):
                sp.dma_start(w1[s][:], ins["L1_ffn_W1"][bass.ds(e, 1), :, :].rearrange("a p n -> p (a n)"))\
                    .then_inc(w_loaded[s], 16)
                sp.dma_start(w2[s][:], ins["L1_ffn_W2"][bass.ds(e, 1), :, :].rearrange("a (f p) n -> p (a f) n", p=P))\
                    .then_inc(w_loaded[s], 16)
                sp.dma_start(b2[s][:], ins["L1_ffn_b2"][bass.ds(e, 1), :].rearrange("a n -> (a n)").partition_broadcast(P))\
                    .then_inc(w_loaded[s], 16)

            weights(0, 0)
            weights(1, 1)
            sp.wait_ge(scattered, 16 * TILES)
            sp.dma_start(xe[:], tile_rows(rows_in)).then_inc(xe_loaded, 16)
            with sp.Fori(0, EXPERTS // 2 - 1) as n:
                for s in range(2):
                    sp.wait_ge(down_done, n * 2 + s + 1)
                    sp.dma_start(rows_out[bass.ds((n * 2 + s) * P, P), :], ye[s][:]).then_inc(y_stored[s], 16)
                    weights(n * 2 + s + 2, s)
            for s in range(2):
                e = EXPERTS - 2 + s
                sp.wait_ge(down_done, e + 1)
                sp.dma_start(rows_out[e * P:(e + 1) * P, :], ye[s][:]).then_inc(y_stored[s], 16)
            sp.wait_ge(stored_ready, 1)
            sp.dma_start(out.rearrange("a (t p) d -> p (a t) d", p=P), x3[:]).then_inc(stored, 16)
            sp.wait_ge(stored, 16)

        @block.gpsimd
        def _(pool):
            k = 0
            for s in range(2):
                pool.sem_inc(y_stored[s], 16)

            def step(i):
                nonlocal k
                i.then_inc(consts, 1)
                k += 1
                pool.wait_ge(consts, k)

            step(pool.memset(zeros[:], 0.0))
            step(pool.iota(iota[:], [[1, EXPERTS]], base=0, channel_multiplier=0, allow_small_or_imprecise_dtypes=True))
            step(pool.memset(onesb[:], 1.0))
            step(pool.affine_select(out=tri[:], in_=onesb[:], compare_op=ALU.is_ge, fill=0.0, base=0,
                                    pattern=[[1, P]], channel_multiplier=-1))
            pool.memset(back[:], 0.0).then_inc(back_zero, 1)
            pool.wait_ge(slots, 1)
            pool.wait_ge(zeroed, 16)
            for k2 in range(TILES):
                pool.indirect_dma_start(rows_in, bass.IndirectOffsetOnAxis(slotu[:, k2:k2 + 1], 0), x3[:, k2, :], None,
                                        bounds_check=S - 1, oob_is_err=False).then_inc(scattered, 16)
            for s in range(2):
                pool.wait_ge(y_stored[s], 16 * (EXPERTS // 2 + 1))
            pool.wait_ge(back_zero, 1)
            for k2 in range(TILES):
                pool.indirect_dma_start(back[:, k2, :], None, rows_out, bass.IndirectOffsetOnAxis(slotu[:, k2:k2 + 1], 0),
                                        bounds_check=S - 1, oob_is_err=False).then_inc(gathered, 16)

        @block.scalar
        def _(act):
            act.wait_ge(asked, 1)
            act.activation(dev[:], var[:], ACT.Sqrt).then_inc(devd, 1)
            for b in range(4):
                act.wait_ge(pe_done, b + 1)
                act.activation(x3t[:, b * G:(b + 1) * G], m.psum[:, b, :], ACT.Copy).then_inc(act_done, 1)
            act.wait_ge(asked, 2)
            act.activation(ex[:], lm[:], ACT.Exp).then_inc(devd, 1)
            for b in range(4):
                act.wait_ge(turned, b + 1)
                act.activation(xet[:, b * G:(b + 1) * G], m.psum[:, b, :], ACT.Copy).then_inc(copied, 1)
            act.wait_ge(turned, 5)
            act.activation(b1[:].rearrange("p e f -> p f e"), m.psum[:, 4, 0:FT * EXPERTS].rearrange("p (f e) -> p f e", e=EXPERTS),
                           ACT.Copy).then_inc(copied, 1)
            act.wait_ge(copied, 5)
            with act.Fori(0, EXPERTS // 2) as n:
                for s in range(2):
                    act.wait_ge(up_full, n * 2 + s + 1)
                    for f in range(FT):
                        last = act.activation(h[s][:, f, :], m.psum[:, 4 + s, f * P:(f + 1) * P], ACT.Relu,
                                              bias=b1[:, bass.ds(n * 2 + s, 1), f:f + 1].rearrange("p a b -> p (a b)"))
                    last.then_inc(up_done, 1)
            act.wait_ge(asked, 3)
            act.activation(dev[:], var[:], ACT.Sqrt).then_inc(devd, 1)

        @block.tensor
        def _(pe):
            pe.wait_ge(x3_ready, 1)
            for b in range(4):
                for k in range(4):
                    last = pe.transpose(m.psum[:, b, k * P:(k + 1) * P], x3[:, 4 * b + k, :], m.ident[:])
                last.then_inc(pe_done, 1)
            pe.wait_ge(loaded, 32)
            for k in range(TILES):
                pe.wait_ge(act_done, k // 4 + 1)
                last = pe.matmul(m.psum[:, 4, k * EXPERTS:(k + 1) * EXPERTS], x3t[:, k * P:(k + 1) * P], wg[:],
                                 start=True, stop=True)
            last.then_inc(pe_done, 1)
            pe.wait_ge(hot_ready, 1)
            pe.wait_ge(consts, 4)
            pe.matmul(m.psum[:, 5, 0:TILES * EXPERTS], tri[:], hot[:].rearrange("p a n -> p (a n)"), start=True, stop=False)
            pe.matmul(m.psum[:, 5, 0:TILES * EXPERTS], onesb[:], before[:].rearrange("p a n -> p (a n)"),
                      start=False, stop=True).then_inc(pe_done, 1)
            pe.wait_ge(xe_loaded, 16)
            for b in range(4):
                for k in range(4):
                    last = pe.transpose(m.psum[:, b, k * P:(k + 1) * P], xe[:, 4 * b + k, :], m.ident[:])
                last.then_inc(turned, 1)
            pe.wait_ge(slots, 1)
            for f in range(FT):
                last = pe.transpose(m.psum[:, 4, f * EXPERTS:(f + 1) * EXPERTS], b1r[:, f * P:(f + 1) * P],
                                    m.ident[0:EXPERTS, 0:EXPERTS])
            last.then_inc(turned, 1)
            pe.wait_ge(copied, 5)
            with pe.Fori(0, EXPERTS // 2) as n:
                for s in range(2):
                    pe.wait_ge(w_loaded[s], n * 48 + 48)
                    x = xet[:, bass.ds((n * 2 + s) * P, P)]
                    for f in range(FT):
                        last = pe.matmul(m.psum[:, 4 + s, f * P:(f + 1) * P], w1[s][:, f * P:(f + 1) * P], x,
                                         start=True, stop=True)
                    last.then_inc(up_full, 1)
                    pe.wait_ge(up_done, n * 2 + s + 1)
                    for f in range(FT):
                        last = pe.matmul(m.psum[:, 6 + s, 0:D], h[s][:, f, :], w2[s][:, f, :], start=(f == 0), stop=(f == FT - 1))
                    last.then_inc(down_full, 1)

        @block.vector
        def _(dve):
            c = Chain(dve, chain)
            c.step(dve.tensor_tensor(r[:], t.x2[:], t.y1[:], ALU.add))
            c.step(dve.tensor_tensor(r[:], r[:], t.pb_b[:].unsqueeze(1).broadcast_to([P, TILES, D]), ALU.add))
            norm_all(dve, c, r, x3, stats, mv, var, dev, asked, devd, 1)
            dve.tensor_copy(pos[:], var[:]).then_inc(x3_ready, 1)
            dve.wait_ge(pe_done, 5)
            c.step(dve.tensor_tensor(logit[:], m.psum[:, 4, 0:TILES * EXPERTS].rearrange("p (a n) -> p a n", n=EXPERTS),
                                     t.bg_b[:].unsqueeze(1).broadcast_to([P, TILES, EXPERTS]), ALU.add))
            for k in range(TILES):
                c.mark(dve.max(top[:, k, :], logit[:, k, :]))
            c.wait()
            for k in range(TILES):
                c.mark(dve.max_index(topi[:, k, :], top[:, k, :], logit[:, k, :]))
            dve.tensor_tensor(lm[:], logit[:], top[:, :, 0:1].broadcast_to([P, TILES, EXPERTS]), ALU.subtract)\
                .then_inc(asked, 1)
            c.wait()
            c.step(dve.tensor_copy(idx[:], topi[:, :, 0]))
            dve.wait_ge(consts, 4)
            c.step(dve.tensor_tensor(hot[:], iota[:].unsqueeze(1).broadcast_to([P, TILES, EXPERTS]),
                                     idx[:].unsqueeze(2).broadcast_to([P, TILES, EXPERTS]), ALU.is_equal))
            c.step(dve.memset(before[:, 0, :], 0.0))
            for k in range(1, TILES):
                ins_ = dve.tensor_tensor(before[:, k, :], before[:, k - 1, :], hot[:, k - 1, :], ALU.add)
                if k < TILES - 1:
                    c.step(ins_)
            ins_.then_inc(hot_ready, 1)
            dve.wait_ge(devd, 2)
            c.step(dve.tensor_reduce(gate[:], ex[:], AX, ALU.add))
            c.step(dve.reciprocal(gate[:], gate[:]))
            dve.wait_ge(pe_done, 6)
            c.step(dve.tensor_tensor(cnt[:], m.psum[:, 5, 0:TILES * EXPERTS].rearrange("p (a n) -> p a n", n=EXPERTS),
                                     hot[:], ALU.mult))
            c.step(dve.tensor_reduce(pos[:], cnt[:], AX, ALU.add))
            c.step(dve.tensor_scalar(keep[:], pos[:], float(CAP), None, ALU.is_le))
            c.step(dve.tensor_tensor(gate[:], gate[:], keep[:], ALU.mult))
            c.step(dve.tensor_scalar(slot[:], idx[:], float(CAP), -1.0, ALU.mult, ALU.add))
            c.step(dve.tensor_tensor(slot[:], slot[:], pos[:], ALU.add))
            c.step(dve.tensor_scalar(keep[:], keep[:], -2.0 * S, 2.0 * S, ALU.mult, ALU.add))
            c.step(dve.tensor_tensor(slot[:], slot[:], keep[:], ALU.add))
            dve.tensor_copy(slotu[:], slot[:]).then_inc(slots, 1)
            with dve.Fori(0, EXPERTS // 2) as n:
                for s in range(2):
                    dve.wait_ge(down_full, n * 2 + s + 1)
                    dve.wait_ge(y_stored[s], n * 16 + 16)
                    dve.tensor_tensor(ye[s][:], m.psum[:, 6 + s, 0:D], b2[s][:], ALU.add).then_inc(down_done, 1)
            dve.wait_ge(gathered, 16 * TILES)
            c.step(dve.tensor_tensor(back[:], back[:], gate[:].unsqueeze(2).broadcast_to([P, TILES, D]), ALU.mult))
            c.step(dve.tensor_tensor(r[:], x3[:], back[:], ALU.add))
            norm_all(dve, c, r, x3, stats, mv, var, dev, asked, devd, 3)
            dve.tensor_copy(pos[:], var[:]).then_inc(stored_ready, 1)


INPUTS = ["L0_attn_x", "L0_attn_Wq", "L0_attn_Wk", "L0_attn_Wv", "L0_attn_Wo", "L0_attn_bo",
          "L0_ffn_W1", "L0_ffn_b1", "L0_ffn_W2", "L0_ffn_b2",
          "L1_attn_qkv_w", "L1_attn_qkv_alpha", "L1_attn_bias_q", "L1_attn_bias_k", "L1_attn_q_alpha",
          "L1_attn_q_zp", "L1_attn_k_alpha", "L1_attn_k_zp", "L1_attn_v_alpha", "L1_attn_v_zp",
          "L1_attn_attn_alpha", "L1_attn_attn_zp", "L1_attn_proj_w", "L1_attn_proj_b", "L1_attn_proj_alpha",
          "L1_ffn_Wg", "L1_ffn_bg", "L1_ffn_W1", "L1_ffn_b1", "L1_ffn_W2", "L1_ffn_b2"]


def build(nc, ins, out):
    with ExitStack() as kept:
        def sem(name):
            return kept.enter_context(nc.semaphore(name))

        with ExitStack() as ctx:
            m = Memory(nc, kept, ctx)
            setup(nc, m, ins, sem)
            attention(nc, m, sem)
        t = Tail(nc, kept)
        for phase in (lambda c: layer0_rest(nc, m, t, ins, sem), lambda c: attention1_check(nc, m, t, sem),
                      lambda c: attention1_general(nc, m, t, sem), lambda c: experts(nc, m, t, ins, out, sem)):
            with ExitStack() as ctx:
                t.scope(ctx)
                phase(ctx)


def kernel(**inputs):
    import concourse.bacc as bacc
    from concourse.bass_utils import run_bass_kernel_spmd

    nc = bacc.Bacc("TRN2", target_bir_lowering=False, num_devices=1)
    arrays, ins = {}, {}
    for name in INPUTS:
        a = np.ascontiguousarray(inputs[name])
        arrays[f"in_{name}"] = a
        ins[name] = nc.dram_tensor(f"in_{name}", a.shape, mybir.dt.from_np(a.dtype), kind="ExternalInput").ap()
    out = nc.dram_tensor("out_x", (1, S, D), F32, kind="ExternalOutput").ap()
    build(nc, ins, out)
    r = run_bass_kernel_spmd(nc, [arrays], core_ids=[0])
    return r.results[0]["out_x"]
```

```python
from contextlib import ExitStack

import numpy as np
import concourse.bass as bass
from concourse import mybir

F32 = mybir.dt.float32
F16 = mybir.dt.float16
BF16 = mybir.dt.bfloat16
I32 = mybir.dt.int32
U32 = mybir.dt.uint32
ALU = mybir.AluOpType
ACT = mybir.ActivationFunctionType
AX = mybir.AxisListType.X

P = 128
S = 2048
D = 128
TILES = S // P
HEADS = 16
HD = 64
PAIRS = HEADS // 2
GROUPS = TILES // 4
RAW_MASK = -8e9
EXP_SCALE = 1.0 / 8.0
VW = 2 * HD + 1
VSTRIDE = VW + 1
ACC = 256
RING = 4
LEAD = 2


class Unit:

    def __init__(self, group, pair):
        self.group = group
        first = 2 * pair
        self.first = pair == 0
        self.last = pair == 2 * group + 1
        r = [max(0, j - 4 * group) for j in (first, first + 1)]
        second = 512 if r[0] == 0 else (4 - r[0]) * P
        self.keys = [(first, r[0], 0), (first + 1, r[1], second)]
        self.width = second + (4 - r[1]) * P


UNITS = [Unit(g, p) for g in range(GROUPS) for p in range(2 * g + 2)]
NU = len(UNITS)
BODY = 2 * NU


def max_jobs(group):
    return [("max", group, r, c) for c in range(group + 1) for r in range(4)]


def job_plan():
    plan = [[] for _ in range(NU)]

    def put(step, ahead, jobs):
        plan[step] += [(ahead, j) for j in jobs]

    m0, m1, m2, m3 = max_jobs(0), max_jobs(1), max_jobs(2), max_jobs(3)
    put(0, 1, [("kq", 0)])
    put(0, 0, m3[0:1])
    put(1, 0, m3[1:3] + [("shift", 2)])
    put(2, 1, [("kq", 1)])
    put(2, 0, m3[3:5])
    put(3, 0, m3[5:7])
    put(4, 1, [("kq", 2)])
    put(4, 0, m3[7:9])
    put(5, 0, m3[9:11])
    put(6, 1, [("kq", 3)])
    put(6, 0, m3[11:13])
    put(7, 0, m3[13:16])
    put(9, 0, [("shift", 3)])
    put(9, 1, [("v", 0)])
    put(10, 1, [("v", 1)] + m0[0:2])
    put(11, 1, m0[2:4] + m1[0:1])
    put(12, 1, m1[1:4])
    put(13, 1, [("shift", 0)] + m1[4:6])
    put(14, 1, m1[6:8] + m2[0:1])
    put(15, 1, m2[1:3])
    put(16, 1, [("shift", 1)] + m2[3:5])
    put(17, 1, m2[5:7])
    put(18, 1, m2[7:10])
    put(19, 1, m2[10:12])
    return plan


PLAN = job_plan()
LAST_KQ = [(1, ("kq", 3)) in step for step in PLAN].index(True)
FIRST_JOBS = [what for step in PLAN for ahead, what in step if ahead]
JOBS_PER_TRIP = 2 * sum(len(p) for p in PLAN)
assert JOBS_PER_TRIP % 2 == 0


class Job:

    def __init__(self, index, trip, head, what):
        self.bank = index % 2
        self.before = index // 2 + (0 if trip is None else trip * (JOBS_PER_TRIP // 2))
        self.head = head
        self.side = head % 2
        self.kind = what[0]
        self.what = what
        self.trip = trip

    def heads_done(self):
        return self.head if self.trip is None else self.trip * 2 + self.head

    def shifts_done(self, group):
        return self.heads_done() * GROUPS + group


def jobs_of(trip, step):
    if step is None:
        return [Job(i, None, 0, w) for i, w in enumerate(FIRST_JOBS)]
    at = len(FIRST_JOBS)
    for s in range(step):
        at += len(PLAN[s % NU])
    return [Job(at + i, trip, step // NU + ahead, w) for i, (ahead, w) in enumerate(PLAN[step % NU])]


def shift_job(trip, head, group):
    if trip is None:
        return [j for j in jobs_of(None, None) if j.what == ("shift", group)][0], 0
    if group < 2 and head == 0:
        steps, head, back = range(NU, BODY), 2, JOBS_PER_TRIP // 2
    else:
        steps, back = range(BODY), 0
    for s in steps:
        for j in jobs_of(trip, s):
            if j.what == ("shift", group) and j.head == head:
                return j, back


class Memory:

    def __init__(self, nc, kept, ctx):
        def keep(name, shape, dt=F32):
            return kept.enter_context(nc.sbuf_tensor(name, shape, dt))

        def sb(name, shape, dt=F32):
            return ctx.enter_context(nc.sbuf_tensor(name, shape, dt))

        self.psum = kept.enter_context(nc.psum_tensor("psum", [P, 8, 512], F32))
        self.x = keep("x", [P, TILES, D])
        self.heads_out = keep("heads_out", [P, TILES, HEADS * HD])
        self.ident = keep("ident", [P, P])
        self.ident16 = keep("ident16", [P, P], F16)
        self.wo = keep("wo", [P, PAIRS, D])
        self.ffn_w1 = keep("ffn_w1", [P, 4, D])
        self.ffn_w2 = keep("ffn_w2", [P, 4 * D])
        self.ffn_b1 = keep("ffn_b1", [P, 4])
        self.xt_hi = sb("xt_hi", [P, S], F16)
        self.xt_lo = sb("xt_lo", [P, S], F16)
        self.wkq_hi = sb("wkq_hi", [P, HEADS + 1, 2 * HD], F16)
        self.wkq_lo = sb("wkq_lo", [P, HEADS + 1, 2 * HD], F16)
        self.wv_hi = sb("wv_hi", [P, (HEADS + 1) * HD], F16)
        self.wv_lo = sb("wv_lo", [P, (HEADS + 1) * HD], F16)
        self.identb = sb("identb", [P, P], BF16)
        self.mask_ik = sb("mask_ik", [P, P], BF16)
        self.mask_ki = sb("mask_ki", [P, P], BF16)
        self.kq_hi = sb("kq_hi", [P, S], F16)
        self.kq_lo = sb("kq_lo", [P, S], F16)
        self.k_hh = [sb(f"k_hh{i}", [P, S], F16) for i in range(2)]
        self.q_hl = [sb(f"q_hl{i}", [P, S], F16) for i in range(2)]
        self.k_l1 = [sb(f"k_l1{i}", [HD + 1, S], F16) for i in range(2)]
        self.q_hm = [sb(f"q_hm{i}", [HD + 1, S], F16) for i in range(2)]
        self.v = [sb(f"v{i}", [P, TILES, VSTRIDE], F16) for i in range(2)]
        self.part_max = sb("part_max", [P, 2, 4, 4])
        self.neg_max = sb("neg_max", [P, 2, 4], F16)
        self.prob = [sb(f"prob{i}", [P, 1024]) for i in range(RING)]
        self.prob_hi = [sb(f"prob_hi{i}", [P, 1024], F16) for i in range(RING)]
        self.prob_lo = [sb(f"prob_lo{i}", [P, 1024], F16) for i in range(RING)]
        self.acc_copy = sb("acc_copy", [P, 2, 4, VW])
        self.acc_sum = sb("acc_sum", [P, 2, 4, HD])
        self.inv_sum = sb("inv_sum", [P, 2, 4, 1])
        self.scores = [self.psum[:, 2 * b:2 * b + 2, :].rearrange("p b n -> p (b n)") for b in range(2)]
        self.bank = [self.psum[:, 4 + b, :] for b in range(2)]
        self.acc = [self.psum[:, 6 + b, :] for b in range(2)]


def setup(nc, m, ins, early, sem):
    wraw = [m.heads_out[:, t, :] for t in range(3)]
    loaded, consts, turned, ready = sem("loaded"), sem("consts"), sem("turned"), sem("ready")
    x_loaded = sem("x_loaded")
    cast, moved = sem("cast"), sem("moved")
    with nc.Block() as block:

        @block.sync
        def _(sp):
            sp.dma_start(m.x[:], ins["L0_attn_x"].rearrange("a (t p) d -> p (a t) d", p=P)).then_inc(x_loaded, 16)
            for t, n in enumerate(("L0_attn_Wk", "L0_attn_Wq", "L0_attn_Wv")):
                sp.dma_start(wraw[t], ins[n]).then_inc(loaded, 16)
            sp.dma_start(m.wo[:], ins["L0_attn_Wo"].rearrange("(a p) n -> p a n", p=P)).then_inc(early, 16)
            sp.dma_start(m.ffn_w1[:], ins["L0_ffn_W1"].rearrange("(a p) n -> p a n", p=P)).then_inc(early, 16)
            sp.dma_start(m.ffn_w2[:], ins["L0_ffn_W2"]).then_inc(early, 16)
            with nc.allow_non_contiguous_dma("one small vector, once"):
                sp.dma_start(m.ffn_b1[:], ins["L0_ffn_b1"].rearrange("(a p) -> p a", p=P)).then_inc(early, 16)

        @block.gpsimd
        def _(pool):
            pool.memset(m.ident[:], 0.0).then_inc(consts, 1)
            pool.memset(m.mask_ik[:], 0.0).then_inc(consts, 1)
            pool.memset(m.mask_ki[:], 0.0).then_inc(consts, 1)
            pool.wait_ge(consts, 3)
            pool.affine_select(out=m.ident[:], in_=m.ident[:], compare_op=ALU.not_equal, fill=1.0,
                               base=0, pattern=[[-1, P]], channel_multiplier=1).then_inc(consts, 1)
            pool.affine_select(out=m.mask_ik[:], in_=m.mask_ik[:], compare_op=ALU.is_ge, fill=RAW_MASK,
                               base=0, pattern=[[-1, P]], channel_multiplier=1).then_inc(consts, 1)
            pool.affine_select(out=m.mask_ki[:], in_=m.mask_ki[:], compare_op=ALU.is_ge, fill=RAW_MASK,
                               base=0, pattern=[[1, P]], channel_multiplier=-1).then_inc(consts, 1)
            pool.wait_ge(consts, 4)
            pool.tensor_scalar(m.ident16[:], m.ident[:], 1.0, None, ALU.mult).then_inc(consts, 1)
            pool.tensor_scalar(m.identb[:], m.ident[:], 1.0, None, ALU.mult).then_inc(consts, 1)
            for side in range(2):
                pool.memset(m.v[side][:, :, 2 * HD:VW], 1.0).then_inc(consts, 1)
            for w in (m.wkq_hi[:, HEADS, :], m.wkq_lo[:, HEADS, :], m.wv_hi[:, HEADS * HD:], m.wv_lo[:, HEADS * HD:]):
                pool.memset(w, 0.0).then_inc(consts, 1)

        @block.tensor
        def _(pe):
            pe.wait_ge(consts, 4)
            pe.wait_ge(x_loaded, 16)
            for b in range(4):
                for t in range(4):
                    last = pe.transpose(m.psum[:, b, t * P:(t + 1) * P], m.x[:, 4 * b + t, :], m.ident[:])
                last.then_inc(turned, 1)

        def heads_of(w):
            return w.rearrange("p (h d) -> p h d", d=HD)

        @block.scalar
        def _(act):
            for b in range(4):
                act.wait_ge(turned, b + 1)
                act.activation(m.xt_hi[:, b * 512:(b + 1) * 512], m.psum[:, b, :], ACT.Copy).then_inc(cast, 1)
            act.wait_ge(loaded, 48)
            act.activation(m.wkq_hi[:, 0:HEADS, 0:HD], heads_of(wraw[0]), ACT.Copy).then_inc(cast, 1)
            act.activation(m.wkq_hi[:, 0:HEADS, HD:2 * HD], heads_of(wraw[1]), ACT.Copy).then_inc(cast, 1)
            act.activation(m.wv_hi[:, 0:HEADS * HD], wraw[2], ACT.Copy).then_inc(cast, 1)

        @block.vector
        def _(dve):
            for side in range(2):
                dve.memset(m.k_l1[side][HD:HD + 1, :], 1.0).then_inc(moved, 1)
            for b in range(4):
                dve.wait_ge(cast, b + 1)
                c = slice(b * 512, (b + 1) * 512)
                dve.tensor_tensor(m.xt_lo[:, c], m.psum[:, b, :], m.xt_hi[:, c], ALU.subtract).then_inc(ready, 1)
            dve.wait_ge(loaded, 48)
            for t in range(2):
                dve.wait_ge(cast, 5 + t)
                c = slice(t * HD, (t + 1) * HD)
                dve.tensor_tensor(m.wkq_lo[:, 0:HEADS, c], heads_of(wraw[t]), m.wkq_hi[:, 0:HEADS, c],
                                  ALU.subtract).then_inc(ready, 1)
            dve.wait_ge(cast, 7)
            dve.tensor_tensor(m.wv_lo[:, 0:HEADS * HD], wraw[2], m.wv_hi[:, 0:HEADS * HD],
                              ALU.subtract).then_inc(ready, 1)


def attention(nc, m, sem):
    bank_full = [sem("bank_full0"), sem("bank_full1")]
    bank_free = [sem("bank_free0"), sem("bank_free1")]
    high_done = sem("high_done")
    low_done = sem("low_done")
    kq_spread = sem("kq_spread")
    neg_max_ready = sem("neg_max_ready")
    scores_full = sem("scores_full")
    exp_done = sem("exp_done")
    low_dve = sem("low_dve")
    low_pool = sem("low_pool")
    prob_free = sem("prob_free")
    acc_free = sem("acc_free")
    inv_ready = sem("inv_ready")
    sum_ready = sem("sum_ready")
    norm_done = sem("norm_done")

    def share(u):
        return u.width * 9 // 640 * 32

    def load_wait(engine, count):
        engine.wait_ge(kq_spread, 96 * count)

    with nc.Block() as block:

        @block.tensor
        def _(pe):
            def run(job):
                full, free = bank_full[job.bank], bank_free[job.bank]
                out = m.bank[job.bank]
                if job.trip is not None or job.before > 0:
                    pe.wait_ge(free, job.before)
                if job.kind == "kq":
                    c = slice(job.what[1] * 512, (job.what[1] + 1) * 512)
                    h = job.heads_done()
                    hi = m.wkq_hi[:, bass.ds(h, 1), :].rearrange("p a n -> p (a n)")
                    lo = m.wkq_lo[:, bass.ds(h, 1), :].rearrange("p a n -> p (a n)")
                    pe.matmul(out, hi, m.xt_hi[:, c], start=True, stop=False)
                    pe.matmul(out, hi, m.xt_lo[:, c], start=False, stop=False)
                    pe.matmul(out, lo, m.xt_hi[:, c], start=False, stop=True).then_inc(full, 1)
                elif job.kind == "v":
                    h = job.heads_done()
                    hi = m.wv_hi[:, bass.ds(h * HD, HD)]
                    lo = m.wv_lo[:, bass.ds(h * HD, HD)]
                    for t in range(8):
                        tok = slice((8 * job.what[1] + t) * P, (8 * job.what[1] + t + 1) * P)
                        o = out[:, t * HD:(t + 1) * HD]
                        pe.matmul(o, m.xt_hi[:, tok], hi, start=True, stop=False)
                        pe.matmul(o, m.xt_hi[:, tok], lo, start=False, stop=False)
                        last = pe.matmul(o, m.xt_lo[:, tok], hi, start=False, stop=True)
                    last.then_inc(full, 1)
                elif job.kind == "max":
                    _, g, r, c = job.what
                    if (g, r, c) == (0, 0, 0):
                        load_wait(pe, job.heads_done() + 1)
                    tile = 4 * g + r
                    q = m.q_hl[job.side][0:HD, tile * P:(tile + 1) * P]
                    width = 512 if c < g else (r + 1) * P
                    k = m.k_hh[job.side][0:HD, c * 512:c * 512 + width]
                    last = pe.matmul(out[:, 0:width], q, k, start=True, stop=(c < g))
                    if c == g:
                        last = pe.matmul(out[:, width - P:width], m.identb[:], m.mask_ik[:],
                                         start=False, stop=True)
                    last.then_inc(full, 1)
                else:
                    g = job.what[1]
                    pe.wait_ge(neg_max_ready, job.shifts_done(g) + 1)
                    for r in range(4):
                        last = pe.matmul(out[0:1, r * P:(r + 1) * P], m.neg_max[:, g % 2, r:r + 1],
                                         m.ident16[:], start=True, stop=True)
                    last.then_inc(full, 1)

            def scores(trip, s):
                u, head = UNITS[s % NU], s // NU
                out = m.scores[s % 2]
                units = s if trip is None else trip * BODY + s
                if trip is not None or s >= 2:
                    pe.wait_ge(exp_done, units - 1)
                if u.first:
                    job, back = shift_job(trip, head, u.group)
                    pe.wait_ge(bank_free[job.bank], job.before - back + 1)
                side = head % 2
                for j, r, col in u.keys:
                    n = (4 - r) * P
                    o = out[:, col:col + n]
                    keys = slice(j * P, (j + 1) * P)
                    queries = slice((4 * u.group + r) * P, (4 * u.group + 4) * P)
                    pe.matmul(o, m.k_hh[side][:, keys], m.q_hl[side][:, queries], start=True, stop=False)
                    if j >= 4 * u.group:
                        pe.matmul(o[:, 0:P], m.identb[:], m.mask_ki[:], start=False, stop=False)
                    last = pe.matmul(o, m.k_l1[side][:, keys], m.q_hm[side][:, queries], start=False, stop=True)
                last.then_inc(scores_full, 1)

            def weigh(trip, s):
                u, side = UNITS[s % NU], s // NU
                pe.wait_ge(low_dve, trip * BODY + s + 1)
                pe.wait_ge(low_pool, trip * BODY + s + 1)
                if u.first:
                    pe.wait_ge(acc_free, trip * 2 * GROUPS + side * GROUPS + u.group + 1)
                for j, first, col in u.keys:
                    for r in range(first, 4):
                        c = slice(col + (r - first) * P, col + (r - first + 1) * P)
                        a = (r % 2) * ACC
                        o = m.acc[r // 2][:, a:a + VW]
                        pe.matmul(o, m.prob_hi[s % RING][:, c], m.v[side][:, j, 0:VW],
                                  start=(j == 0 and r % 2 == 0), stop=False, skip_group_check=True)
                        last = pe.matmul(o[:, HD:VW], m.prob_lo[s % RING][:, c], m.v[side][:, j, HD:VW],
                                         start=False, stop=(j == 4 * u.group + r), skip_group_check=True)
                last.then_inc(prob_free, 1)

            for job in jobs_of(None, None):
                run(job)
            for s in range(LEAD):
                scores(None, s)
            with pe.Fori(0, PAIRS) as trip:
                for s in range(BODY):
                    jobs = jobs_of(trip, s)
                    half = (len(jobs) + 1) // 2
                    for job in jobs[:half]:
                        run(job)
                    scores(trip, s + LEAD)
                    for job in jobs[half:]:
                        run(job)
                    weigh(trip, s)

        @block.scalar
        def _(act):
            def run(job):
                full, free = bank_full[job.bank], bank_free[job.bank]
                src = m.bank[job.bank]
                if job.kind == "max":
                    return
                act.wait_ge(full, job.before + 1)
                if job.kind == "kq":
                    c = slice(job.what[1] * 512, (job.what[1] + 1) * 512)
                    if job.what[1] == 0 and not (job.trip is None):
                        load_wait(act, job.heads_done())
                    act.activation(m.kq_hi[:, c], src, ACT.Copy).then_inc(high_done, 1)
                elif job.kind == "v":
                    v = m.v[job.side][:, 8 * job.what[1]:8 * job.what[1] + 8, HD:2 * HD]
                    act.activation(v, src.rearrange("p (t d) -> p t d", d=HD), ACT.Copy).then_inc(high_done, 1)
                else:
                    g = job.what[1]
                    act.activation(m.q_hm[job.side][HD:HD + 1, g * 512:(g + 1) * 512], src[0:1, :],
                                   ACT.Copy).then_inc(free, 1)

            def exp_high(trip, s):
                u = UNITS[s % NU]
                n = s if trip is None else trip * BODY + s
                act.wait_ge(scores_full, n + 1)
                act.wait_ge(prob_free, n + 1)
                act.activation(m.prob_hi[s % RING][:, 0:u.width], m.scores[s % 2][:, 0:u.width], ACT.Exp,
                               scale=EXP_SCALE)

            def exp_full(s):
                u = UNITS[s % NU]
                act.activation(m.prob[s % RING][:, 0:u.width], m.scores[s % 2][:, 0:u.width], ACT.Exp,
                               scale=EXP_SCALE).then_inc(exp_done, 1)

            def copy_acc(trip, s):
                g = UNITS[s % NU].group
                n = trip * 2 * GROUPS + (s // NU) * GROUPS + g
                act.wait_ge(prob_free, trip * BODY + s + 1 + RING)
                act.wait_ge(norm_done, n + 1)
                for b in range(2):
                    src = m.acc[b].rearrange("p (t n) -> p t n", n=ACC)[:, :, 0:VW]
                    last = act.activation(m.acc_copy[:, g % 2, 2 * b:2 * b + 2, :], src, ACT.Copy)
                last.then_inc(acc_free, 1)

            for job in jobs_of(None, None):
                run(job)
            for s in range(LEAD - 1):
                exp_high(None, s)
                exp_full(s)
            with act.Fori(0, PAIRS) as trip:
                for s in range(BODY):
                    exp_high(trip, s + LEAD - 1)
                    if s > 0 and UNITS[(s - 1) % NU].last:
                        copy_acc(trip, s - 1)
                    for job in jobs_of(trip, s):
                        run(job)
                    exp_full(s + LEAD - 1)
                copy_acc(trip, BODY - 1)

        @block.vector
        def _(dve):
            def run(job):
                full, free = bank_full[job.bank], bank_free[job.bank]
                src = m.bank[job.bank]
                if job.kind == "shift":
                    return
                if job.kind == "max":
                    _, g, r, c = job.what
                    dve.wait_ge(full, job.before + 1)
                    width = 512 if c < g else (r + 1) * P
                    dve.tensor_reduce(m.part_max[:, g % 2, r, c:c + 1], src[:, 0:width], AX, ALU.max).then_inc(free, 1)
                    if (r, c) == (3, g):
                        dve.wait_ge(free, job.before + 1)
                        dve.wait_ge(bank_free[1 - job.bank], job.before + job.bank)
                        dve.tensor_reduce(m.neg_max[:, g % 2, :], m.part_max[:, g % 2, :, 0:g + 1], AX, ALU.max,
                                          negate=True).then_inc(neg_max_ready, 1)
                    return
                k = job.what[1] + (4 if job.kind == "v" else 0)
                dve.wait_ge(high_done, job.heads_done() * 6 + k + 1)
                if job.kind == "kq":
                    c = slice(job.what[1] * 512, (job.what[1] + 1) * 512)
                    dve.tensor_tensor(m.kq_lo[:, c], src, m.kq_hi[:, c], ALU.subtract).then_inc(free, 1)
                else:
                    t = slice(8 * job.what[1], 8 * job.what[1] + 8)
                    dve.tensor_tensor(m.v[job.side][:, t, 0:HD], src.rearrange("p (t d) -> p t d", d=HD),
                                      m.v[job.side][:, t, HD:2 * HD], ALU.subtract).then_inc(free, 1)

            def low(trip, s):
                u = UNITS[s % NU]
                dve.wait_ge(exp_done, trip * BODY + s + 1)
                c = slice(0, share(u))
                b = s % RING
                dve.tensor_tensor(m.prob_lo[b][:, c], m.prob[b][:, c], m.prob_hi[b][:, c],
                                  ALU.subtract).then_inc(low_dve, 1)

            def invert(trip, s):
                g = UNITS[s % NU].group
                n = trip * 2 * GROUPS + (s // NU) * GROUPS + g
                dve.wait_ge(acc_free, n + 2)
                dve.reciprocal(m.inv_sum[:, g % 2, :, :], m.acc_copy[:, g % 2, :, 2 * HD:VW]).then_inc(inv_ready, 1)

            for job in jobs_of(None, None):
                run(job)
            with dve.Fori(0, PAIRS) as trip:
                for s in range(BODY):
                    low(trip, s)
                    for job in jobs_of(trip, s):
                        run(job)
                    if s > 0 and UNITS[(s - 1) % NU].last:
                        invert(trip, s - 1)
                invert(trip, BODY - 1)

        @block.gpsimd
        def _(pool):
            def low(trip, s):
                u = UNITS[s % NU]
                pool.wait_ge(exp_done, trip * BODY + s + 1)
                c = slice(share(u), u.width)
                b = s % RING
                pool.tensor_tensor(m.prob_lo[b][:, c], m.prob[b][:, c], m.prob_hi[b][:, c],
                                   ALU.subtract).then_inc(low_pool, 1)

            def normalise(trip, s):
                u, side = UNITS[s % NU], s // NU
                g = u.group
                n = trip * 2 * GROUPS + side * GROUPS + g
                pool.wait_ge(inv_ready, n + 1)
                a = m.acc_copy[:, g % 2, :, :]
                pool.tensor_tensor(m.acc_sum[:, g % 2, :, :], a[:, :, 0:HD], a[:, :, HD:2 * HD],
                                   ALU.add).then_inc(sum_ready, 1)
                pool.wait_ge(sum_ready, n + 1)
                out = m.heads_out[:, 4 * g:4 * g + 4, bass.ds(trip * 2 * HD + side * HD, HD)]
                pool.tensor_tensor(out, m.acc_sum[:, g % 2, :, :],
                                   m.inv_sum[:, g % 2, :, :].broadcast_to([P, 4, HD]), ALU.mult).then_inc(norm_done, 1)

            pool.sem_inc(prob_free, RING)
            pool.sem_inc(acc_free, 1)
            pool.sem_inc(norm_done, 2)
            with pool.Fori(0, PAIRS) as trip:
                for s in range(BODY):
                    low(trip, s)
                    if s > 1 and UNITS[(s - 2) % NU].last:
                        normalise(trip, s - 2)
                normalise(trip, BODY - 1)

        @block.sync
        def _(sp):
            def spread(heads, side):
                hi, lo = m.kq_hi, m.kq_lo
                for dst, src in ((m.k_hh[side][0:HD, :], hi[0:HD, :]), (m.q_hl[side][0:HD, :], hi[HD:P, :]),
                                 (m.k_hh[side][HD:P, :], hi[0:HD, :]), (m.q_hl[side][HD:P, :], lo[HD:P, :]),
                                 (m.k_l1[side][0:HD, :], lo[0:HD, :]), (m.q_hm[side][0:HD, :], hi[HD:P, :])):
                    sp.dma_start(dst, src).then_inc(kq_spread, 16)

            last = [j for j in jobs_of(None, None) if j.kind == "kq"][-2:]
            for j in last:
                sp.wait_ge(bank_free[j.bank], j.before + 1)
            spread(0, 0)
            with sp.Fori(0, PAIRS) as trip:
                for head in range(2):
                    for j in [j for j in jobs_of(trip, head * NU + LAST_KQ) if j.kind == "kq"]:
                        sp.wait_ge(bank_free[j.bank], j.before + 1)
                    spread(None, (head + 1) % 2)


ROUND = 12582912.0
EPS = 1e-5
FF = 512
FT = FF // P
Q1 = 64
H1 = 4
SCALE1 = H1 ** -0.5
EXPERTS = 16
CAP = S // EXPERTS
SLOTS = 8
G = 512
PARAMS = ["L1_attn_bias_q", "L1_attn_bias_k", "L1_attn_q_alpha", "L1_attn_k_alpha", "L1_attn_v_alpha",
          "L1_attn_q_zp", "L1_attn_k_zp", "L1_attn_v_zp", "L1_attn_attn_alpha", "L1_attn_attn_zp"]
BQ, BK, QA, KA, VA, QZ, KZ, VZ, AA, AZ = range(10)


class Chain:

    def __init__(self, engine, sem, base=0):
        self.engine, self.sem, self.base, self.count = engine, sem, base, 0

    def mark(self, instruction):
        instruction.then_inc(self.sem, 1)
        self.count += 1

    def wait(self):
        self.engine.wait_ge(self.sem, self.base + self.count)

    def step(self, instruction):
        self.mark(instruction)
        self.wait()


def moments(dve, c, stats, mv):
    c.mark(dve.tensor_tensor(mv[:, :, 0:2], stats[:, :, 1:3], stats[:, :, 4:6], ALU.add))
    c.step(dve.tensor_tensor(mv[:, :, 2:3], stats[:, :, 1:2], stats[:, :, 4:5], ALU.subtract))
    c.step(dve.scalar_tensor_tensor(mv[:, :, 3:4], mv[:, :, 2:3], 0.25, mv[:, :, 2:3], ALU.mult, ALU.mult))
    c.mark(dve.tensor_scalar(mv[:, :, 0:1], mv[:, :, 0:1], 0.5, None, ALU.mult))
    c.step(dve.scalar_tensor_tensor(mv[:, :, 1:2], mv[:, :, 1:2], 1.0 / D, mv[:, :, 3:4], ALU.mult, ALU.add))


class Tail:

    def __init__(self, nc, m, ctx):
        def sb(name, shape, dt=F32):
            return ctx.enter_context(nc.sbuf_tensor(name, shape, dt))

        self.nc = nc
        self.ew1 = sb("ew1", [P, SLOTS, FF])
        self.ew2 = sb("ew2", [P, SLOTS, FT, D])
        self.eb2 = sb("eb2", [P, EXPERTS, D])
        self.x2 = sb("x2", [P, TILES, D])
        self.x2t = sb("x2t", [P, 2, S], F16)
        self.wkq1 = sb("wkq1", [P, 3 * Q1], F16)
        self.row = sb("row", [1, 10, HEADS])
        self.aw_row = sb("aw_row", [1, 3 * Q1])
        self.bad = sb("bad", [1, 1], I32)
        self.y1 = m.x
        self.free = m.heads_out[:].rearrange("p t n -> p (t n)")
        self.ones = sb("ones", [P, P])
        self.bo_b = sb("bo_b", [P, D])
        self.b2_b = sb("b2_b", [P, D])
        self.pb_b = sb("pb_b", [P, D])
        self.bg_b = sb("bg_b", [P, EXPERTS])
        self.pw = sb("pw", [P, Q1])
        self.pa = sb("pa", [P, 1])

    def scope(self, ctx):
        self.sb = lambda name, shape, dt=F32: ctx.enter_context(self.nc.sbuf_tensor(name, shape, dt))


def load_expert(queue, t, ins, e):
    s = e % SLOTS
    queue.dma_start(t.ew1[:, s, :], ins["L1_ffn_W1"][e, :, :]).then_inc(t.w_loaded[s], 16)
    queue.dma_start(t.ew2[:, s, :, :], ins["L1_ffn_W2"][e, :, :].rearrange("(f p) n -> p f n", p=P))\
        .then_inc(t.w_loaded[s], 16)


def layer0_rest(nc, m, t, ins, early, sem):
    sb = t.sb
    wo_hi = sb("wo_hi", [P, PAIRS, D], F16)
    wo_lo = sb("wo_lo", [P, PAIRS, D], F16)
    w1q = sb("w1q", [P, FF], F16)
    w2q = sb("w2q", [P, FF], F16)
    w1t = sb("w1t", [P, FF], F16)
    w2t = sb("w2t", [P, FT, D], F16)
    qkv = sb("qkv", [Q1, 3, D])
    qkv_a = sb("qkv_a", [Q1, 3, 1])
    qkv_ia = sb("qkv_ia", [Q1, 3, 1])
    qkv_q = sb("qkv_q", [Q1, 3, D], F16)
    part = sb("part", [P, 2])
    gamma = sb("gamma", [P, 2])
    inv_gamma = sb("inv_gamma", [P, 2])
    rounded = sb("rounded", [P, FF])
    ot_hi = [sb(f"ot_hi{i}", [P, 4, P], F16) for i in range(2)]
    ot_lo = [sb(f"ot_lo{i}", [P, 4, P], F16) for i in range(2)]
    r = sb("r", [P, 4, D])
    stats = sb("stats", [P, 4, 6])
    mv = sb("mv", [P, 4, 4])
    rstd = sb("rstd", [P, 4])
    dev = sb("dev", [P, 4])
    x1 = sb("x1", [P, 4, D])
    x1b = sb("x1b", [P, 4, D])
    x_hi = sb("x_hi", [P, 4, D], F16)
    x_lo = sb("x_lo", [P, 4, D], F16)
    x1t = sb("x1t", [P, 2, G], F16)
    up = sb("up", [P, FT, G])
    up_hi = sb("up_hi", [P, FT, G], F16)
    up_lo = sb("up_lo", [P, FT, G], F16)
    turned_o = [m.psum[:, b, :] for b in range(2)]
    y_bank, x_bank, down_bank = m.psum[:, 2, :], m.psum[:, 3, :], m.psum[:, 6, :]
    up_bank = [m.psum[:, 4 + b, :] for b in range(2)]
    halves = lambda bank: bank.bitcast(F16)

    loaded = sem("r_loaded")
    bo_loaded, b2_loaded, qkv_loaded = sem("bo_loaded"), sem("b2_loaded"), sem("qkv_loaded")
    xb_done = sem("xb_done")
    wo_hi_done, wo_lo_done = sem("wo_hi_done"), sem("wo_lo_done")
    sums_made, sums_added = sem("sums_made"), sem("sums_added")
    prep = sem("r_prep")
    scale_made = sem("scale_made")
    rounding = sem("rounding")
    quantised = sem("quantised")
    w_turned, w_placed = sem("w_turned"), sem("w_placed")
    o_turned = sem("o_turned")
    ot_hi_done, ot_lo_done = sem("ot_hi_done"), sem("ot_lo_done")
    y_done, y_read = sem("y_done"), sem("y_read")
    dev_asked, dev_done = sem("dev_asked"), sem("dev_done")
    x_ready = sem("x_ready")
    x_hi_done, x_lo_done, x1b_done = sem("x_hi_done"), sem("x_lo_done"), sem("x1b_done")
    x_turned, xt_done = sem("x_turned"), sem("xt_done")
    up_full, up_done = sem("up_full"), sem("up_done")
    up_lo_done, down_done = sem("up_lo_done"), sem("down_done")
    chain = sem("r_chain")
    PER = 27
    LAST = GROUPS - 1

    with nc.Block() as block:

        @block.sync
        def _(sp):
            with nc.allow_non_contiguous_dma("small parameters, once"):
                sp.dma_start(t.bo_b[:], ins["L0_attn_bo"].partition_broadcast(P)).then_inc(bo_loaded, 16)
                sp.dma_start(qkv[:], ins["L1_attn_qkv_w"].rearrange("(a p) n -> p a n", p=Q1)).then_inc(qkv_loaded, 16)
                sp.dma_start(qkv_a[:], ins["L1_attn_qkv_alpha"].rearrange("(a p) n -> p a n", p=Q1))\
                    .then_inc(qkv_loaded, 16)
                sp.dma_start(t.b2_b[:], ins["L0_ffn_b2"].partition_broadcast(P)).then_inc(b2_loaded, 16)
                loads = [(t.aw_row[:], ins["L1_attn_qkv_alpha"].rearrange("o a -> a o")),
                         (t.pb_b[:], ins["L1_attn_proj_b"].partition_broadcast(P)),
                         (t.bg_b[:], ins["L1_ffn_bg"].partition_broadcast(P)),
                         (t.pw[:], ins["L1_attn_proj_w"]),
                         (t.pa[:], ins["L1_attn_proj_alpha"])]
                loads += [(t.row[:, i, :], ins[n].rearrange("a h b c -> (a b c) h")) for i, n in enumerate(PARAMS)]
                loads += [(t.eb2[:], ins["L1_ffn_b2"].partition_broadcast(P))]
                for dst, src in loads:
                    sp.dma_start(dst, src).then_inc(loaded, 16)
            for e in range(SLOTS):
                load_expert(sp, t, ins, e)
            sp.wait_ge(loaded, 16 * len(loads))

        @block.tensor
        def _(pe):
            def turn_o(g, j):
                for a in range(4):
                    col = ((j % 2) * 4 + a) * P
                    o = m.heads_out[:, g * 4 + j // 2, col:col + P]
                    last = pe.transpose(turned_o[j % 2][:, a * P:(a + 1) * P], o, m.ident[:])
                last.then_inc(o_turned, 1)

            def project(g, j):
                n = g * 8 + j + 1
                pe.wait_ge(ot_hi_done, n)
                pe.wait_ge(ot_lo_done, n)
                if j == 0:
                    pe.wait_ge(y_read, g + 1)
                out = y_bank[:, (j // 2) * P:(j // 2 + 1) * P]
                hi, lo = ot_hi[j % 2], ot_lo[j % 2]
                for a in range(4):
                    w = (j % 2) * 4 + a
                    pe.matmul(out, hi[:, a, :], wo_hi[:, w, :], start=(w == 0), stop=False)
                    pe.matmul(out, hi[:, a, :], wo_lo[:, w, :], start=False, stop=False)
                    last = pe.matmul(out, lo[:, a, :], wo_hi[:, w, :], start=False, stop=(w == PAIRS - 1))
                if j == 7:
                    last.then_inc(y_done, 1)

            def turn_x(g, n):
                pe.wait_ge(x_hi_done, g * 2 + n + 1)
                pe.wait_ge(x_lo_done, g * 2 + n + 1)
                for a, x in enumerate((x_hi, x_lo)):
                    for k in range(4):
                        last = pe.transpose(halves(x_bank)[:, a * G + k * P:a * G + (k + 1) * P], x[:, k, :], m.ident16[:])
                last.then_inc(x_turned, 1)

            def up_product(g, f):
                if f == 0:
                    pe.wait_ge(xt_done, g * 2 + 1)
                if f >= 2:
                    pe.wait_ge(up_done, g * FT + f - 1)
                w = w1t[:, f * P:(f + 1) * P]
                pe.matmul(up_bank[f % 2], w, x1t[:, 0, :], start=True, stop=False)
                pe.matmul(up_bank[f % 2], w, x1t[:, 1, :], start=False, stop=True).then_inc(up_full, 1)

            def down_product(g):
                pe.wait_ge(up_lo_done, (g + 1) * FT)
                for k in range(4):
                    out = down_bank[:, k * P:(k + 1) * P]
                    for f in range(FT):
                        pe.matmul(out, up_hi[:, f, k * P:(k + 1) * P], w2t[:, f, :], start=(f == 0), stop=False)
                        last = pe.matmul(out, up_lo[:, f, k * P:(k + 1) * P], w2t[:, f, :], start=False, stop=(f == FT - 1))
                last.then_inc(down_done, 1)

            pe.wait_ge(sums_made, 1)
            pe.matmul(down_bank[:, 0:2], t.ones[:], part[:], start=True, stop=True).then_inc(sums_added, 1)
            pe.wait_ge(wo_hi_done, 1)
            pe.wait_ge(wo_lo_done, 1)
            for j in range(8):
                turn_o(0, j)
                if j:
                    project(0, j - 1)
            project(0, 7)
            pe.wait_ge(quantised, 1)
            for f in range(FT):
                pe.transpose(halves(up_bank[0])[:, f * P:(f + 1) * P], w1q[:, f * P:(f + 1) * P], m.ident16[:])
                last = pe.transpose(halves(up_bank[1])[:, f * P:(f + 1) * P], w2q[:, f * P:(f + 1) * P], m.ident16[:])
            last.then_inc(w_turned, 1)
            pe.wait_ge(quantised, 2)
            for k in range(3):
                last = pe.transpose(halves(x_bank)[:, k * Q1:(k + 1) * Q1], qkv_q[:, k, :], m.ident16[0:Q1, 0:Q1])
            last.then_inc(w_turned, 1)
            pe.wait_ge(w_placed, 2)

            def trip(g, following):
                def half(j):
                    if following:
                        if j < 8:
                            turn_o(g + 1, j)
                        if j:
                            project(g + 1, j - 1)

                half(0)
                half(1)
                turn_x(g, 0)
                half(2)
                up_product(g, 0)
                up_product(g, 1)
                half(3)
                up_product(g, 2)
                up_product(g, 3)
                half(4)
                half(5)
                down_product(g)
                half(6)
                half(7)
                half(8)
                turn_x(g, 1)

            for g in range(GROUPS):
                trip(g, g < LAST)

        @block.scalar
        def _(act):
            act.wait_ge(early, 16 * 4)
            act.activation(wo_hi[:], m.wo[:], ACT.Copy).then_inc(wo_hi_done, 1)

            def high_o(g, j):
                act.wait_ge(o_turned, g * 8 + j + 1)
                act.activation(ot_hi[j % 2][:].rearrange("p a n -> p (a n)"), turned_o[j % 2], ACT.Copy).then_inc(ot_hi_done, 1)

            def deviation(g, n):
                act.wait_ge(dev_asked, g * 2 + n + 1)
                act.activation(dev[:], rstd[:], ACT.Sqrt).then_inc(dev_done, 1)

            def high_x(g, n):
                act.wait_ge(x_ready, g * 2 + n + 1)
                x = x1[:] if n == 0 else t.x2[:, g * 4:g * 4 + 4, :] if isinstance(g, int) else t.x2[:, bass.ds(g * 4, 4), :]
                act.activation(x_hi[:], x, ACT.Copy).then_inc(x_hi_done, 1)

            def place_x(g, n):
                dst = x1t[:] if n == 0 else t.x2t[:, :, g * G:(g + 1) * G] if isinstance(g, int) else \
                    t.x2t[:, :, bass.ds(g * G, G)]
                act.wait_ge(x_turned, g * 2 + n + 1)
                act.activation(dst, halves(x_bank).rearrange("p (a n) -> p a n", a=2), ACT.Copy).then_inc(xt_done, 1)

            def relu(g, f):
                act.wait_ge(up_full, g * FT + f + 1)
                act.activation(up_hi[:, f, :], up_bank[f % 2], ACT.Relu, bias=m.ffn_b1[:, f:f + 1])
                act.activation(up[:, f, :], up_bank[f % 2], ACT.Relu, bias=m.ffn_b1[:, f:f + 1]).then_inc(up_done, 1)

            for j in range(8):
                high_o(0, j)
            act.wait_ge(w_turned, 1)
            act.activation(w1t[:], halves(up_bank[0])[:, 0:FF], ACT.Copy).then_inc(w_placed, 1)
            act.wait_ge(w_turned, 2)
            act.activation(w2t[:].rearrange("p a n -> p (a n)"), halves(up_bank[1])[:, 0:FF], ACT.Copy)
            act.activation(t.wkq1[:], halves(x_bank)[:, 0:3 * Q1], ACT.Copy).then_inc(w_placed, 1)

            def trip(g, following):
                def half(j):
                    if following:
                        high_o(g + 1, j)

                half(0)
                deviation(g, 0)
                half(1)
                high_x(g, 0)
                place_x(g, 0)
                half(2)
                relu(g, 0)
                relu(g, 1)
                half(3)
                relu(g, 2)
                relu(g, 3)
                for j in range(4, 7):
                    half(j)
                deviation(g, 1)
                half(7)
                high_x(g, 1)
                place_x(g, 1)

            with act.Fori(0, LAST) as g:
                trip(g, True)
            trip(LAST, False)

        @block.vector
        def _(dve):
            c = Chain(dve, prep)
            c.step(dve.memset(t.ones[:], 1.0))
            dve.wait_ge(early, 16 * 4)
            dve.tensor_reduce(part[:, 0:1], m.ffn_w1[:].rearrange("p a n -> p (a n)"), AX, ALU.add,
                              apply_absolute_value=True)
            dve.tensor_reduce(part[:, 1:2], m.ffn_w2[:], AX, ALU.add, apply_absolute_value=True).then_inc(sums_made, 1)
            dve.wait_ge(wo_hi_done, 1)
            dve.tensor_tensor(wo_lo[:], m.wo[:], wo_hi[:], ALU.subtract).then_inc(wo_lo_done, 1)
            dve.wait_ge(sums_added, 1)
            c.step(dve.tensor_scalar(gamma[:], down_bank[:, 0:2], 1.0 / (FF * D), EPS, ALU.mult, ALU.add))
            dve.wait_ge(qkv_loaded, 32)
            dve.reciprocal(inv_gamma[:], gamma[:])
            dve.reciprocal(qkv_ia[:], qkv_a[:]).then_inc(scale_made, 1)

            def low_o(g, j):
                dve.wait_ge(ot_hi_done, g * 8 + j + 1)
                dve.tensor_tensor(ot_lo[j % 2][:].rearrange("p a n -> p (a n)"), turned_o[j % 2],
                                  ot_hi[j % 2][:].rearrange("p a n -> p (a n)"), ALU.subtract).then_inc(ot_lo_done, 1)

            for j in range(8):
                low_o(0, j)

            def trip(g, following):
                c = Chain(dve, chain, g * PER)
                x2 = t.x2[:, g * 4:g * 4 + 4, :] if isinstance(g, int) else t.x2[:, bass.ds(g * 4, 4), :]
                xb = m.x[:, g * 4:g * 4 + 4, :] if isinstance(g, int) else m.x[:, bass.ds(g * 4, 4), :]

                def low(*halves_):
                    if following:
                        for j in halves_:
                            low_o(g + 1, j)

                def norm(n, x, before_moments, before_rstd):
                    for k in range(4):
                        c.mark(dve.bn_stats(stats[:, k, :], r[:, k, :]))
                    low(*before_moments)
                    c.wait()
                    moments(dve, c, stats, mv)
                    dve.tensor_scalar(rstd[:], mv[:, :, 1], EPS, None, ALU.add).then_inc(dev_asked, 1)
                    low(*before_rstd)
                    dve.wait_ge(dev_done, g * 2 + n + 1)
                    c.step(dve.reciprocal(rstd[:], dev[:]))
                    for k in range(4):
                        last = dve.tensor_scalar(x[:, k, :], r[:, k, :], mv[:, k, 0:1], rstd[:, k:k + 1],
                                                 ALU.subtract, ALU.mult)
                        if k < 3:
                            c.mark(last)
                    last.then_inc(x_ready, 1)
                    dve.wait_ge(x_hi_done, g * 2 + n + 1)
                    dve.tensor_tensor(x_lo[:], x, x_hi[:], ALU.subtract).then_inc(x_lo_done, 1)

                dve.wait_ge(y_done, g + 1)
                dve.tensor_tensor(r[:], y_bank.rearrange("p (a n) -> p a n", n=D), xb, ALU.add).then_inc(y_read, 1)
                dve.wait_ge(y_read, g + 2)
                norm(0, x1[:], (0,), (1,))
                dve.tensor_tensor(x1b[:], x1[:], t.b2_b[:].unsqueeze(1).broadcast_to([P, 4, D]), ALU.add)\
                    .then_inc(x1b_done, 1)
                low(2, 3, 4, 5)
                dve.wait_ge(down_done, g + 1)
                dve.wait_ge(x1b_done, g + 1)
                c.step(dve.tensor_tensor(r[:], down_bank.rearrange("p (a n) -> p a n", n=D), x1b[:], ALU.add))
                norm(1, x2, (6,), (7,))
                assert c.count == PER, c.count

            dve.wait_ge(xb_done, 1)
            dve.wait_ge(b2_loaded, 16)
            with dve.Fori(0, LAST) as g:
                trip(g, True)
            trip(LAST, False)

        @block.gpsimd
        def _(pool):
            pool.sem_inc(y_read, 1)
            pool.wait_ge(scale_made, 1)
            count = 0

            def step(i):
                nonlocal count
                i.then_inc(rounding, 1)
                count += 1
                pool.wait_ge(rounding, count)

            for k, (w, q) in enumerate(((m.ffn_w1[:].rearrange("p a n -> p (a n)"), w1q), (m.ffn_w2[:], w2q))):
                step(pool.tensor_scalar(rounded[:], w, inv_gamma[:, k:k + 1], ROUND, ALU.mult, ALU.add))
                step(pool.tensor_scalar(rounded[:], rounded[:], -ROUND, 1.0, ALU.add, ALU.min))
                last = pool.tensor_scalar(q[:], rounded[:], -1.0, None, ALU.max)
                if k == 0:
                    step(last)
            last.then_inc(quantised, 1)
            pool.wait_ge(quantised, 1)
            for k in range(3):
                w = rounded[0:Q1, k * D:(k + 1) * D]
                step(pool.tensor_scalar(w, qkv[:, k, :], qkv_ia[:, k, :], -8.0, ALU.mult, ALU.max))
                step(pool.tensor_scalar(w, w, 7.0, ROUND, ALU.min, ALU.add))
                last = pool.tensor_scalar(qkv_q[:, k, :], w, -ROUND, None, ALU.add)
                if k < 2:
                    step(last)
            last.then_inc(quantised, 1)
            pool.wait_ge(bo_loaded, 16)
            pool.tensor_tensor(m.x[:], m.x[:], t.bo_b[:].unsqueeze(1).broadcast_to([P, TILES, D]),
                               ALU.add).then_inc(xb_done, 1)

            def trip(g):
                for f in range(FT):
                    pool.wait_ge(up_done, g * FT + f + 1)
                    pool.tensor_tensor(up_lo[:, f, :], up[:, f, :], up_hi[:, f, :], ALU.subtract).then_inc(up_lo_done, 1)

            with pool.Fori(0, GROUPS) as g:
                trip(g)


def turn_rows(pe, out, cols, ident):
    return pe.matmul(out, cols, ident, start=True, stop=True)


def attention1_check(nc, m, t, sem):
    sb = t.sb
    ext = sb("ext", [P, 2, 4])
    ext1 = sb("ext1", [P, 2])
    v = sb("v_row", [1, 2, P])
    mag = sb("mag", [1, 3, P])
    small = sb("small", [1, 8, HEADS])
    prm = sb("prm", [1, 8, HEADS])
    zero_done, t.zeroed = sem("c_zero"), sem("c_zeroed")
    t.rows_in = nc.dram_tensor("expert_rows", (S, D), F32, kind="Internal").ap()
    full, done, chain, asked, expd = (sem("c_full"), sem("c_done"), sem("c_chain"), sem("c_asked"), sem("c_exp"))
    with nc.Block() as block:

        @block.tensor
        def _(pe):
            for c in range(4):
                cols = slice(c * G, (c + 1) * G)
                pe.matmul(m.psum[:, c, :], t.wkq1[:, 0:P], t.x2t[:, 0, cols], start=True, stop=False)
                pe.matmul(m.psum[:, c, :], t.wkq1[:, 0:P], t.x2t[:, 1, cols], start=False, stop=True).then_inc(full, 1)
            pe.wait_ge(done, 1)
            for k in range(2):
                last = turn_rows(pe, m.psum[0:1, 4, k * P:(k + 1) * P], ext1[:, k:k + 1], m.ident[:])
            last.then_inc(full, 1)

        @block.vector
        def _(dve):
            c = Chain(dve, chain)
            for k in range(4):
                dve.wait_ge(full, k + 1)
                c.mark(dve.tensor_reduce(ext[:, 0, k:k + 1], m.psum[:, k, :], AX, ALU.max))
                c.mark(dve.tensor_reduce(ext[:, 1, k:k + 1], m.psum[:, k, :], AX, ALU.min))
            c.wait()
            c.step(dve.tensor_reduce(ext1[:, 0:1], ext[:, 0, :], AX, ALU.max))
            dve.tensor_reduce(ext1[:, 1:2], ext[:, 1, :], AX, ALU.min).then_inc(done, 1)

            def both(x):
                return x.unsqueeze(3).broadcast_to([1, 2, HEADS, H1])

            c.mark(dve.reciprocal(prm[:, 0:2, :], t.row[:, QA:QA + 2, :]))
            c.step(dve.tensor_scalar(prm[:, 2:4, :], t.row[:, QZ:QZ + 2, :], ROUND, -ROUND, ALU.add, ALU.add))
            dve.wait_ge(full, 5)
            for k in range(2):
                w = v[:, k, :]
                q = w.rearrange("a (b h d) -> a b h d", b=2, d=H1)
                c.step(dve.tensor_tensor(w, m.psum[0:1, 4, k * P:(k + 1) * P], t.aw_row[:, 0:P], ALU.mult))
                c.step(dve.tensor_tensor(q, q, both(t.row[:, BQ:BQ + 2, :]), ALU.add))
                c.step(dve.tensor_tensor(q, q, both(prm[:, 0:2, :]), ALU.mult))
                c.step(dve.tensor_tensor(q, q, both(prm[:, 2:4, :]), ALU.add))
                c.step(dve.tensor_scalar(w, w, -8.0, 7.0, ALU.max, ALU.min))
                c.step(dve.tensor_scalar(w, w, ROUND, -ROUND, ALU.add, ALU.add))
                c.step(dve.tensor_tensor(q, q, both(prm[:, 2:4, :]), ALU.subtract))
                c.step(dve.tensor_tensor(q, q, both(t.row[:, QA:QA + 2, :]), ALU.mult))
            c.step(dve.scalar_tensor_tensor(mag[:, 0:2, :], v[:], -1.0, v[:], ALU.mult, ALU.max))
            c.step(dve.tensor_tensor(mag[:, 0, 0:Q1], mag[:, 0, 0:Q1], mag[:, 1, 0:Q1], ALU.max))
            c.step(dve.tensor_tensor(mag[:, 2, Q1:P], v[:, 0, Q1:P], v[:, 1, Q1:P], ALU.subtract))
            c.step(dve.scalar_tensor_tensor(mag[:, 2, Q1:P], mag[:, 2, Q1:P], -1.0, mag[:, 2, Q1:P], ALU.mult, ALU.max))
            c.step(dve.tensor_tensor(mag[:, 2, 0:Q1], mag[:, 0, 0:Q1], mag[:, 2, Q1:P], ALU.mult))
            c.step(dve.tensor_reduce(small[:, 0, :], mag[:, 2, 0:Q1].rearrange("a (h d) -> a h d", d=H1), AX, ALU.add))
            dve.tensor_scalar(small[:, 1, :], small[:, 0, :], -SCALE1, None, ALU.mult).then_inc(asked, 1)
            dve.wait_ge(expd, 1)
            c.step(dve.tensor_tensor(small[:, 3, :], small[:, 2, :], t.row[:, AA, :], ALU.mult))
            c.step(dve.tensor_scalar(small[:, 3, :], small[:, 3, :], 2.02 / S, None, ALU.is_gt))
            c.step(dve.tensor_scalar(small[:, 4, :], t.row[:, AZ, :], ROUND, -ROUND, ALU.add, ALU.add))
            c.mark(dve.tensor_scalar(small[:, 5, :], small[:, 4, :], -128.0, None, ALU.is_ge))
            c.mark(dve.tensor_scalar(small[:, 6, :], small[:, 4, :], 127.0, None, ALU.is_le))
            c.wait()
            c.step(dve.tensor_tensor(small[:, 3, :], small[:, 3, :], small[:, 5, :], ALU.mult))
            c.step(dve.tensor_tensor(small[:, 3, :], small[:, 3, :], small[:, 6, :], ALU.mult))
            c.step(dve.tensor_reduce(small[:, 7, 0:1], small[:, 3, :], AX, ALU.min))
            c.step(dve.tensor_scalar(t.bad[:], small[:, 7, 0:1], -1.0, 1.0, ALU.mult, ALU.add))

        @block.gpsimd
        def _(pool):
            pool.memset(t.y1[:], 0.0).then_inc(zero_done, 1)

        @block.sync
        def _(sp):
            sp.wait_ge(zero_done, 1)
            sp.dma_start(t.rows_in.rearrange("(e c) d -> c e d", c=P), t.y1[:]).then_inc(t.zeroed, 16)
            sp.wait_ge(t.zeroed, 16)

        @block.scalar
        def _(act):
            act.wait_ge(asked, 1)
            act.activation(small[:, 2, :], small[:, 1, :], ACT.Exp).then_inc(expd, 1)


def attention1_general(nc, m, t, sem):
    sb = t.sb
    qt = t.free[0:Q1, 0:3 * S].rearrange("p (a n) -> p a n", n=S)
    vn = sb("g_vn", [P, TILES, Q1])
    rows = sb("g_rows", [1, 15, Q1])
    cols = sb("g_cols", [Q1, 15])
    arow = sb("g_arow", [1, 3, HEADS])
    acols = sb("g_acols", [P, 3, HEADS])
    sel = sb("g_sel", [Q1, HEADS])
    seln = sb("g_seln", [Q1, HEADS])
    qi = sb("g_qi", [Q1, P])
    hp = sb("g_hp", [P, 3])
    nmax = sb("g_nmax", [P, 1])
    tot = sb("g_tot", [P, 1])
    inv = sb("g_inv", [P, 1])
    e = t.free[:, 3 * S:4 * S]
    at = t.free[:, 4 * S:5 * S]
    o1 = sb("g_o1", [P, TILES, Q1])
    ot = sb("g_ot", [Q1, P])
    wp = sb("g_wp", [P, Q1])
    wpt = sb("g_wpt", [Q1, D])
    oi = sb("g_oi", [P, Q1])
    pe_done, dve_done, act_done, pool_done = sem("g_pe"), sem("g_dve"), sem("g_act"), sem("g_pool")
    wp_rounded = sem("g_wp")
    flat = lambda a: m.psum[:, a:a + 4, :].rearrange("p b n -> p (b n)")
    PE0, DVE0 = 7, 35
    PE1, DVE1, ACT1 = 3, 13, 1
    PE2, DVE2 = 2, 3

    with nc.Block() as block:

        @block.gpsimd
        def _(pool):
            taken = pool.value_load(t.bad[0:1, 0:1], min_val=0, max_val=1)
            with pool.If(taken):
                pool.memset(seln[:], 1.0).then_inc(pool_done, 1)
                pool.wait_ge(pool_done, 1)
                pool.affine_select(out=sel[:], in_=seln[:], compare_op=ALU.is_ge, fill=0.0, base=0,
                                   pattern=[[-H1, HEADS]], channel_multiplier=1).then_inc(pool_done, 1)
                pool.wait_ge(pool_done, 2)
                pool.affine_select(out=sel[:], in_=sel[:], compare_op=ALU.is_ge, fill=0.0, base=H1 - 1,
                                   pattern=[[H1, HEADS]], channel_multiplier=-1).then_inc(pool_done, 1)

        @block.tensor
        def _(pe):
            taken = pe.value_load(t.bad[0:1, 0:1], min_val=0, max_val=1)
            with pe.If(taken):
                pe.wait_ge(dve_done, 10)
                for k in range(15):
                    pe.matmul(m.psum[0:Q1, 4, 2 * k:2 * k + 1], rows[:, k, :], t.ones[0:1, 0:1], start=True, stop=True)
                last = pe.matmul(m.psum[:, 5, 0:3 * HEADS], t.ones[0:1, :], arow[:].rearrange("a b h -> a (b h)"),
                                 start=True, stop=True)
                last.then_inc(pe_done, 1)
                for k in range(3):
                    if k:
                        pe.wait_ge(dve_done, 12 + 6 * k)
                    for c in range(4):
                        o = m.psum[0:Q1, c, :]
                        w = t.wkq1[:, k * Q1:(k + 1) * Q1]
                        tok = slice(c * G, (c + 1) * G)
                        pe.matmul(o, w, t.x2t[:, 0, tok], start=True, stop=False)
                        last = pe.matmul(o, w, t.x2t[:, 1, tok], start=False, stop=True)
                    last.then_inc(pe_done, 1)
                pe.wait_ge(dve_done, 30)
                for b in range(2):
                    for k in range(8):
                        last = pe.transpose(m.psum[:, 6 + b, k * Q1:(k + 1) * Q1],
                                            qt[:, 2, (8 * b + k) * P:(8 * b + k + 1) * P], m.ident[0:Q1, 0:Q1])
                    last.then_inc(pe_done, 1)
                pe.wait_ge(dve_done, 34)
                pe.transpose(m.psum[0:Q1, 5, 0:D], wp[:], m.ident[:]).then_inc(pe_done, 1)
                with pe.Fori(0, HEADS) as h:
                    with pe.Fori(0, TILES) as i:
                        p0 = h * (TILES * PE1) + i * PE1 + PE0
                        d0 = h * (TILES * DVE1) + i * DVE1 + DVE0
                        pe.wait_ge(dve_done, d0 + 4)
                        for c in range(4):
                            last = pe.matmul(m.psum[:, c, :], qi[:], qt[:, 1, c * G:(c + 1) * G], start=True, stop=True)
                        last.then_inc(pe_done, 1)
                        pe.wait_ge(dve_done, d0 + 10)
                        for k in range(TILES):
                            last = pe.transpose(flat(4)[:, k * P:(k + 1) * P], e[:, k * P:(k + 1) * P], m.ident[:])
                        last.then_inc(pe_done, 1)
                        pe.wait_ge(dve_done, d0 + 11)
                        for k in range(TILES):
                            last = pe.matmul(m.psum[:, 0, 0:H1], at[:, k * P:(k + 1) * P],
                                             vn[:, k, bass.ds(h * H1, H1)], start=(k == 0), stop=(k == TILES - 1))
                        last.then_inc(pe_done, 1)
                with pe.Fori(0, TILES) as i:
                    d0 = HEADS * TILES * DVE1 + DVE0 + i * DVE2
                    pe.wait_ge(dve_done, d0 + 1)
                    pe.matmul(m.psum[0:Q1, 0, 0:P], oi[:], m.ident[:], start=True, stop=True).then_inc(pe_done, 1)
                    pe.wait_ge(dve_done, d0 + 2)
                    pe.matmul(m.psum[:, 1, 0:D], ot[:], wpt[:], start=True, stop=True).then_inc(pe_done, 1)

        @block.scalar
        def _(act):
            taken = act.value_load(t.bad[0:1, 0:1], min_val=0, max_val=1)
            with act.If(taken):
                with act.Fori(0, HEADS) as h:
                    with act.Fori(0, TILES) as i:
                        act.wait_ge(dve_done, h * (TILES * DVE1) + i * DVE1 + DVE0 + 5)
                        act.activation(e[:], flat(0), ACT.Exp, bias=nmax[:], accum_out=tot[:]).then_inc(act_done, 1)

        @block.vector
        def _(dve):
            taken = dve.value_load(t.bad[0:1, 0:1], min_val=0, max_val=1)
            with dve.If(taken):
                c = Chain(dve, dve_done)

                def spread(x):
                    return x.unsqueeze(3).broadcast_to([1, x.shape[1], HEADS, H1])

                def by_head(k, n):
                    return rows[:, k:k + n, :].rearrange("a b (h d) -> a b h d", d=H1)

                c.step(dve.tensor_copy(rows[:, 0:3, :], t.aw_row[:].rearrange("a (b n) -> a b n", b=3)))
                c.step(dve.memset(rows[:, 5, :], 0.0))
                c.step(dve.tensor_copy(by_head(3, 2), spread(t.row[:, BQ:BQ + 2, :])))
                c.step(dve.tensor_copy(by_head(6, 3), spread(t.row[:, QA:QA + 3, :])))
                c.step(dve.reciprocal(rows[:, 9:12, :], rows[:, 6:9, :]))
                c.step(dve.tensor_copy(by_head(12, 3), spread(t.row[:, QZ:QZ + 3, :])))
                c.step(dve.tensor_scalar(rows[:, 12:15, :], rows[:, 12:15, :], ROUND, -ROUND, ALU.add, ALU.add))
                c.step(dve.tensor_copy(arow[:, 0, :], t.row[:, AA, :]))
                c.step(dve.reciprocal(arow[:, 1, :], t.row[:, AA, :]))
                c.step(dve.tensor_scalar(arow[:, 2, :], t.row[:, AZ, :], ROUND, -ROUND, ALU.add, ALU.add))
                assert c.count == 10
                dve.wait_ge(pe_done, 1)
                c.step(dve.tensor_copy(cols[:], m.psum[0:Q1, 4, 0:30].rearrange("p (a b) -> p a b", b=2)[:, :, 0]))
                c.step(dve.tensor_copy(acols[:], m.psum[:, 5, 0:3 * HEADS].rearrange("p (a b) -> p a b", b=HEADS)))
                for k in range(3):
                    assert c.count == 12 + 6 * k
                    x = qt[:, k, :]
                    col = lambda n: cols[:, n + k:n + k + 1]
                    dve.wait_ge(pe_done, 2 + k)
                    c.step(dve.tensor_scalar(x, flat(0)[0:Q1, :], col(0), col(3), ALU.mult, ALU.add))
                    c.step(dve.tensor_scalar(x, x, col(9), col(12), ALU.mult, ALU.add))
                    c.step(dve.tensor_scalar(x, x, -8.0, 7.0, ALU.max, ALU.min))
                    c.step(dve.tensor_scalar(x, x, ROUND, -ROUND, ALU.add, ALU.add))
                    c.step(dve.tensor_scalar(x, x, col(12), col(6), ALU.subtract, ALU.mult))
                    c.step(dve.tensor_scalar(x, x, SCALE1 if k == 0 else 1.0, None, ALU.mult))
                assert c.count == 30
                dve.wait_ge(pe_done, 6)
                c.mark(dve.tensor_copy(vn[:], m.psum[:, 6:8, :].rearrange("p b (k n) -> p (b k) n", n=Q1)))
                c.step(dve.reciprocal(tot[:], t.pa[:]))
                c.step(dve.tensor_scalar(wp[:], t.pw[:], tot[:], -8.0, ALU.mult, ALU.max))
                dve.tensor_scalar(wp[:], wp[:], 7.0, ROUND, ALU.min, ALU.add).then_inc(wp_rounded, 1)
                dve.wait_ge(wp_rounded, 1)
                c.step(dve.tensor_scalar(wp[:], wp[:], -ROUND, t.pa[:], ALU.add, ALU.mult))
                assert c.count == 34
                dve.wait_ge(pe_done, 7)
                c.step(dve.tensor_copy(wpt[:], m.psum[0:Q1, 5, 0:D]))
                assert c.count == DVE0
                dve.wait_ge(pool_done, 3)
                with dve.Fori(0, HEADS) as h:
                    with dve.Fori(0, TILES) as i:
                        p0 = h * (TILES * PE1) + i * PE1 + PE0
                        c = Chain(dve, dve_done, h * (TILES * DVE1) + i * DVE1 + DVE0)
                        c.step(dve.tensor_copy(hp[:], acols[:, :, bass.ds(h, 1)].rearrange("p a b -> p (a b)")))
                        c.step(dve.tensor_copy(seln[:, 0:1], sel[:, bass.ds(h, 1)]))
                        c.step(dve.tensor_copy(qi[:], qt[:, 0, bass.ds(i * P, P)]))
                        c.step(dve.tensor_scalar(qi[:], qi[:], seln[:, 0:1], None, ALU.mult))
                        dve.wait_ge(pe_done, p0 + 1)
                        c.step(dve.tensor_reduce(nmax[:], flat(0), AX, ALU.max, negate=True))
                        dve.wait_ge(act_done, h * TILES + i + 1)
                        c.step(dve.reciprocal(inv[:], tot[:]))
                        c.step(dve.tensor_scalar(e[:], e[:], inv[:], hp[:, 1:2], ALU.mult, ALU.mult))
                        c.step(dve.tensor_scalar(e[:], e[:], hp[:, 2:3], -128.0, ALU.add, ALU.max))
                        c.step(dve.tensor_scalar(e[:], e[:], 127.0, ROUND, ALU.min, ALU.add))
                        c.step(dve.tensor_scalar(e[:], e[:], -ROUND, hp[:, 2:3], ALU.add, ALU.subtract))
                        dve.wait_ge(pe_done, p0 + 2)
                        c.step(dve.tensor_copy(at[:], flat(4)))
                        dve.wait_ge(pe_done, p0 + 3)
                        c.step(dve.tensor_scalar(oi[:, 0:H1], m.psum[:, 0, 0:H1], hp[:, 0:1], None, ALU.mult))
                        c.step(dve.tensor_copy(o1[:, bass.ds(i, 1), bass.ds(h * H1, H1)].rearrange("p a n -> p (a n)"), oi[:, 0:H1]))
                        assert c.count == DVE1
                with dve.Fori(0, TILES) as i:
                    p0 = HEADS * TILES * PE1 + PE0 + i * PE2
                    c = Chain(dve, dve_done, HEADS * TILES * DVE1 + DVE0 + i * DVE2)
                    c.step(dve.tensor_copy(oi[:], o1[:, bass.ds(i, 1), :].rearrange("p a n -> p (a n)")))
                    dve.wait_ge(pe_done, p0 + 1)
                    c.step(dve.tensor_copy(ot[:], m.psum[0:Q1, 0, 0:P]))
                    dve.wait_ge(pe_done, p0 + 2)
                    c.step(dve.tensor_copy(t.y1[:, bass.ds(i, 1), :].rearrange("p a n -> p (a n)"), m.psum[:, 1, 0:D]))
                    assert c.count == DVE2


def norm_all(dve, c, r, x, stats, mv, var, dev, asked, devd, nth):
    for k in range(TILES):
        c.mark(dve.bn_stats(stats[:, k, :], r[:, k, :]))
    c.wait()
    moments(dve, c, stats, mv)
    dve.tensor_scalar(var[:], mv[:, :, 1], EPS, None, ALU.add).then_inc(asked, 1)
    dve.wait_ge(devd, nth)
    c.step(dve.reciprocal(var[:], dev[:]))
    for k in range(TILES):
        c.mark(dve.tensor_scalar(x[:, k, :], r[:, k, :], mv[:, k, 0:1], var[:, k:k + 1], ALU.subtract, ALU.mult))
    c.wait()


def experts(nc, m, t, ins, out, sem):
    sb = t.sb
    r = sb("e_r", [P, TILES, D])
    x3 = sb("e_x3", [P, TILES, D])
    stats = sb("e_stats", [P, TILES, 6])
    mv = sb("e_mv", [P, TILES, 4])
    var = sb("e_var", [P, TILES])
    dev = sb("e_dev", [P, TILES])
    wg = sb("e_wg", [P, EXPERTS])
    x3t = t.free[:, 0:S]
    logit = sb("e_logit", [P, TILES, EXPERTS])
    lm = sb("e_lm", [P, TILES, EXPERTS])
    ex = sb("e_ex", [P, TILES, EXPERTS])
    top = sb("e_top", [P, TILES, 8])
    topi = sb("e_topi", [P, TILES, 8], U32)
    idx = sb("e_idx", [P, TILES])
    iota = sb("e_iota", [P, EXPERTS])
    hot = sb("e_hot", [P, TILES, EXPERTS], BF16)
    before = sb("e_before", [P, TILES, EXPERTS], BF16)
    tri = sb("e_tri", [P, P], BF16)
    onesb = sb("e_onesb", [P, P], BF16)
    cnt = sb("e_cnt", [P, TILES, EXPERTS])
    pos = sb("e_pos", [P, TILES])
    keep = sb("e_keep", [P, TILES])
    gate = sb("e_gate", [P, TILES])
    slot = sb("e_slot", [P, TILES])
    slotu = sb("e_slotu", [P, TILES], U32)
    xe = t.free[:, S:2 * S].rearrange("p (a n) -> p a n", n=D)
    xet = sb("e_xet", [P, EXPERTS * CAP])
    w1 = [t.ew1[:, i, :] for i in range(SLOTS)]
    w2 = [t.ew2[:, i, :, :] for i in range(SLOTS)]
    b1 = sb("e_b1", [P, EXPERTS, FT])
    b1r = sb("e_b1r", [EXPERTS, FF])
    h = [sb(f"e_h{i}", [P, FT, CAP]) for i in range(2)]
    ye = [sb(f"e_ye{i}", [P, D]) for i in range(2)]
    back = t.free[:, 2 * S:3 * S].rearrange("p (a n) -> p a n", n=D)
    rows_in = t.rows_in
    rows_out = nc.dram_tensor("expert_out", (S, D), F32, kind="Internal").ap()

    chain, asked, devd, pe_done, act_done = sem("e_chain"), sem("e_asked"), sem("e_devd"), sem("e_pe"), sem("e_act")
    loaded, consts, slots = sem("e_loaded"), sem("e_consts"), sem("e_slots")
    scattered, gathered, turned = sem("e_scattered"), sem("e_gathered"), sem("e_turned")
    xe_loaded = sem("e_xe")
    w_loaded = t.w_loaded
    up_full, up_done, down_full, down_done = sem("e_upf"), sem("e_upd"), sem("e_dnf"), sem("e_dnd")
    y_stored, back_zero, stored, copied = [sem("e_ys0"), sem("e_ys1")], sem("e_bz"), sem("e_stored"), sem("e_copied")

    x3_ready, hot_ready, stored_ready = sem("e_x3r"), sem("e_hotr"), sem("e_storer")

    def tile_rows(a):
        return a.rearrange("(e c) d -> c e d", c=P)

    with nc.Block() as block:

        @block.sync
        def _(sp):
            sp.dma_start(wg[:], ins["L1_ffn_Wg"]).then_inc(loaded, 16)
            sp.dma_start(b1r[:], ins["L1_ffn_b1"]).then_inc(loaded, 16)
            sp.wait_ge(scattered, 16 * TILES)
            sp.dma_start(xe[:], tile_rows(rows_in)).then_inc(xe_loaded, 16)
            for e in range(EXPERTS):
                sp.wait_ge(down_done, e + 1)
                sp.dma_start(rows_out[e * P:(e + 1) * P, :], ye[e % 2][:]).then_inc(y_stored[e % 2], 16)
                if e + SLOTS < EXPERTS:
                    load_expert(sp, t, ins, e + SLOTS)
            sp.wait_ge(stored_ready, 1)
            sp.dma_start(out.rearrange("a (t p) d -> p (a t) d", p=P), x3[:]).then_inc(stored, 16)
            sp.wait_ge(stored, 16)

        @block.gpsimd
        def _(pool):
            k = 0
            def step(i):
                nonlocal k
                i.then_inc(consts, 1)
                k += 1
                pool.wait_ge(consts, k)

            step(pool.iota(iota[:], [[1, EXPERTS]], base=0, channel_multiplier=0, allow_small_or_imprecise_dtypes=True))
            step(pool.memset(onesb[:], 1.0))
            step(pool.affine_select(out=tri[:], in_=onesb[:], compare_op=ALU.is_ge, fill=0.0, base=0,
                                    pattern=[[1, P]], channel_multiplier=-1))
            pool.memset(back[:], 0.0).then_inc(back_zero, 1)
            pool.wait_ge(slots, 1)
            for k2 in range(TILES):
                pool.indirect_dma_start(rows_in, bass.IndirectOffsetOnAxis(slotu[:, k2:k2 + 1], 0), x3[:, k2, :], None,
                                        bounds_check=S - 1, oob_is_err=False).then_inc(scattered, 16)
            for s in range(2):
                pool.wait_ge(y_stored[s], 16 * (EXPERTS // 2))
            pool.wait_ge(back_zero, 1)
            for k2 in range(TILES):
                pool.indirect_dma_start(back[:, k2, :], None, rows_out, bass.IndirectOffsetOnAxis(slotu[:, k2:k2 + 1], 0),
                                        bounds_check=S - 1, oob_is_err=False).then_inc(gathered, 16)

        @block.scalar
        def _(act):
            act.wait_ge(asked, 1)
            act.activation(dev[:], var[:], ACT.Sqrt).then_inc(devd, 1)
            for b in range(4):
                act.wait_ge(pe_done, b + 1)
                act.activation(x3t[:, b * G:(b + 1) * G], m.psum[:, b, :], ACT.Copy).then_inc(act_done, 1)
            act.wait_ge(asked, 2)
            act.activation(ex[:], lm[:], ACT.Exp).then_inc(devd, 1)
            for b in range(4):
                act.wait_ge(turned, b + 1)
                act.activation(xet[:, b * G:(b + 1) * G], m.psum[:, b, :], ACT.Copy).then_inc(copied, 1)
            act.wait_ge(turned, 5)
            act.activation(b1[:].rearrange("p e f -> p f e"), m.psum[:, 4, 0:FT * EXPERTS].rearrange("p (f e) -> p f e", e=EXPERTS),
                           ACT.Copy).then_inc(copied, 1)
            act.wait_ge(copied, 5)
            for e in range(EXPERTS):
                act.wait_ge(up_full, e + 1)
                if e > 1:
                    act.wait_ge(down_full, e - 1)
                for f in range(FT):
                    last = act.activation(h[e % 2][:, f, :], m.psum[:, 4 + e % 2, f * P:(f + 1) * P], ACT.Relu,
                                          bias=b1[:, e, f:f + 1])
                last.then_inc(up_done, 1)
            act.wait_ge(asked, 3)
            act.activation(dev[:], var[:], ACT.Sqrt).then_inc(devd, 1)

        @block.tensor
        def _(pe):
            pe.wait_ge(x3_ready, 1)
            for b in range(4):
                for k in range(4):
                    last = pe.transpose(m.psum[:, b, k * P:(k + 1) * P], x3[:, 4 * b + k, :], m.ident[:])
                last.then_inc(pe_done, 1)
            pe.wait_ge(loaded, 32)
            for k in range(TILES):
                pe.wait_ge(act_done, k // 4 + 1)
                last = pe.matmul(m.psum[:, 4, k * EXPERTS:(k + 1) * EXPERTS], x3t[:, k * P:(k + 1) * P], wg[:],
                                 start=True, stop=True)
            last.then_inc(pe_done, 1)
            pe.wait_ge(hot_ready, 1)
            pe.wait_ge(consts, 3)
            pe.matmul(m.psum[:, 5, 0:TILES * EXPERTS], tri[:], hot[:].rearrange("p a n -> p (a n)"), start=True, stop=False)
            pe.matmul(m.psum[:, 5, 0:TILES * EXPERTS], onesb[:], before[:].rearrange("p a n -> p (a n)"),
                      start=False, stop=True).then_inc(pe_done, 1)
            pe.wait_ge(xe_loaded, 16)
            for b in range(4):
                for k in range(4):
                    last = pe.transpose(m.psum[:, b, k * P:(k + 1) * P], xe[:, 4 * b + k, :], m.ident[:])
                last.then_inc(turned, 1)
            pe.wait_ge(slots, 1)
            for f in range(FT):
                last = pe.transpose(m.psum[:, 4, f * EXPERTS:(f + 1) * EXPERTS], b1r[:, f * P:(f + 1) * P],
                                    m.ident[0:EXPERTS, 0:EXPERTS])
            last.then_inc(turned, 1)
            pe.wait_ge(copied, 5)

            def up(e):
                if e > 1:
                    pe.wait_ge(up_done, e - 1)
                pe.wait_ge(w_loaded[e % SLOTS], 32 * (e // SLOTS + 1))
                for f in range(FT):
                    last = pe.matmul(m.psum[:, 4 + e % 2, f * P:(f + 1) * P], w1[e % SLOTS][:, f * P:(f + 1) * P],
                                     xet[:, e * P:(e + 1) * P], start=True, stop=True)
                last.then_inc(up_full, 1)

            def down(e):
                pe.wait_ge(up_done, e + 1)
                if e > 1:
                    pe.wait_ge(down_done, e - 1)
                for f in range(FT):
                    last = pe.matmul(m.psum[:, 6 + e % 2, 0:D], h[e % 2][:, f, :], w2[e % SLOTS][:, f, :],
                                     start=(f == 0), stop=(f == FT - 1))
                last.then_inc(down_full, 1)

            up(0)
            for e in range(1, EXPERTS):
                up(e)
                down(e - 1)
            down(EXPERTS - 1)

        @block.vector
        def _(dve):
            c = Chain(dve, chain)
            c.step(dve.tensor_tensor(r[:], t.x2[:], t.y1[:], ALU.add))
            c.step(dve.tensor_tensor(r[:], r[:], t.pb_b[:].unsqueeze(1).broadcast_to([P, TILES, D]), ALU.add))
            norm_all(dve, c, r, x3, stats, mv, var, dev, asked, devd, 1)
            dve.tensor_copy(pos[:], var[:]).then_inc(x3_ready, 1)
            dve.wait_ge(pe_done, 5)
            c.step(dve.tensor_tensor(logit[:], m.psum[:, 4, 0:TILES * EXPERTS].rearrange("p (a n) -> p a n", n=EXPERTS),
                                     t.bg_b[:].unsqueeze(1).broadcast_to([P, TILES, EXPERTS]), ALU.add))
            for k in range(TILES):
                c.mark(dve.max(top[:, k, :], logit[:, k, :]))
            c.wait()
            for k in range(TILES):
                c.mark(dve.max_index(topi[:, k, :], top[:, k, :], logit[:, k, :]))
            dve.tensor_tensor(lm[:], logit[:], top[:, :, 0:1].broadcast_to([P, TILES, EXPERTS]), ALU.subtract)\
                .then_inc(asked, 1)
            c.wait()
            c.step(dve.tensor_copy(idx[:], topi[:, :, 0]))
            dve.wait_ge(consts, 3)
            c.step(dve.tensor_tensor(hot[:], iota[:].unsqueeze(1).broadcast_to([P, TILES, EXPERTS]),
                                     idx[:].unsqueeze(2).broadcast_to([P, TILES, EXPERTS]), ALU.is_equal))
            c.step(dve.memset(before[:, 0, :], 0.0))
            for k in range(1, TILES):
                ins_ = dve.tensor_tensor(before[:, k, :], before[:, k - 1, :], hot[:, k - 1, :], ALU.add)
                if k < TILES - 1:
                    c.step(ins_)
            ins_.then_inc(hot_ready, 1)
            dve.wait_ge(devd, 2)
            c.step(dve.tensor_reduce(gate[:], ex[:], AX, ALU.add))
            c.step(dve.reciprocal(gate[:], gate[:]))
            dve.wait_ge(pe_done, 6)
            c.step(dve.tensor_tensor(cnt[:], m.psum[:, 5, 0:TILES * EXPERTS].rearrange("p (a n) -> p a n", n=EXPERTS),
                                     hot[:], ALU.mult))
            c.step(dve.tensor_reduce(pos[:], cnt[:], AX, ALU.add))
            c.step(dve.tensor_scalar(keep[:], pos[:], float(CAP), None, ALU.is_le))
            c.step(dve.tensor_tensor(gate[:], gate[:], keep[:], ALU.mult))
            c.step(dve.tensor_scalar(slot[:], idx[:], float(CAP), -1.0, ALU.mult, ALU.add))
            c.step(dve.tensor_tensor(slot[:], slot[:], pos[:], ALU.add))
            c.step(dve.tensor_scalar(keep[:], keep[:], -2.0 * S, 2.0 * S, ALU.mult, ALU.add))
            c.step(dve.tensor_tensor(slot[:], slot[:], keep[:], ALU.add))
            dve.tensor_copy(slotu[:], slot[:]).then_inc(slots, 1)
            for e in range(EXPERTS):
                dve.wait_ge(down_full, e + 1)
                if e > 1:
                    dve.wait_ge(y_stored[e % 2], 16 * (e // 2))
                dve.tensor_tensor(ye[e % 2][:], m.psum[:, 6 + e % 2, 0:D], t.eb2[:, e, :], ALU.add).then_inc(down_done, 1)
            dve.wait_ge(gathered, 16 * TILES)
            c.step(dve.tensor_tensor(back[:], back[:], gate[:].unsqueeze(2).broadcast_to([P, TILES, D]), ALU.mult))
            c.step(dve.tensor_tensor(r[:], x3[:], back[:], ALU.add))
            norm_all(dve, c, r, x3, stats, mv, var, dev, asked, devd, 3)
            dve.tensor_copy(pos[:], var[:]).then_inc(stored_ready, 1)


INPUTS = ["L0_attn_x", "L0_attn_Wq", "L0_attn_Wk", "L0_attn_Wv", "L0_attn_Wo", "L0_attn_bo",
          "L0_ffn_W1", "L0_ffn_b1", "L0_ffn_W2", "L0_ffn_b2",
          "L1_attn_qkv_w", "L1_attn_qkv_alpha", "L1_attn_bias_q", "L1_attn_bias_k", "L1_attn_q_alpha",
          "L1_attn_q_zp", "L1_attn_k_alpha", "L1_attn_k_zp", "L1_attn_v_alpha", "L1_attn_v_zp",
          "L1_attn_attn_alpha", "L1_attn_attn_zp", "L1_attn_proj_w", "L1_attn_proj_b", "L1_attn_proj_alpha",
          "L1_ffn_Wg", "L1_ffn_bg", "L1_ffn_W1", "L1_ffn_b1", "L1_ffn_W2", "L1_ffn_b2"]


def build(nc, ins, out):
    with ExitStack() as kept:
        def sem(name):
            return kept.enter_context(nc.semaphore(name))

        with ExitStack() as ctx:
            m = Memory(nc, kept, ctx)
            early = sem("early")
            setup(nc, m, ins, early, sem)
            attention(nc, m, sem)
        t = Tail(nc, m, kept)
        t.w_loaded = [sem(f"w_loaded{i}") for i in range(SLOTS)]
        for phase in (lambda c: layer0_rest(nc, m, t, ins, early, sem), lambda c: attention1_check(nc, m, t, sem),
                      lambda c: attention1_general(nc, m, t, sem), lambda c: experts(nc, m, t, ins, out, sem)):
            with ExitStack() as ctx:
                t.scope(ctx)
                phase(ctx)


def kernel(**inputs):
    import concourse.bacc as bacc
    from concourse.bass_utils import run_bass_kernel_spmd

    nc = bacc.Bacc("TRN2", target_bir_lowering=False, num_devices=1)
    arrays, ins = {}, {}
    for name in INPUTS:
        a = np.ascontiguousarray(inputs[name])
        arrays[f"in_{name}"] = a
        ins[name] = nc.dram_tensor(f"in_{name}", a.shape, mybir.dt.from_np(a.dtype), kind="ExternalInput").ap()
    out = nc.dram_tensor("out_x", (1, S, D), F32, kind="ExternalOutput").ap()
    build(nc, ins, out)
    r = run_bass_kernel_spmd(nc, [arrays], core_ids=[0])
    return r.results[0]["out_x"]
```

```python
from contextlib import ExitStack

import numpy as np
import concourse.bass as bass
from concourse import mybir

F32 = mybir.dt.float32
F16 = mybir.dt.float16
BF16 = mybir.dt.bfloat16
I32 = mybir.dt.int32
U32 = mybir.dt.uint32
ALU = mybir.AluOpType
ACT = mybir.ActivationFunctionType
AX = mybir.AxisListType.X

P = 128
S = 2048
D = 128
TILES = S // P
HEADS = 16
HD = 64
PAIRS = HEADS // 2
GROUPS = TILES // 4
RAW_MASK = -8e9
EXP_SCALE = 1.0 / 8.0
VW = 2 * HD + 1
VSTRIDE = VW + 1
ACC = 256
RING = 4
LEAD = 2


class Unit:

    def __init__(self, group, pair):
        self.group = group
        first = 2 * pair
        self.first = pair == 0
        self.last = pair == 2 * group + 1
        r = [max(0, j - 4 * group) for j in (first, first + 1)]
        second = 512 if r[0] == 0 else (4 - r[0]) * P
        self.keys = [(first, r[0], 0), (first + 1, r[1], second)]
        self.width = second + (4 - r[1]) * P


UNITS = [Unit(g, p) for g in range(GROUPS) for p in range(2 * g + 2)]
NU = len(UNITS)
BODY = 2 * NU


def max_jobs(group):
    return [("max", group, r, c) for c in range(group + 1) for r in range(4)]


def job_plan():
    plan = [[] for _ in range(NU)]

    def put(step, ahead, jobs):
        plan[step] += [(ahead, j) for j in jobs]

    m0, m1, m2, m3 = max_jobs(0), max_jobs(1), max_jobs(2), max_jobs(3)
    put(0, 1, [("kq", 0)])
    put(0, 0, m3[0:1])
    put(1, 0, m3[1:3] + [("shift", 2)])
    put(2, 1, [("kq", 1)])
    put(2, 0, m3[3:5])
    put(3, 0, m3[5:7])
    put(4, 1, [("kq", 2)])
    put(4, 0, m3[7:9])
    put(5, 0, m3[9:11])
    put(6, 1, [("kq", 3)])
    put(6, 0, m3[11:13])
    put(7, 0, m3[13:16])
    put(9, 0, [("shift", 3)])
    put(9, 1, [("v", 0)])
    put(10, 1, [("v", 1)] + m0[0:2])
    put(11, 1, m0[2:4] + m1[0:1])
    put(12, 1, m1[1:4])
    put(13, 1, [("shift", 0)] + m1[4:6])
    put(14, 1, m1[6:8] + m2[0:1])
    put(15, 1, m2[1:3])
    put(16, 1, [("shift", 1)] + m2[3:5])
    put(17, 1, m2[5:7])
    put(18, 1, m2[7:10])
    put(19, 1, m2[10:12])
    return plan


PLAN = job_plan()
LAST_KQ = [(1, ("kq", 3)) in step for step in PLAN].index(True)
FIRST_JOBS = [what for step in PLAN for ahead, what in step if ahead]
JOBS_PER_TRIP = 2 * sum(len(p) for p in PLAN)
assert JOBS_PER_TRIP % 2 == 0


class Job:

    def __init__(self, index, trip, head, what):
        self.bank = index % 2
        self.before = index // 2 + (0 if trip is None else trip * (JOBS_PER_TRIP // 2))
        self.head = head
        self.side = head % 2
        self.kind = what[0]
        self.what = what
        self.trip = trip

    def heads_done(self):
        return self.head if self.trip is None else self.trip * 2 + self.head

    def shifts_done(self, group):
        return self.heads_done() * GROUPS + group


def jobs_of(trip, step):
    if step is None:
        return [Job(i, None, 0, w) for i, w in enumerate(FIRST_JOBS)]
    at = len(FIRST_JOBS)
    for s in range(step):
        at += len(PLAN[s % NU])
    return [Job(at + i, trip, step // NU + ahead, w) for i, (ahead, w) in enumerate(PLAN[step % NU])]


def shift_job(trip, head, group):
    if trip is None:
        return [j for j in jobs_of(None, None) if j.what == ("shift", group)][0], 0
    if group < 2 and head == 0:
        steps, head, back = range(NU, BODY), 2, JOBS_PER_TRIP // 2
    else:
        steps, back = range(BODY), 0
    for s in steps:
        for j in jobs_of(trip, s):
            if j.what == ("shift", group) and j.head == head:
                return j, back


class Memory:

    def __init__(self, nc, kept, ctx):
        def keep(name, shape, dt=F32):
            return kept.enter_context(nc.sbuf_tensor(name, shape, dt))

        def sb(name, shape, dt=F32):
            return ctx.enter_context(nc.sbuf_tensor(name, shape, dt))

        self.psum = kept.enter_context(nc.psum_tensor("psum", [P, 8, 512], F32))
        self.x = keep("x", [P, TILES, D])
        self.heads_out = keep("heads_out", [P, TILES, HEADS * HD])
        self.ident = keep("ident", [P, P])
        self.ident16 = keep("ident16", [P, P], F16)
        self.wo = keep("wo", [P, PAIRS, D])
        self.ffn_w1 = keep("ffn_w1", [P, 4, D])
        self.ffn_w2 = keep("ffn_w2", [P, 4 * D])
        self.ffn_b1 = keep("ffn_b1", [P, 4])
        self.xt_hi = sb("xt_hi", [P, S], F16)
        self.xt_lo = sb("xt_lo", [P, S], F16)
        self.wkq_hi = sb("wkq_hi", [P, HEADS + 1, 2 * HD], F16)
        self.wkq_lo = sb("wkq_lo", [P, HEADS + 1, 2 * HD], F16)
        self.wv_hi = sb("wv_hi", [P, (HEADS + 1) * HD], F16)
        self.wv_lo = sb("wv_lo", [P, (HEADS + 1) * HD], F16)
        self.identb = sb("identb", [P, P], BF16)
        self.mask_ik = sb("mask_ik", [P, P], BF16)
        self.mask_ki = sb("mask_ki", [P, P], BF16)
        self.kq_hi = sb("kq_hi", [P, S], F16)
        self.kq_lo = sb("kq_lo", [P, S], F16)
        self.k_hh = [sb(f"k_hh{i}", [P, S], F16) for i in range(2)]
        self.q_hl = [sb(f"q_hl{i}", [P, S], F16) for i in range(2)]
        self.k_l1 = [sb(f"k_l1{i}", [HD + 1, S], F16) for i in range(2)]
        self.q_hm = [sb(f"q_hm{i}", [HD + 1, S], F16) for i in range(2)]
        self.v = [sb(f"v{i}", [P, TILES, VSTRIDE], F16) for i in range(2)]
        self.part_max = sb("part_max", [P, 2, 4, 4])
        self.neg_max = sb("neg_max", [P, 2, 4], F16)
        self.prob = [sb(f"prob{i}", [P, 1024]) for i in range(RING)]
        self.prob_hi = [sb(f"prob_hi{i}", [P, 1024], F16) for i in range(RING)]
        self.prob_lo = [sb(f"prob_lo{i}", [P, 1024], F16) for i in range(RING)]
        self.acc_copy = sb("acc_copy", [P, 2, 4, VW])
        self.acc_sum = sb("acc_sum", [P, 2, 4, HD])
        self.inv_sum = sb("inv_sum", [P, 2, 4, 1])
        self.scores = [self.psum[:, 2 * b:2 * b + 2, :].rearrange("p b n -> p (b n)") for b in range(2)]
        self.bank = [self.psum[:, 4 + b, :] for b in range(2)]
        self.acc = [self.psum[:, 6 + b, :] for b in range(2)]


def setup(nc, m, ins, early, sem):
    wraw = [m.heads_out[:, t, :] for t in range(3)]
    loaded, consts, turned, ready = sem("loaded"), sem("consts"), sem("turned"), sem("ready")
    x_loaded = sem("x_loaded")
    cast, moved = sem("cast"), sem("moved")
    with nc.Block() as block:

        @block.sync
        def _(sp):
            sp.dma_start(m.x[:], ins["L0_attn_x"].rearrange("a (t p) d -> p (a t) d", p=P)).then_inc(x_loaded, 16)
            for t, n in enumerate(("L0_attn_Wk", "L0_attn_Wq", "L0_attn_Wv")):
                sp.dma_start(wraw[t], ins[n]).then_inc(loaded, 16)
            sp.dma_start(m.wo[:], ins["L0_attn_Wo"].rearrange("(a p) n -> p a n", p=P)).then_inc(early, 16)
            sp.dma_start(m.ffn_w1[:], ins["L0_ffn_W1"].rearrange("(a p) n -> p a n", p=P)).then_inc(early, 16)
            sp.dma_start(m.ffn_w2[:], ins["L0_ffn_W2"]).then_inc(early, 16)
            with nc.allow_non_contiguous_dma("one small vector, once"):
                sp.dma_start(m.ffn_b1[:], ins["L0_ffn_b1"].rearrange("(a p) -> p a", p=P)).then_inc(early, 16)

        @block.gpsimd
        def _(pool):
            pool.memset(m.ident[:], 0.0).then_inc(consts, 1)
            pool.memset(m.mask_ik[:], 0.0).then_inc(consts, 1)
            pool.memset(m.mask_ki[:], 0.0).then_inc(consts, 1)
            pool.wait_ge(consts, 3)
            pool.affine_select(out=m.ident[:], in_=m.ident[:], compare_op=ALU.not_equal, fill=1.0,
                               base=0, pattern=[[-1, P]], channel_multiplier=1).then_inc(consts, 1)
            pool.affine_select(out=m.mask_ik[:], in_=m.mask_ik[:], compare_op=ALU.is_ge, fill=RAW_MASK,
                               base=0, pattern=[[-1, P]], channel_multiplier=1).then_inc(consts, 1)
            pool.affine_select(out=m.mask_ki[:], in_=m.mask_ki[:], compare_op=ALU.is_ge, fill=RAW_MASK,
                               base=0, pattern=[[1, P]], channel_multiplier=-1).then_inc(consts, 1)
            pool.wait_ge(consts, 4)
            pool.tensor_scalar(m.ident16[:], m.ident[:], 1.0, None, ALU.mult).then_inc(consts, 1)
            pool.tensor_scalar(m.identb[:], m.ident[:], 1.0, None, ALU.mult).then_inc(consts, 1)
            for side in range(2):
                pool.memset(m.v[side][:, :, 2 * HD:VW], 1.0).then_inc(consts, 1)
            for w in (m.wkq_hi[:, HEADS, :], m.wkq_lo[:, HEADS, :], m.wv_hi[:, HEADS * HD:], m.wv_lo[:, HEADS * HD:]):
                pool.memset(w, 0.0).then_inc(consts, 1)

        @block.tensor
        def _(pe):
            pe.wait_ge(consts, 4)
            pe.wait_ge(x_loaded, 16)
            for b in range(4):
                for t in range(4):
                    last = pe.transpose(m.psum[:, b, t * P:(t + 1) * P], m.x[:, 4 * b + t, :], m.ident[:])
                last.then_inc(turned, 1)

        def heads_of(w):
            return w.rearrange("p (h d) -> p h d", d=HD)

        @block.scalar
        def _(act):
            for b in range(4):
                act.wait_ge(turned, b + 1)
                act.activation(m.xt_hi[:, b * 512:(b + 1) * 512], m.psum[:, b, :], ACT.Copy).then_inc(cast, 1)
            act.wait_ge(loaded, 48)
            act.activation(m.wkq_hi[:, 0:HEADS, 0:HD], heads_of(wraw[0]), ACT.Copy).then_inc(cast, 1)
            act.activation(m.wkq_hi[:, 0:HEADS, HD:2 * HD], heads_of(wraw[1]), ACT.Copy).then_inc(cast, 1)
            act.activation(m.wv_hi[:, 0:HEADS * HD], wraw[2], ACT.Copy).then_inc(cast, 1)

        @block.vector
        def _(dve):
            for side in range(2):
                dve.memset(m.k_l1[side][HD:HD + 1, :], 1.0).then_inc(moved, 1)
            for b in range(4):
                dve.wait_ge(cast, b + 1)
                c = slice(b * 512, (b + 1) * 512)
                dve.tensor_tensor(m.xt_lo[:, c], m.psum[:, b, :], m.xt_hi[:, c], ALU.subtract).then_inc(ready, 1)
            dve.wait_ge(loaded, 48)
            for t in range(2):
                dve.wait_ge(cast, 5 + t)
                c = slice(t * HD, (t + 1) * HD)
                dve.tensor_tensor(m.wkq_lo[:, 0:HEADS, c], heads_of(wraw[t]), m.wkq_hi[:, 0:HEADS, c],
                                  ALU.subtract).then_inc(ready, 1)
            dve.wait_ge(cast, 7)
            dve.tensor_tensor(m.wv_lo[:, 0:HEADS * HD], wraw[2], m.wv_hi[:, 0:HEADS * HD],
                              ALU.subtract).then_inc(ready, 1)


def attention(nc, m, sem):
    bank_full = [sem("bank_full0"), sem("bank_full1")]
    bank_free = [sem("bank_free0"), sem("bank_free1")]
    high_done = sem("high_done")
    kq_spread = sem("kq_spread")
    neg_max_ready = sem("neg_max_ready")
    scores_full = sem("scores_full")
    exp_done = sem("exp_done")
    low_dve = sem("low_dve")
    low_pool = sem("low_pool")
    prob_free = sem("prob_free")
    acc_free = sem("acc_free")
    inv_ready = sem("inv_ready")
    sum_ready = sem("sum_ready")
    norm_done = sem("norm_done")

    def share(u):
        return u.width * 9 // 640 * 32

    def load_wait(engine, count):
        engine.wait_ge(kq_spread, 96 * count)

    with nc.Block() as block:

        @block.tensor
        def _(pe):
            def run(job):
                full, free = bank_full[job.bank], bank_free[job.bank]
                out = m.bank[job.bank]
                if job.trip is not None or job.before > 0:
                    pe.wait_ge(free, job.before)
                if job.kind == "kq":
                    c = slice(job.what[1] * 512, (job.what[1] + 1) * 512)
                    h = job.heads_done()
                    hi = m.wkq_hi[:, bass.ds(h, 1), :].rearrange("p a n -> p (a n)")
                    lo = m.wkq_lo[:, bass.ds(h, 1), :].rearrange("p a n -> p (a n)")
                    pe.matmul(out, hi, m.xt_hi[:, c], start=True, stop=False)
                    pe.matmul(out, hi, m.xt_lo[:, c], start=False, stop=False)
                    pe.matmul(out, lo, m.xt_hi[:, c], start=False, stop=True).then_inc(full, 1)
                elif job.kind == "v":
                    h = job.heads_done()
                    hi = m.wv_hi[:, bass.ds(h * HD, HD)]
                    lo = m.wv_lo[:, bass.ds(h * HD, HD)]
                    for t in range(8):
                        tok = slice((8 * job.what[1] + t) * P, (8 * job.what[1] + t + 1) * P)
                        o = out[:, t * HD:(t + 1) * HD]
                        pe.matmul(o, m.xt_hi[:, tok], hi, start=True, stop=False)
                        pe.matmul(o, m.xt_hi[:, tok], lo, start=False, stop=False)
                        last = pe.matmul(o, m.xt_lo[:, tok], hi, start=False, stop=True)
                    last.then_inc(full, 1)
                elif job.kind == "max":
                    _, g, r, c = job.what
                    if (g, r, c) == (0, 0, 0):
                        load_wait(pe, job.heads_done() + 1)
                    tile = 4 * g + r
                    q = m.q_hl[job.side][0:HD, tile * P:(tile + 1) * P]
                    width = 512 if c < g else (r + 1) * P
                    k = m.k_hh[job.side][0:HD, c * 512:c * 512 + width]
                    last = pe.matmul(out[:, 0:width], q, k, start=True, stop=(c < g))
                    if c == g:
                        last = pe.matmul(out[:, width - P:width], m.identb[:], m.mask_ik[:],
                                         start=False, stop=True)
                    last.then_inc(full, 1)
                else:
                    g = job.what[1]
                    pe.wait_ge(neg_max_ready, job.shifts_done(g) + 1)
                    for r in range(4):
                        last = pe.matmul(out[0:1, r * P:(r + 1) * P], m.neg_max[:, g % 2, r:r + 1],
                                         m.ident16[:], start=True, stop=True)
                    last.then_inc(full, 1)

            def scores(trip, s):
                u, head = UNITS[s % NU], s // NU
                out = m.scores[s % 2]
                units = s if trip is None else trip * BODY + s
                if trip is not None or s >= 2:
                    pe.wait_ge(exp_done, units - 1)
                if u.first:
                    job, back = shift_job(trip, head, u.group)
                    pe.wait_ge(bank_free[job.bank], job.before - back + 1)
                side = head % 2
                for j, r, col in u.keys:
                    n = (4 - r) * P
                    o = out[:, col:col + n]
                    keys = slice(j * P, (j + 1) * P)
                    queries = slice((4 * u.group + r) * P, (4 * u.group + 4) * P)
                    pe.matmul(o, m.k_hh[side][:, keys], m.q_hl[side][:, queries], start=True, stop=False)
                    if j >= 4 * u.group:
                        pe.matmul(o[:, 0:P], m.identb[:], m.mask_ki[:], start=False, stop=False)
                    last = pe.matmul(o, m.k_l1[side][:, keys], m.q_hm[side][:, queries], start=False, stop=True)
                last.then_inc(scores_full, 1)

            def weigh(trip, s):
                u, side = UNITS[s % NU], s // NU
                pe.wait_ge(low_dve, trip * BODY + s + 1)
                pe.wait_ge(low_pool, trip * BODY + s + 1)
                if u.first:
                    pe.wait_ge(acc_free, trip * 2 * GROUPS + side * GROUPS + u.group + 1)
                for j, first, col in u.keys:
                    for r in range(first, 4):
                        c = slice(col + (r - first) * P, col + (r - first + 1) * P)
                        a = (r % 2) * ACC
                        o = m.acc[r // 2][:, a:a + VW]
                        pe.matmul(o, m.prob_hi[s % RING][:, c], m.v[side][:, j, 0:VW],
                                  start=(j == 0 and r % 2 == 0), stop=False, skip_group_check=True)
                        last = pe.matmul(o[:, HD:VW], m.prob_lo[s % RING][:, c], m.v[side][:, j, HD:VW],
                                         start=False, stop=(j == 4 * u.group + r), skip_group_check=True)
                last.then_inc(prob_free, 1)

            for job in jobs_of(None, None):
                run(job)
            for s in range(LEAD):
                scores(None, s)
            with pe.Fori(0, PAIRS) as trip:
                for s in range(BODY):
                    jobs = jobs_of(trip, s)
                    half = (len(jobs) + 1) // 2
                    for job in jobs[:half]:
                        run(job)
                    scores(trip, s + LEAD)
                    for job in jobs[half:]:
                        run(job)
                    weigh(trip, s)

        @block.scalar
        def _(act):
            def run(job):
                full, free = bank_full[job.bank], bank_free[job.bank]
                src = m.bank[job.bank]
                if job.kind == "max":
                    return
                act.wait_ge(full, job.before + 1)
                if job.kind == "kq":
                    c = slice(job.what[1] * 512, (job.what[1] + 1) * 512)
                    if job.what[1] == 0 and not (job.trip is None):
                        load_wait(act, job.heads_done())
                    act.activation(m.kq_hi[:, c], src, ACT.Copy).then_inc(high_done, 1)
                elif job.kind == "v":
                    v = m.v[job.side][:, 8 * job.what[1]:8 * job.what[1] + 8, HD:2 * HD]
                    act.activation(v, src.rearrange("p (t d) -> p t d", d=HD), ACT.Copy).then_inc(high_done, 1)
                else:
                    g = job.what[1]
                    act.activation(m.q_hm[job.side][HD:HD + 1, g * 512:(g + 1) * 512], src[0:1, :],
                                   ACT.Copy).then_inc(free, 1)

            def exp_high(trip, s):
                u = UNITS[s % NU]
                n = s if trip is None else trip * BODY + s
                act.wait_ge(scores_full, n + 1)
                act.wait_ge(prob_free, n + 1)
                act.activation(m.prob_hi[s % RING][:, 0:u.width], m.scores[s % 2][:, 0:u.width], ACT.Exp,
                               scale=EXP_SCALE)

            def exp_full(s):
                u = UNITS[s % NU]
                act.activation(m.prob[s % RING][:, 0:u.width], m.scores[s % 2][:, 0:u.width], ACT.Exp,
                               scale=EXP_SCALE).then_inc(exp_done, 1)

            def copy_acc(trip, s):
                g = UNITS[s % NU].group
                n = trip * 2 * GROUPS + (s // NU) * GROUPS + g
                act.wait_ge(prob_free, trip * BODY + s + 1 + RING)
                act.wait_ge(norm_done, n + 1)
                for b in range(2):
                    src = m.acc[b].rearrange("p (t n) -> p t n", n=ACC)[:, :, 0:VW]
                    last = act.activation(m.acc_copy[:, g % 2, 2 * b:2 * b + 2, :], src, ACT.Copy)
                last.then_inc(acc_free, 1)

            for job in jobs_of(None, None):
                run(job)
            for s in range(LEAD - 1):
                exp_high(None, s)
                exp_full(s)
            with act.Fori(0, PAIRS) as trip:
                for s in range(BODY):
                    exp_high(trip, s + LEAD - 1)
                    if s > 0 and UNITS[(s - 1) % NU].last:
                        copy_acc(trip, s - 1)
                    for job in jobs_of(trip, s):
                        run(job)
                    exp_full(s + LEAD - 1)
                copy_acc(trip, BODY - 1)

        @block.vector
        def _(dve):
            def run(job):
                full, free = bank_full[job.bank], bank_free[job.bank]
                src = m.bank[job.bank]
                if job.kind == "shift":
                    return
                if job.kind == "max":
                    _, g, r, c = job.what
                    dve.wait_ge(full, job.before + 1)
                    width = 512 if c < g else (r + 1) * P
                    dve.tensor_reduce(m.part_max[:, g % 2, r, c:c + 1], src[:, 0:width], AX, ALU.max).then_inc(free, 1)
                    if (r, c) == (3, g):
                        dve.wait_ge(free, job.before + 1)
                        dve.wait_ge(bank_free[1 - job.bank], job.before + job.bank)
                        dve.tensor_reduce(m.neg_max[:, g % 2, :], m.part_max[:, g % 2, :, 0:g + 1], AX, ALU.max,
                                          negate=True).then_inc(neg_max_ready, 1)
                    return
                k = job.what[1] + (4 if job.kind == "v" else 0)
                dve.wait_ge(high_done, job.heads_done() * 6 + k + 1)
                if job.kind == "kq":
                    c = slice(job.what[1] * 512, (job.what[1] + 1) * 512)
                    dve.tensor_tensor(m.kq_lo[:, c], src, m.kq_hi[:, c], ALU.subtract).then_inc(free, 1)
                else:
                    t = slice(8 * job.what[1], 8 * job.what[1] + 8)
                    dve.tensor_tensor(m.v[job.side][:, t, 0:HD], src.rearrange("p (t d) -> p t d", d=HD),
                                      m.v[job.side][:, t, HD:2 * HD], ALU.subtract).then_inc(free, 1)

            def low(trip, s):
                u = UNITS[s % NU]
                dve.wait_ge(exp_done, trip * BODY + s + 1)
                c = slice(0, share(u))
                b = s % RING
                dve.tensor_tensor(m.prob_lo[b][:, c], m.prob[b][:, c], m.prob_hi[b][:, c],
                                  ALU.subtract).then_inc(low_dve, 1)

            def invert(trip, s):
                g = UNITS[s % NU].group
                n = trip * 2 * GROUPS + (s // NU) * GROUPS + g
                dve.wait_ge(acc_free, n + 2)
                dve.reciprocal(m.inv_sum[:, g % 2, :, :], m.acc_copy[:, g % 2, :, 2 * HD:VW]).then_inc(inv_ready, 1)

            for job in jobs_of(None, None):
                run(job)
            with dve.Fori(0, PAIRS) as trip:
                for s in range(BODY):
                    low(trip, s)
                    for job in jobs_of(trip, s):
                        run(job)
                    if s > 0 and UNITS[(s - 1) % NU].last:
                        invert(trip, s - 1)
                invert(trip, BODY - 1)

        @block.gpsimd
        def _(pool):
            def low(trip, s):
                u = UNITS[s % NU]
                pool.wait_ge(exp_done, trip * BODY + s + 1)
                c = slice(share(u), u.width)
                b = s % RING
                pool.tensor_tensor(m.prob_lo[b][:, c], m.prob[b][:, c], m.prob_hi[b][:, c],
                                   ALU.subtract).then_inc(low_pool, 1)

            def normalise(trip, s):
                u, side = UNITS[s % NU], s // NU
                g = u.group
                n = trip * 2 * GROUPS + side * GROUPS + g
                pool.wait_ge(inv_ready, n + 1)
                a = m.acc_copy[:, g % 2, :, :]
                pool.tensor_tensor(m.acc_sum[:, g % 2, :, :], a[:, :, 0:HD], a[:, :, HD:2 * HD],
                                   ALU.add).then_inc(sum_ready, 1)
                pool.wait_ge(sum_ready, n + 1)
                out = m.heads_out[:, 4 * g:4 * g + 4, bass.ds(trip * 2 * HD + side * HD, HD)]
                pool.tensor_tensor(out, m.acc_sum[:, g % 2, :, :],
                                   m.inv_sum[:, g % 2, :, :].broadcast_to([P, 4, HD]), ALU.mult).then_inc(norm_done, 1)

            pool.sem_inc(prob_free, RING)
            pool.sem_inc(acc_free, 1)
            pool.sem_inc(norm_done, 2)
            with pool.Fori(0, PAIRS) as trip:
                for s in range(BODY):
                    low(trip, s)
                    if s > 1 and UNITS[(s - 2) % NU].last:
                        normalise(trip, s - 2)
                normalise(trip, BODY - 1)

        @block.sync
        def _(sp):
            def spread(heads, side):
                hi, lo = m.kq_hi, m.kq_lo
                for dst, src in ((m.k_hh[side][0:HD, :], hi[0:HD, :]), (m.q_hl[side][0:HD, :], hi[HD:P, :]),
                                 (m.k_hh[side][HD:P, :], hi[0:HD, :]), (m.q_hl[side][HD:P, :], lo[HD:P, :]),
                                 (m.k_l1[side][0:HD, :], lo[0:HD, :]), (m.q_hm[side][0:HD, :], hi[HD:P, :])):
                    sp.dma_start(dst, src).then_inc(kq_spread, 16)

            last = [j for j in jobs_of(None, None) if j.kind == "kq"][-2:]
            for j in last:
                sp.wait_ge(bank_free[j.bank], j.before + 1)
            spread(0, 0)
            with sp.Fori(0, PAIRS) as trip:
                for head in range(2):
                    for j in [j for j in jobs_of(trip, head * NU + LAST_KQ) if j.kind == "kq"]:
                        sp.wait_ge(bank_free[j.bank], j.before + 1)
                    spread(None, (head + 1) % 2)


ROUND = 12582912.0
EPS = 1e-5
FF = 512
FT = FF // P
Q1 = 64
H1 = 4
SCALE1 = H1 ** -0.5
EXPERTS = 16
CAP = S // EXPERTS
ROW = D + 1
YE = 4
SLOTS = 8
G = 512
PARAMS = ["L1_attn_bias_q", "L1_attn_bias_k", "L1_attn_q_alpha", "L1_attn_k_alpha", "L1_attn_v_alpha",
          "L1_attn_q_zp", "L1_attn_k_zp", "L1_attn_v_zp", "L1_attn_attn_alpha", "L1_attn_attn_zp"]
BQ, BK, QA, KA, VA, QZ, KZ, VZ, AA, AZ = range(10)


class Chain:

    def __init__(self, engine, sem, base=0):
        self.engine, self.sem, self.base, self.count = engine, sem, base, 0

    def mark(self, instruction):
        instruction.then_inc(self.sem, 1)
        self.count += 1

    def wait(self):
        self.engine.wait_ge(self.sem, self.base + self.count)

    def step(self, instruction):
        self.mark(instruction)
        self.wait()


def moments(dve, c, stats, mv):
    c.mark(dve.tensor_tensor(mv[:, :, 0:2], stats[:, :, 1:3], stats[:, :, 4:6], ALU.add))
    c.step(dve.tensor_tensor(mv[:, :, 2:3], stats[:, :, 1:2], stats[:, :, 4:5], ALU.subtract))
    c.step(dve.scalar_tensor_tensor(mv[:, :, 3:4], mv[:, :, 2:3], 0.25, mv[:, :, 2:3], ALU.mult, ALU.mult))
    c.mark(dve.tensor_scalar(mv[:, :, 0:1], mv[:, :, 0:1], 0.5, None, ALU.mult))
    c.step(dve.scalar_tensor_tensor(mv[:, :, 1:2], mv[:, :, 1:2], 1.0 / D, mv[:, :, 3:4], ALU.mult, ALU.add))


class Tail:

    def __init__(self, nc, m, ctx):
        def sb(name, shape, dt=F32):
            return ctx.enter_context(nc.sbuf_tensor(name, shape, dt))

        self.nc = nc
        self.ew1 = sb("ew1", [P, SLOTS, FF])
        self.ew2 = sb("ew2", [P, SLOTS, FT, D])
        self.eb2 = sb("eb2", [P, EXPERTS, D])
        self.x2 = sb("x2", [P, TILES, D])
        self.stats = sb("e_stats", [P, TILES, 6])
        self.mv = sb("e_mv", [P, TILES, 4])
        self.var = sb("e_var", [P, TILES])
        self.dev = sb("e_dev", [P, TILES])
        self.rstd = sb("e_rstd", [P, TILES])
        self.shift = sb("e_shift", [P, TILES])
        self.wg = sb("e_wg", [P, EXPERTS])
        self.x2t = sb("x2t", [P, 2, S], F16)
        self.wkq1 = sb("wkq1", [P, 3 * Q1], F16)
        self.ext = sb("ext", [P, 2, GROUPS])
        self.ext1 = sb("ext1", [P, 2])
        self.row = sb("row", [1, 10, HEADS])
        self.aw_row = sb("aw_row", [1, 3 * Q1])
        self.bad = sb("bad", [1, 1], I32)
        self.y1 = m.x
        self.free = m.heads_out[:].rearrange("p t n -> p (t n)")
        self.x3t = self.free[:, 3 * S:4 * S]
        self.x3 = self.free[:, 5 * S:5 * S + TILES * ROW].rearrange("p (a n) -> p a n", n=ROW)
        self.ones = sb("ones", [P, P])
        self.bo_b = sb("bo_b", [P, D])
        self.b2_b = sb("b2_b", [P, D])
        self.pb_b = sb("pb_b", [P, D])
        self.bg_b = sb("bg_b", [P, EXPERTS])
        self.pw = sb("pw", [P, Q1])
        self.pa = sb("pa", [P, 1])

    def scope(self, ctx):
        self.sb = lambda name, shape, dt=F32: ctx.enter_context(self.nc.sbuf_tensor(name, shape, dt))


def load_expert(queue, t, ins, e):
    s = e % SLOTS
    queue.dma_start(t.ew1[:, s, :], ins["L1_ffn_W1"][e, :, :]).then_inc(t.w_loaded[s], 16)
    queue.dma_start(t.ew2[:, s, :, :], ins["L1_ffn_W2"][e, :, :].rearrange("(f p) n -> p f n", p=P))\
        .then_inc(t.w_loaded[s], 16)


def layer0_rest(nc, m, t, ins, early, sem):
    sb = t.sb
    wo_hi = sb("wo_hi", [P, PAIRS, D], F16)
    wo_lo = sb("wo_lo", [P, PAIRS, D], F16)
    w1q = sb("w1q", [P, FF], F16)
    w2q = sb("w2q", [P, FF], F16)
    w1t = sb("w1t", [P, FF], F16)
    w2t = sb("w2t", [P, FT, D], F16)
    qkv = sb("qkv", [Q1, 3, D])
    qkv_a = sb("qkv_a", [Q1, 3, 1])
    qkv_ia = sb("qkv_ia", [Q1, 3, 1])
    qkv_q = sb("qkv_q", [Q1, 3, D], F16)
    part = sb("part", [P, 2])
    gamma = sb("gamma", [P, 2])
    inv_gamma = sb("inv_gamma", [P, 2])
    rounded = sb("rounded", [P, FF])
    ot_hi = [sb(f"ot_hi{i}", [P, 4, P], F16) for i in range(3)]
    ot_lo = [sb(f"ot_lo{i}", [P, 4, P], F16) for i in range(3)]
    ot = [sb(f"ot{i}", [P, 4 * P]) for i in range(3)]
    r = [sb(f"r{i}", [P, 4, D]) for i in range(2)]
    stats = sb("stats", [P, 4, 6])
    mv = sb("mv", [P, 4, 4])
    rstd = sb("rstd", [P, 4])
    dev = sb("dev", [P, 4])
    x1 = sb("x1", [P, 4, D])
    x1b = [sb(f"x1b{i}", [P, 4, D]) for i in range(2)]
    x_hi = [sb(f"x_hi{i}", [P, 4, D], F16) for i in range(2)]
    x_lo = [sb(f"x_lo{i}", [P, 4, D], F16) for i in range(2)]
    x1t = [sb(f"x1t{i}", [P, 2, G], F16) for i in range(2)]
    up = sb("up", [P, FT, G])
    up_hi = sb("up_hi", [P, FT, G], F16)
    up_lo = sb("up_lo", [P, FT, G], F16)
    turned_o = [m.psum[:, b, :] for b in (0, 1, 7)]
    y_bank, down_bank = m.psum[:, 2, :], m.psum[:, 6, :]
    x_bank = m.psum[:, 3, :]
    range_bank = x_bank
    up_bank = [m.psum[:, 4 + b, :] for b in range(2)]
    halves = lambda bank: bank.bitcast(F16)

    loaded = sem("r_loaded")
    bo_loaded, b2_loaded, qkv_loaded = sem("bo_loaded"), sem("b2_loaded"), sem("qkv_loaded")
    xb_done = sem("xb_done")
    wo_hi_done, wo_lo_done = sem("wo_hi_done"), sem("wo_lo_done")
    sums_made, sums_added = sem("sums_made"), sem("sums_added")
    prep = sem("r_prep")
    scale_made = sem("scale_made")
    rounding = sem("rounding")
    quantised, qkv_quantised = sem("quantised"), sem("qkv_quantised")
    w_turned, w_placed = sem("w_turned"), sem("w_placed")
    o_turned = sem("o_turned")
    ot_hi_done = sem("ot_hi_done")
    ot_lo_first, ot_lo_done = sem("ot_lo_first"), sem("ot_lo_done")
    y_done, y_read = sem("y_done"), sem("y_read")
    def pair(name):
        return [sem(f"{name}0"), sem(f"{name}1")]

    dev_asked, dev_done = pair("dev_asked"), pair("dev_done")
    x_ready = pair("x_ready")
    x_hi_done, x_lo_done, x1b_done = pair("x_hi_done"), pair("x_lo_done"), sem("x1b_done")
    x_turned, xt_done = pair("x_turned"), pair("xt_done")
    range_full, range_read = sem("range_full"), sem("range_read")
    up_full, up_done = sem("up_full"), sem("up_done")
    up_lo_done, down_done = sem("up_lo_done"), sem("down_done")
    chain = sem("r_chain")
    LAST = GROUPS - 1

    def low_o(engine, g, j):
        n = g * 8 + j
        engine.wait_ge(ot_hi_done, n + 1)
        return engine.tensor_tensor(ot_lo[n % 3][:].rearrange("p a n -> p (a n)"), ot[n % 3][:],
                                    ot_hi[n % 3][:].rearrange("p a n -> p (a n)"), ALU.subtract)

    with nc.Block() as block:

        @block.sync
        def _(sp):
            with nc.allow_non_contiguous_dma("small parameters, once"):
                sp.dma_start(t.bo_b[:], ins["L0_attn_bo"].partition_broadcast(P)).then_inc(bo_loaded, 16)
                sp.dma_start(qkv[:], ins["L1_attn_qkv_w"].rearrange("(a p) n -> p a n", p=Q1)).then_inc(qkv_loaded, 16)
                sp.dma_start(qkv_a[:], ins["L1_attn_qkv_alpha"].rearrange("(a p) n -> p a n", p=Q1))\
                    .then_inc(qkv_loaded, 16)
                sp.dma_start(t.b2_b[:], ins["L0_ffn_b2"].partition_broadcast(P)).then_inc(b2_loaded, 16)
                sp.dma_start(t.pb_b[:], ins["L1_attn_proj_b"].partition_broadcast(P)).then_inc(b2_loaded, 16)
                loads = [(t.aw_row[:], ins["L1_attn_qkv_alpha"].rearrange("o a -> a o")),
                         (t.bg_b[:], ins["L1_ffn_bg"].partition_broadcast(P)),
                         (t.wg[:], ins["L1_ffn_Wg"]),
                         (t.pw[:], ins["L1_attn_proj_w"]),
                         (t.pa[:], ins["L1_attn_proj_alpha"])]
                loads += [(t.row[:, i, :], ins[n].rearrange("a h b c -> (a b c) h")) for i, n in enumerate(PARAMS)]
                loads += [(t.eb2[:], ins["L1_ffn_b2"].partition_broadcast(P))]
                for dst, src in loads:
                    sp.dma_start(dst, src).then_inc(loaded, 16)
            for e in range(SLOTS):
                load_expert(sp, t, ins, e)
            sp.wait_ge(loaded, 16 * len(loads))

        @block.tensor
        def _(pe):
            def turn_o(g, j):
                b = (g * 8 + j) % 3
                for a in range(4):
                    col = ((j % 2) * 4 + a) * P
                    o = m.heads_out[:, g * 4 + j // 2, col:col + P]
                    last = pe.transpose(turned_o[b][:, a * P:(a + 1) * P], o, m.ident[:])
                last.then_inc(o_turned, 1)

            def project(g, j):
                n = g * 8 + j + 1
                pe.wait_ge(ot_hi_done, n)
                if g == 0:
                    pe.wait_ge(ot_lo_first, n)
                else:
                    pe.wait_ge(ot_lo_done, n - 8)
                if j == 0:
                    pe.wait_ge(y_read, g + 1)
                out = y_bank[:, (j // 2) * P:(j // 2 + 1) * P]
                hi, lo = ot_hi[(n - 1) % 3], ot_lo[(n - 1) % 3]
                for a in range(4):
                    w = (j % 2) * 4 + a
                    pe.matmul(out, hi[:, a, :], wo_hi[:, w, :], start=(w == 0), stop=False)
                    pe.matmul(out, hi[:, a, :], wo_lo[:, w, :], start=False, stop=False)
                    last = pe.matmul(out, lo[:, a, :], wo_hi[:, w, :], start=False, stop=(w == PAIRS - 1))
                if j == 7:
                    last.then_inc(y_done, 1)

            def turn_x(g, n):
                pe.wait_ge(x_hi_done[n], g + 1)
                pe.wait_ge(x_lo_done[n], g + 1)
                if n == 0 and g > 1:
                    pe.wait_ge(xt_done[1], g - 1)
                if n == 1 and g > 0:
                    pe.wait_ge(range_read, g)
                elif n == 1:
                    pe.wait_ge(xt_done[0], 2)
                for a, x in enumerate((x_hi[n], x_lo[n])):
                    for k in range(4):
                        last = pe.transpose(halves(x_bank)[:, a * G + k * P:a * G + (k + 1) * P], x[:, k, :], m.ident16[:])
                last.then_inc(x_turned[n], 1)

            def range_product(g):
                pe.wait_ge(xt_done[1], g + 1)
                if g + 3 <= GROUPS:
                    pe.wait_ge(xt_done[0], g + 3)
                tok = slice(g * G, (g + 1) * G)
                pe.matmul(range_bank, t.wkq1[:, 0:P], t.x2t[:, 0, tok], start=True, stop=False)
                pe.matmul(range_bank, t.wkq1[:, 0:P], t.x2t[:, 1, tok], start=False, stop=True).then_inc(range_full, 1)

            def up_product(g, f):
                if f == 0:
                    pe.wait_ge(xt_done[0], g + 1)
                if f >= 2:
                    pe.wait_ge(up_done, g * FT + f - 1)
                w = w1t[:, f * P:(f + 1) * P]
                pe.matmul(up_bank[f % 2], w, x1t[g % 2][:, 0, :], start=True, stop=False)
                pe.matmul(up_bank[f % 2], w, x1t[g % 2][:, 1, :], start=False, stop=True).then_inc(up_full, 1)

            def down_product(g):
                pe.wait_ge(up_lo_done, (g + 1) * FT)
                for k in range(4):
                    out = down_bank[:, k * P:(k + 1) * P]
                    for f in range(FT):
                        pe.matmul(out, up_hi[:, f, k * P:(k + 1) * P], w2t[:, f, :], start=(f == 0), stop=False)
                        last = pe.matmul(out, up_lo[:, f, k * P:(k + 1) * P], w2t[:, f, :], start=False, stop=(f == FT - 1))
                last.then_inc(down_done, 1)

            pe.wait_ge(sums_made, 1)
            pe.matmul(down_bank[:, 0:2], t.ones[:], part[:], start=True, stop=True).then_inc(sums_added, 1)
            pe.wait_ge(wo_hi_done, 1)
            pe.wait_ge(wo_lo_done, 1)
            for j in range(10):
                if j < 8:
                    turn_o(0, j)
                if j > 1:
                    project(0, j - 2)
            pe.wait_ge(quantised, 1)
            for f in range(FT):
                pe.transpose(halves(up_bank[0])[:, f * P:(f + 1) * P], w1q[:, f * P:(f + 1) * P], m.ident16[:])
                last = pe.transpose(halves(up_bank[1])[:, f * P:(f + 1) * P], w2q[:, f * P:(f + 1) * P], m.ident16[:])
            last.then_inc(w_turned, 1)
            pe.wait_ge(w_placed, 1)

            def turn_qkv():
                pe.wait_ge(qkv_quantised, 1)
                for k in range(3):
                    last = pe.transpose(halves(down_bank)[:, k * Q1:(k + 1) * Q1], qkv_q[:, k, :], m.ident16[0:Q1, 0:Q1])
                last.then_inc(w_turned, 1)

            def step(g):
                ffn, norm, projection = g >= 0, g + 1 < GROUPS, g + 2 < GROUPS

                def half(j):
                    if projection:
                        if j < 8:
                            turn_o(g + 2, j)
                        if j > 1:
                            project(g + 2, j - 2)

                if ffn:
                    up_product(g, 0)
                    up_product(g, 1)
                half(0)
                if ffn:
                    up_product(g, 2)
                half(1)
                if ffn:
                    up_product(g, 3)
                half(2)
                half(3)
                if norm:
                    turn_x(g + 1, 0)
                half(4)
                if g > 0:
                    range_product(g - 1)
                if ffn:
                    if g == 0:
                        pe.wait_ge(w_placed, 2)
                    down_product(g)
                half(5)
                half(6)
                half(7)
                half(8)
                half(9)
                if ffn:
                    turn_x(g, 1)
                else:
                    turn_qkv()

            for g in range(-1, GROUPS):
                step(g)
            range_product(LAST)

        @block.scalar
        def _(act):
            act.wait_ge(early, 16 * 4)
            act.activation(wo_hi[:], m.wo[:], ACT.Copy).then_inc(wo_hi_done, 1)

            def high_o(g, j):
                act.wait_ge(o_turned, g * 8 + j + 1)
                b = (g * 8 + j) % 3
                act.activation(ot_hi[b][:].rearrange("p a n -> p (a n)"), turned_o[b], ACT.Copy)
                act.activation(ot[b][:], turned_o[b], ACT.Copy).then_inc(ot_hi_done, 1)

            def deviation(g, n):
                act.wait_ge(dev_asked[n], g + 1)
                act.activation(dev[:], rstd[:], ACT.Sqrt).then_inc(dev_done[n], 1)

            def high_x(g, n):
                act.wait_ge(x_ready[n], g + 1)
                x = x1[:] if n == 0 else t.x2[:, g * 4:g * 4 + 4, :]
                act.activation(x_hi[n][:], x, ACT.Copy).then_inc(x_hi_done[n], 1)

            def place_x(g, n):
                dst = x1t[g % 2][:] if n == 0 else t.x2t[:, :, g * G:(g + 1) * G]
                act.wait_ge(x_turned[n], g + 1)
                act.activation(dst, halves(x_bank).rearrange("p (a n) -> p a n", a=2), ACT.Copy).then_inc(xt_done[n], 1)

            def relu(g, f):
                act.wait_ge(up_full, g * FT + f + 1)
                act.activation(up_hi[:, f, :], up_bank[f % 2], ACT.Relu, bias=m.ffn_b1[:, f:f + 1])
                act.activation(up[:, f, :], up_bank[f % 2], ACT.Relu, bias=m.ffn_b1[:, f:f + 1]).then_inc(up_done, 1)

            for j in range(8):
                high_o(0, j)
            act.wait_ge(w_turned, 1)
            act.activation(w1t[:], halves(up_bank[0])[:, 0:FF], ACT.Copy)
            act.activation(w2t[:].rearrange("p a n -> p (a n)"), halves(up_bank[1])[:, 0:FF], ACT.Copy)\
                .then_inc(w_placed, 1)

            def step(g):
                ffn, norm, projection = g >= 0, g + 1 < GROUPS, g + 2 < GROUPS

                def half(j):
                    if projection:
                        high_o(g + 2, j)

                if ffn:
                    relu(g, 0)
                    relu(g, 1)
                half(0)
                if norm:
                    deviation(g + 1, 0)
                if ffn:
                    relu(g, 2)
                half(1)
                if ffn:
                    relu(g, 3)
                if norm:
                    high_x(g + 1, 0)
                half(2)
                half(3)
                if norm:
                    place_x(g + 1, 0)
                half(4)
                half(5)
                if ffn:
                    deviation(g, 1)
                half(6)
                half(7)
                if ffn:
                    high_x(g, 1)
                    place_x(g, 1)
                else:
                    act.wait_ge(w_turned, 2)
                    act.activation(t.wkq1[:], halves(down_bank)[:, 0:3 * Q1], ACT.Copy).then_inc(w_placed, 1)

            for g in range(-1, GROUPS):
                step(g)

        @block.vector
        def _(dve):
            c = Chain(dve, prep)
            c.step(dve.memset(t.ones[:], 1.0))
            dve.wait_ge(early, 16 * 4)
            dve.tensor_reduce(part[:, 0:1], m.ffn_w1[:].rearrange("p a n -> p (a n)"), AX, ALU.add,
                              apply_absolute_value=True)
            dve.tensor_reduce(part[:, 1:2], m.ffn_w2[:], AX, ALU.add, apply_absolute_value=True).then_inc(sums_made, 1)
            dve.wait_ge(wo_hi_done, 1)
            dve.tensor_tensor(wo_lo[:], m.wo[:], wo_hi[:], ALU.subtract).then_inc(wo_lo_done, 1)
            dve.wait_ge(sums_added, 1)
            c.step(dve.tensor_scalar(gamma[:], down_bank[:, 0:2], 1.0 / (FF * D), EPS, ALU.mult, ALU.add))
            dve.wait_ge(qkv_loaded, 32)
            dve.reciprocal(inv_gamma[:], gamma[:])
            dve.reciprocal(qkv_ia[:], qkv_a[:]).then_inc(scale_made, 1)

            dve.wait_ge(bo_loaded, 16)
            for j in range(8):
                low_o(dve, 0, j).then_inc(ot_lo_first, 1)
                if j % 2:
                    x = m.x[:, j // 2 * 4:j // 2 * 4 + 4, :]
                    dve.tensor_tensor(x, x, t.bo_b[:].unsqueeze(1).broadcast_to([P, 4, D]), ALU.add).then_inc(xb_done, 1)

            c = Chain(dve, chain)
            for k in range(3):
                c.mark(dve.tensor_scalar(qkv[:, k, :], qkv[:, k, :], qkv_ia[:, k, :], -8.0, ALU.mult, ALU.max))
            c.wait()
            c.step(dve.tensor_scalar(qkv[:], qkv[:], 7.0, ROUND, ALU.min, ALU.add))
            dve.tensor_scalar(qkv_q[:], qkv[:], -ROUND, None, ALU.add).then_inc(qkv_quantised, 1)

            def norm(g, n, x):
                for k in range(4):
                    c.mark(dve.bn_stats(stats[:, k, :], r[n][:, k, :]))
                c.wait()
                moments(dve, c, stats, mv)
                dve.tensor_scalar(rstd[:], mv[:, :, 1], EPS, None, ALU.add).then_inc(dev_asked[n], 1)
                dve.wait_ge(dev_done[n], g + 1)
                c.step(dve.reciprocal(rstd[:], dev[:]))
                for k in range(4):
                    last = dve.tensor_scalar(x[:, k, :], r[n][:, k, :], mv[:, k, 0:1], rstd[:, k:k + 1],
                                             ALU.subtract, ALU.mult)
                    if k < 3:
                        c.mark(last)
                last.then_inc(x_ready[n], 1)
                dve.wait_ge(x_hi_done[n], g + 1)
                dve.tensor_tensor(x_lo[n][:], x, x_hi[n][:], ALU.subtract).then_inc(x_lo_done[n], 1)

            def extremes(g):
                dve.wait_ge(range_full, g + 1)
                c.mark(dve.tensor_reduce(t.ext[:, 0, g:g + 1], range_bank, AX, ALU.max))
                dve.tensor_reduce(t.ext[:, 1, g:g + 1], range_bank, AX, ALU.min).then_inc(range_read, 1)

            def step(g):
                if g + 1 < GROUPS:
                    n = g + 1
                    dve.wait_ge(y_done, n + 1)
                    dve.tensor_tensor(r[0][:], y_bank.rearrange("p (a n) -> p a n", n=D), m.x[:, n * 4:n * 4 + 4, :],
                                      ALU.add).then_inc(y_read, 1)
                    dve.wait_ge(y_read, n + 2)
                    norm(n, 0, x1[:])
                    dve.tensor_tensor(x1b[n % 2][:], x1[:], t.b2_b[:].unsqueeze(1).broadcast_to([P, 4, D]), ALU.add)\
                        .then_inc(x1b_done, 1)
                if g > 0:
                    extremes(g - 1)
                if g >= 0:
                    dve.wait_ge(down_done, g + 1)
                    dve.wait_ge(x1b_done, g + 1)
                    c.step(dve.tensor_tensor(r[1][:], down_bank.rearrange("p (a n) -> p a n", n=D), x1b[g % 2][:], ALU.add))
                    x2 = t.x2[:, g * 4:g * 4 + 4, :]
                    norm(g, 1, x2)
                    dve.wait_ge(x_lo_done[1], g + 1)
                    c.step(dve.tensor_tensor(x2, x2, t.pb_b[:].unsqueeze(1).broadcast_to([P, 4, D]), ALU.add))
                    for k in range(4 * g, 4 * g + 4):
                        c.mark(dve.bn_stats(t.stats[:, k, :], t.x2[:, k, :]))

            dve.wait_ge(xb_done, GROUPS)
            dve.wait_ge(b2_loaded, 32)
            for g in range(-1, GROUPS):
                step(g)
            extremes(LAST)
            c.wait()
            dve.wait_ge(range_read, GROUPS)
            c.mark(dve.tensor_reduce(t.ext1[:, 0:1], t.ext[:, 0, :], AX, ALU.max))
            dve.tensor_reduce(t.ext1[:, 1:2], t.ext[:, 1, :], AX, ALU.min)

        @block.gpsimd
        def _(pool):
            pool.sem_inc(y_read, 1)
            pool.wait_ge(scale_made, 1)
            count = 0

            def step(i):
                nonlocal count
                i.then_inc(rounding, 1)
                count += 1
                pool.wait_ge(rounding, count)

            for k, (w, q) in enumerate(((m.ffn_w1[:].rearrange("p a n -> p (a n)"), w1q), (m.ffn_w2[:], w2q))):
                step(pool.tensor_scalar(rounded[:], w, inv_gamma[:, k:k + 1], ROUND, ALU.mult, ALU.add))
                step(pool.tensor_scalar(rounded[:], rounded[:], -ROUND, 1.0, ALU.add, ALU.min))
                last = pool.tensor_scalar(q[:], rounded[:], -1.0, None, ALU.max)
                if k == 0:
                    step(last)
            last.then_inc(quantised, 1)

            def low_up(g, f):
                pool.wait_ge(up_done, g * FT + f + 1)
                pool.tensor_tensor(up_lo[:, f, :], up[:, f, :], up_hi[:, f, :], ALU.subtract).then_inc(up_lo_done, 1)

            def step_of(g):
                ffn, projection = g >= 0, g + 2 < GROUPS

                def half(j):
                    if projection:
                        low_o(pool, g + 2, j).then_inc(ot_lo_done, 1)

                if ffn:
                    low_up(g, 0)
                    low_up(g, 1)
                half(0)
                if ffn:
                    low_up(g, 2)
                half(1)
                if ffn:
                    low_up(g, 3)
                for j in range(2, 8):
                    half(j)

            for g in range(-1, GROUPS):
                step_of(g)


def turn_rows(pe, out, cols, ident):
    return pe.matmul(out, cols, ident, start=True, stop=True)


class Front:

    def __init__(self, m, t, sem, name):
        self.m, self.t = m, t
        self.asked, self.dev_done = sem(f"{name}_asked"), sem(f"{name}_dev_done")
        self.scale_ready = sem(f"{name}_scale_ready")
        self.x3_ready = sem(f"{name}_x3_ready")
        self.x3_turned, self.x3_placed = sem(f"{name}_x3_turned"), sem(f"{name}_x3_placed")

    def variance(self, dve, c):
        t = self.t
        moments(dve, c, t.stats, t.mv)
        dve.tensor_scalar(t.var[:], t.mv[:, :, 1], EPS, None, ALU.add).then_inc(self.asked, 1)

    def scale(self, dve, c):
        t = self.t
        dve.wait_ge(self.dev_done, 1)
        c.step(dve.reciprocal(t.rstd[:], t.dev[:]))
        dve.scalar_tensor_tensor(t.shift[:], t.mv[:, :, 0], -1.0, t.rstd[:], ALU.mult, ALU.mult)\
            .then_inc(self.scale_ready, 1)

    def on_act(self, act):
        m, t = self.m, self.t
        act.wait_ge(self.asked, 1)
        act.activation(t.dev[:], t.var[:], ACT.Sqrt).then_inc(self.dev_done, 1)
        act.wait_ge(self.scale_ready, 1)
        for g in range(GROUPS + 1):
            if g < GROUPS:
                for k in range(4 * g, 4 * g + 4):
                    last = act.activation(t.x3[:, k, 0:D], t.x2[:, k, :], ACT.Identity, scale=t.rstd[:, k:k + 1],
                                          bias=t.shift[:, k:k + 1])
                last.then_inc(self.x3_ready, 1)
            if g:
                act.wait_ge(self.x3_turned, g)
                act.activation(t.x3t[:, (g - 1) * G:g * G], m.psum[:, g - 1, :], ACT.Copy).then_inc(self.x3_placed, 1)

    def on_pe(self, pe):
        m, t = self.m, self.t
        for g in range(GROUPS + 1):
            if g < GROUPS:
                pe.wait_ge(self.x3_ready, g + 1)
                for k in range(4):
                    last = pe.transpose(m.psum[:, g, k * P:(k + 1) * P], t.x3[:, 4 * g + k, 0:D], m.ident[:])
                last.then_inc(self.x3_turned, 1)
            if g:
                pe.wait_ge(self.x3_placed, g)
                for k in range(4 * g - 4, 4 * g):
                    pe.matmul(m.psum[:, 5, k * EXPERTS:(k + 1) * EXPERTS], t.x3t[:, k * P:(k + 1) * P], t.wg[:],
                              start=True, stop=True)


def attention1_check(nc, m, t, sem):
    front = Front(m, t, sem, "c_front")
    sb = t.sb
    v = sb("v_row", [1, 2, P])
    mag = sb("mag", [1, 3, P])
    small = sb("small", [1, 8, HEADS])
    prm = sb("prm", [1, 8, HEADS])
    empty = t.free[:, 0:TILES * ROW].rearrange("p (a n) -> p a n", n=ROW)
    zero_done, filled = sem("c_zero"), sem("c_filled")
    t.rows_in = nc.dram_tensor("expert_rows", (S, ROW), F32, kind="Internal").ap()
    t.rows_out = nc.dram_tensor("expert_out", (S, D), F32, kind="Internal").ap()
    full, chain, asked, expd = (sem("c_full"), sem("c_chain"), sem("c_asked"), sem("c_exp"))
    with nc.Block() as block:

        @block.tensor
        def _(pe):
            for k in range(2):
                last = turn_rows(pe, m.psum[0:1, 4, k * P:(k + 1) * P], t.ext1[:, k:k + 1], m.ident[:])
            last.then_inc(full, 1)
            front.on_pe(pe)

        @block.vector
        def _(dve):
            c = Chain(dve, chain)
            front.variance(dve, c)
            def both(x):
                return x.unsqueeze(3).broadcast_to([1, 2, HEADS, H1])

            c.mark(dve.reciprocal(prm[:, 0:2, :], t.row[:, QA:QA + 2, :]))
            c.step(dve.tensor_scalar(prm[:, 2:4, :], t.row[:, QZ:QZ + 2, :], ROUND, -ROUND, ALU.add, ALU.add))
            front.scale(dve, c)
            dve.wait_ge(full, 1)
            for k in range(2):
                w = v[:, k, :]
                q = w.rearrange("a (b h d) -> a b h d", b=2, d=H1)
                c.step(dve.tensor_tensor(w, m.psum[0:1, 4, k * P:(k + 1) * P], t.aw_row[:, 0:P], ALU.mult))
                c.step(dve.tensor_tensor(q, q, both(t.row[:, BQ:BQ + 2, :]), ALU.add))
                c.step(dve.tensor_tensor(q, q, both(prm[:, 0:2, :]), ALU.mult))
                c.step(dve.tensor_tensor(q, q, both(prm[:, 2:4, :]), ALU.add))
                c.step(dve.tensor_scalar(w, w, -8.0, 7.0, ALU.max, ALU.min))
                c.step(dve.tensor_scalar(w, w, ROUND, -ROUND, ALU.add, ALU.add))
                c.step(dve.tensor_tensor(q, q, both(prm[:, 2:4, :]), ALU.subtract))
                c.step(dve.tensor_tensor(q, q, both(t.row[:, QA:QA + 2, :]), ALU.mult))
            c.step(dve.scalar_tensor_tensor(mag[:, 0:2, :], v[:], -1.0, v[:], ALU.mult, ALU.max))
            c.step(dve.tensor_tensor(mag[:, 0, 0:Q1], mag[:, 0, 0:Q1], mag[:, 1, 0:Q1], ALU.max))
            c.step(dve.tensor_tensor(mag[:, 2, Q1:P], v[:, 0, Q1:P], v[:, 1, Q1:P], ALU.subtract))
            c.step(dve.scalar_tensor_tensor(mag[:, 2, Q1:P], mag[:, 2, Q1:P], -1.0, mag[:, 2, Q1:P], ALU.mult, ALU.max))
            c.step(dve.tensor_tensor(mag[:, 2, 0:Q1], mag[:, 0, 0:Q1], mag[:, 2, Q1:P], ALU.mult))
            c.step(dve.tensor_reduce(small[:, 0, :], mag[:, 2, 0:Q1].rearrange("a (h d) -> a h d", d=H1), AX, ALU.add))
            dve.tensor_scalar(small[:, 1, :], small[:, 0, :], -SCALE1, None, ALU.mult).then_inc(asked, 1)
            dve.wait_ge(expd, 1)
            c.step(dve.tensor_tensor(small[:, 3, :], small[:, 2, :], t.row[:, AA, :], ALU.mult))
            c.step(dve.tensor_scalar(small[:, 3, :], small[:, 3, :], 2.02 / S, None, ALU.is_gt))
            c.step(dve.tensor_scalar(small[:, 4, :], t.row[:, AZ, :], ROUND, -ROUND, ALU.add, ALU.add))
            c.mark(dve.tensor_scalar(small[:, 5, :], small[:, 4, :], -128.0, None, ALU.is_ge))
            c.mark(dve.tensor_scalar(small[:, 6, :], small[:, 4, :], 127.0, None, ALU.is_le))
            c.wait()
            c.step(dve.tensor_tensor(small[:, 3, :], small[:, 3, :], small[:, 5, :], ALU.mult))
            c.step(dve.tensor_tensor(small[:, 3, :], small[:, 3, :], small[:, 6, :], ALU.mult))
            c.step(dve.tensor_reduce(small[:, 7, 0:1], small[:, 3, :], AX, ALU.min))
            c.step(dve.tensor_scalar(t.bad[:], small[:, 7, 0:1], -1.0, 1.0, ALU.mult, ALU.add))

        @block.gpsimd
        def _(pool):
            pool.memset(empty[:, :, 0:D], 0.0).then_inc(zero_done, 1)
            pool.memset(empty[:, :, D:ROW].bitcast(I32), 2 * S).then_inc(zero_done, 1)
            pool.memset(t.y1[:], 0.0).then_inc(zero_done, 1)
            pool.iota(t.x3[:, :, D:ROW].bitcast(I32), [[P, TILES], [1, 1]], base=0, channel_multiplier=1)\
                .then_inc(zero_done, 1)

        @block.sync
        def _(sp):
            sp.wait_ge(zero_done, 2)
            sp.dma_start(t.rows_in.rearrange("(e c) d -> c e d", c=P), empty[:]).then_inc(filled, 16)
            sp.dma_start(t.rows_out.rearrange("(e c) d -> c e d", c=P), empty[:, :, 0:D]).then_inc(filled, 16)
            sp.wait_ge(filled, 32)

        @block.scalar
        def _(act):
            front.on_act(act)
            act.wait_ge(asked, 1)
            act.activation(small[:, 2, :], small[:, 1, :], ACT.Exp).then_inc(expd, 1)


def attention1_general(nc, m, t, sem):
    sb = t.sb
    qt = t.free[0:Q1, 0:3 * S].rearrange("p (a n) -> p a n", n=S)
    vn = sb("g_vn", [P, TILES, Q1])
    rows = sb("g_rows", [1, 15, Q1])
    cols = sb("g_cols", [Q1, 15])
    arow = sb("g_arow", [1, 3, HEADS])
    acols = sb("g_acols", [P, 3, HEADS])
    sel = sb("g_sel", [Q1, HEADS])
    seln = sb("g_seln", [Q1, HEADS])
    qi = sb("g_qi", [Q1, P])
    hp = sb("g_hp", [P, 3])
    nmax = sb("g_nmax", [P, 1])
    tot = sb("g_tot", [P, 1])
    inv = sb("g_inv", [P, 1])
    e = t.free[:, 3 * S:4 * S]
    at = t.free[:, 4 * S:5 * S]
    o1 = sb("g_o1", [P, TILES, Q1])
    ot = sb("g_ot", [Q1, P])
    wp = sb("g_wp", [P, Q1])
    wpt = sb("g_wpt", [Q1, D])
    oi = sb("g_oi", [P, Q1])
    front = Front(m, t, sem, "g_front")
    pe_done, dve_done, act_done, pool_done = sem("g_pe"), sem("g_dve"), sem("g_act"), sem("g_pool")
    wp_rounded = sem("g_wp")
    flat = lambda a: m.psum[:, a:a + 4, :].rearrange("p b n -> p (b n)")
    PE0, DVE0 = 7, 35
    PE1, DVE1 = 3, 13
    PE2, DVE2 = 2, 3

    with nc.Block() as block:

        @block.gpsimd
        def _(pool):
            taken = pool.value_load(t.bad[0:1, 0:1], min_val=0, max_val=1)
            with pool.If(taken):
                pool.memset(seln[:], 1.0).then_inc(pool_done, 1)
                pool.wait_ge(pool_done, 1)
                pool.affine_select(out=sel[:], in_=seln[:], compare_op=ALU.is_ge, fill=0.0, base=0,
                                   pattern=[[-H1, HEADS]], channel_multiplier=1).then_inc(pool_done, 1)
                pool.wait_ge(pool_done, 2)
                pool.affine_select(out=sel[:], in_=sel[:], compare_op=ALU.is_ge, fill=0.0, base=H1 - 1,
                                   pattern=[[H1, HEADS]], channel_multiplier=-1).then_inc(pool_done, 1)

        @block.tensor
        def _(pe):
            taken = pe.value_load(t.bad[0:1, 0:1], min_val=0, max_val=1)
            with pe.If(taken):
                pe.wait_ge(dve_done, 10)
                for k in range(15):
                    pe.matmul(m.psum[0:Q1, 4, 2 * k:2 * k + 1], rows[:, k, :], t.ones[0:1, 0:1], start=True, stop=True)
                last = pe.matmul(m.psum[:, 5, 0:3 * HEADS], t.ones[0:1, :], arow[:].rearrange("a b h -> a (b h)"),
                                 start=True, stop=True)
                last.then_inc(pe_done, 1)
                for k in range(3):
                    if k:
                        pe.wait_ge(dve_done, 12 + 6 * k)
                    for c in range(4):
                        o = m.psum[0:Q1, c, :]
                        w = t.wkq1[:, k * Q1:(k + 1) * Q1]
                        tok = slice(c * G, (c + 1) * G)
                        pe.matmul(o, w, t.x2t[:, 0, tok], start=True, stop=False)
                        last = pe.matmul(o, w, t.x2t[:, 1, tok], start=False, stop=True)
                    last.then_inc(pe_done, 1)
                pe.wait_ge(dve_done, 30)
                for b in range(2):
                    for k in range(8):
                        last = pe.transpose(m.psum[:, 6 + b, k * Q1:(k + 1) * Q1],
                                            qt[:, 2, (8 * b + k) * P:(8 * b + k + 1) * P], m.ident[0:Q1, 0:Q1])
                    last.then_inc(pe_done, 1)
                pe.wait_ge(dve_done, 34)
                pe.transpose(m.psum[0:Q1, 5, 0:D], wp[:], m.ident[:]).then_inc(pe_done, 1)
                with pe.Fori(0, HEADS) as h:
                    with pe.Fori(0, TILES) as i:
                        p0 = h * (TILES * PE1) + i * PE1 + PE0
                        d0 = h * (TILES * DVE1) + i * DVE1 + DVE0
                        pe.wait_ge(dve_done, d0 + 4)
                        for c in range(4):
                            last = pe.matmul(m.psum[:, c, :], qi[:], qt[:, 1, c * G:(c + 1) * G], start=True, stop=True)
                        last.then_inc(pe_done, 1)
                        pe.wait_ge(dve_done, d0 + 10)
                        for k in range(TILES):
                            last = pe.transpose(flat(4)[:, k * P:(k + 1) * P], e[:, k * P:(k + 1) * P], m.ident[:])
                        last.then_inc(pe_done, 1)
                        pe.wait_ge(dve_done, d0 + 11)
                        for k in range(TILES):
                            last = pe.matmul(m.psum[:, 0, 0:H1], at[:, k * P:(k + 1) * P],
                                             vn[:, k, bass.ds(h * H1, H1)], start=(k == 0), stop=(k == TILES - 1))
                        last.then_inc(pe_done, 1)
                with pe.Fori(0, TILES) as i:
                    d0 = HEADS * TILES * DVE1 + DVE0 + i * DVE2
                    pe.wait_ge(dve_done, d0 + 1)
                    pe.matmul(m.psum[0:Q1, 0, 0:P], oi[:], m.ident[:], start=True, stop=True).then_inc(pe_done, 1)
                    pe.wait_ge(dve_done, d0 + 2)
                    pe.matmul(m.psum[:, 1, 0:D], ot[:], wpt[:], start=True, stop=True).then_inc(pe_done, 1)
                front.on_pe(pe)

        @block.scalar
        def _(act):
            taken = act.value_load(t.bad[0:1, 0:1], min_val=0, max_val=1)
            with act.If(taken):
                with act.Fori(0, HEADS) as h:
                    with act.Fori(0, TILES) as i:
                        act.wait_ge(dve_done, h * (TILES * DVE1) + i * DVE1 + DVE0 + 5)
                        act.activation(e[:], flat(0), ACT.Exp, bias=nmax[:], accum_out=tot[:]).then_inc(act_done, 1)
                front.on_act(act)

        @block.vector
        def _(dve):
            taken = dve.value_load(t.bad[0:1, 0:1], min_val=0, max_val=1)
            with dve.If(taken):
                c = Chain(dve, dve_done)

                def spread(x):
                    return x.unsqueeze(3).broadcast_to([1, x.shape[1], HEADS, H1])

                def by_head(k, n):
                    return rows[:, k:k + n, :].rearrange("a b (h d) -> a b h d", d=H1)

                c.step(dve.tensor_copy(rows[:, 0:3, :], t.aw_row[:].rearrange("a (b n) -> a b n", b=3)))
                c.step(dve.memset(rows[:, 5, :], 0.0))
                c.step(dve.tensor_copy(by_head(3, 2), spread(t.row[:, BQ:BQ + 2, :])))
                c.step(dve.tensor_copy(by_head(6, 3), spread(t.row[:, QA:QA + 3, :])))
                c.step(dve.reciprocal(rows[:, 9:12, :], rows[:, 6:9, :]))
                c.step(dve.tensor_copy(by_head(12, 3), spread(t.row[:, QZ:QZ + 3, :])))
                c.step(dve.tensor_scalar(rows[:, 12:15, :], rows[:, 12:15, :], ROUND, -ROUND, ALU.add, ALU.add))
                c.step(dve.tensor_copy(arow[:, 0, :], t.row[:, AA, :]))
                c.step(dve.reciprocal(arow[:, 1, :], t.row[:, AA, :]))
                c.step(dve.tensor_scalar(arow[:, 2, :], t.row[:, AZ, :], ROUND, -ROUND, ALU.add, ALU.add))
                assert c.count == 10
                dve.wait_ge(pe_done, 1)
                c.step(dve.tensor_copy(cols[:], m.psum[0:Q1, 4, 0:30].rearrange("p (a b) -> p a b", b=2)[:, :, 0]))
                c.step(dve.tensor_copy(acols[:], m.psum[:, 5, 0:3 * HEADS].rearrange("p (a b) -> p a b", b=HEADS)))
                for k in range(3):
                    assert c.count == 12 + 6 * k
                    x = qt[:, k, :]
                    col = lambda n: cols[:, n + k:n + k + 1]
                    dve.wait_ge(pe_done, 2 + k)
                    c.step(dve.tensor_scalar(x, flat(0)[0:Q1, :], col(0), col(3), ALU.mult, ALU.add))
                    c.step(dve.tensor_scalar(x, x, col(9), col(12), ALU.mult, ALU.add))
                    c.step(dve.tensor_scalar(x, x, -8.0, 7.0, ALU.max, ALU.min))
                    c.step(dve.tensor_scalar(x, x, ROUND, -ROUND, ALU.add, ALU.add))
                    c.step(dve.tensor_scalar(x, x, col(12), col(6), ALU.subtract, ALU.mult))
                    c.step(dve.tensor_scalar(x, x, SCALE1 if k == 0 else 1.0, None, ALU.mult))
                assert c.count == 30
                dve.wait_ge(pe_done, 6)
                c.mark(dve.tensor_copy(vn[:], m.psum[:, 6:8, :].rearrange("p b (k n) -> p (b k) n", n=Q1)))
                c.step(dve.reciprocal(tot[:], t.pa[:]))
                c.step(dve.tensor_scalar(wp[:], t.pw[:], tot[:], -8.0, ALU.mult, ALU.max))
                dve.tensor_scalar(wp[:], wp[:], 7.0, ROUND, ALU.min, ALU.add).then_inc(wp_rounded, 1)
                dve.wait_ge(wp_rounded, 1)
                c.step(dve.tensor_scalar(wp[:], wp[:], -ROUND, t.pa[:], ALU.add, ALU.mult))
                assert c.count == 34
                dve.wait_ge(pe_done, 7)
                c.step(dve.tensor_copy(wpt[:], m.psum[0:Q1, 5, 0:D]))
                assert c.count == DVE0
                dve.wait_ge(pool_done, 3)
                with dve.Fori(0, HEADS) as h:
                    with dve.Fori(0, TILES) as i:
                        p0 = h * (TILES * PE1) + i * PE1 + PE0
                        c = Chain(dve, dve_done, h * (TILES * DVE1) + i * DVE1 + DVE0)
                        c.step(dve.tensor_copy(hp[:], acols[:, :, bass.ds(h, 1)].rearrange("p a b -> p (a b)")))
                        c.step(dve.tensor_copy(seln[:, 0:1], sel[:, bass.ds(h, 1)]))
                        c.step(dve.tensor_copy(qi[:], qt[:, 0, bass.ds(i * P, P)]))
                        c.step(dve.tensor_scalar(qi[:], qi[:], seln[:, 0:1], None, ALU.mult))
                        dve.wait_ge(pe_done, p0 + 1)
                        c.step(dve.tensor_reduce(nmax[:], flat(0), AX, ALU.max, negate=True))
                        dve.wait_ge(act_done, h * TILES + i + 1)
                        c.step(dve.reciprocal(inv[:], tot[:]))
                        c.step(dve.tensor_scalar(e[:], e[:], inv[:], hp[:, 1:2], ALU.mult, ALU.mult))
                        c.step(dve.tensor_scalar(e[:], e[:], hp[:, 2:3], -128.0, ALU.add, ALU.max))
                        c.step(dve.tensor_scalar(e[:], e[:], 127.0, ROUND, ALU.min, ALU.add))
                        c.step(dve.tensor_scalar(e[:], e[:], -ROUND, hp[:, 2:3], ALU.add, ALU.subtract))
                        dve.wait_ge(pe_done, p0 + 2)
                        c.step(dve.tensor_copy(at[:], flat(4)))
                        dve.wait_ge(pe_done, p0 + 3)
                        c.step(dve.tensor_scalar(oi[:, 0:H1], m.psum[:, 0, 0:H1], hp[:, 0:1], None, ALU.mult))
                        c.step(dve.tensor_copy(o1[:, bass.ds(i, 1), bass.ds(h * H1, H1)].rearrange("p a n -> p (a n)"), oi[:, 0:H1]))
                        assert c.count == DVE1
                with dve.Fori(0, TILES) as i:
                    p0 = HEADS * TILES * PE1 + PE0 + i * PE2
                    c = Chain(dve, dve_done, HEADS * TILES * DVE1 + DVE0 + i * DVE2)
                    c.step(dve.tensor_copy(oi[:], o1[:, bass.ds(i, 1), :].rearrange("p a n -> p (a n)")))
                    dve.wait_ge(pe_done, p0 + 1)
                    c.step(dve.tensor_copy(ot[:], m.psum[0:Q1, 0, 0:P]))
                    dve.wait_ge(pe_done, p0 + 2)
                    c.step(dve.tensor_copy(t.y1[:, bass.ds(i, 1), :].rearrange("p a n -> p (a n)"), m.psum[:, 1, 0:D]))
                    assert c.count == DVE2
                c = Chain(dve, dve_done, HEADS * TILES * DVE1 + DVE0 + TILES * DVE2)
                c.step(dve.tensor_tensor(t.x2[:], t.x2[:], t.y1[:], ALU.add))
                for k in range(TILES):
                    c.mark(dve.bn_stats(t.stats[:, k, :], t.x2[:, k, :]))
                c.wait()
                front.variance(dve, c)
                front.scale(dve, c)


def experts(nc, m, t, ins, out, sem):
    sb = t.sb
    r = sb("e_r", [P, TILES, D])
    x3, stats, mv, var, dev, rstd, shift = t.x3, t.stats, t.mv, t.var, t.dev, t.rstd, t.shift
    logit = sb("e_logit", [P, TILES, EXPERTS])
    lm = sb("e_lm", [P, TILES, EXPERTS])
    ex = sb("e_ex", [P, TILES, EXPERTS])
    top = sb("e_top", [P, TILES, 8])
    topi = sb("e_topi", [P, TILES, 8], U32)
    idx = sb("e_idx", [P, TILES])
    iota = sb("e_iota", [P, EXPERTS])
    hot = sb("e_hot", [P, TILES, EXPERTS], BF16)
    tri = sb("e_tri", [P, P], BF16)
    onesb = sb("e_onesb", [P, P], BF16)
    cnt = sb("e_cnt", [P, TILES, EXPERTS])
    pos = sb("e_pos", [P, TILES])
    keep = sb("e_keep", [P, TILES])
    gate = sb("e_gate", [P, TILES])
    slot = sb("e_slot", [P, TILES])
    slotu = sb("e_slotu", [P, TILES], U32)
    xe = sb("e_xe", [P, EXPERTS, ROW])
    xet = sb("e_xet", [P, EXPERTS * CAP])
    b1 = sb("e_b1", [P, EXPERTS, FT])
    b1r = sb("e_b1r", [EXPERTS, FF])
    h = [sb(f"e_h{i}", [P, FT, CAP]) for i in range(2)]
    ye = [sb(f"e_ye{i}", [P, D]) for i in range(YE)]
    back = t.free[:, S:2 * S].rearrange("p (a n) -> p a n", n=D)
    rows_in, rows_out = t.rows_in, t.rows_out
    w1 = [t.ew1[:, i, :] for i in range(SLOTS)]
    w2 = [t.ew2[:, i, :, :] for i in range(SLOTS)]
    w_loaded = t.w_loaded

    loaded = sem("e_loaded")
    consts = sem("e_consts")
    chain = sem("e_chain")
    last_scale = sem("e_last_scale")
    lm_ready, exp_done = sem("e_lm_ready"), sem("e_exp_done")
    hot_ready, counted = sem("e_hot_ready"), sem("e_counted")
    slots_ready, scattered = sem("e_slots_ready"), sem("e_scattered")
    b1_turned, b1_placed = sem("e_b1_turned"), sem("e_b1_placed")
    xe_loaded = [sem(f"e_xe_loaded{b}") for b in range(4)]
    xe_turned, xe_placed = sem("e_xe_turned"), sem("e_xe_placed")
    up_full, up_done, down_full, down_done = sem("e_upf"), sem("e_upd"), sem("e_dnf"), sem("e_dnd")
    y_sent = [sem(f"e_y_sent{i}") for i in range(YE)]
    back_loaded = [sem(f"e_back_loaded{g}") for g in range(GROUPS)]
    last_asked, last_dev = sem("e_last_asked"), sem("e_last_dev")
    out_ready, stored = sem("e_out_ready"), sem("e_stored")

    count_bank = [m.psum[:, b, 0:4 * EXPERTS] for b in (4, 6)]

    def tiles(g):
        return slice(4 * g, 4 * g + 4)

    with nc.Block() as block:

        @block.sync
        def _(sp):
            sp.dma_start(b1r[:], ins["L1_ffn_b1"]).then_inc(loaded, 16)
            sp.wait_ge(scattered, 16 * TILES)
            for b in range(4):
                src = rows_in[4 * b * P:(4 * b + 4) * P, :].rearrange("(e c) d -> c e d", c=P)
                sp.dma_start(xe[:, tiles(b), :], src).then_inc(xe_loaded[b], 16)
            for e in range(EXPERTS - SLOTS):
                sp.wait_ge(down_done, e + 1)
                load_expert(sp, t, ins, e + SLOTS)
            for i in range(YE):
                sp.wait_ge(y_sent[i], 16 * (EXPERTS // YE))
            for g in range(GROUPS):
                src = rows_out[4 * g * P:(4 * g + 4) * P, :].rearrange("(t p) d -> p t d", p=P)
                sp.dma_start(back[:, tiles(g), :], src).then_inc(back_loaded[g], 16)
            for g in range(GROUPS):
                sp.wait_ge(out_ready, g + 1)
                dst = out[:, 4 * g * P:(4 * g + 4) * P, :].rearrange("a (t p) d -> p (a t) d", p=P)
                sp.dma_start(dst, r[:, tiles(g), :]).then_inc(stored, 16)
            sp.wait_ge(stored, 16 * GROUPS)

        @block.gpsimd
        def _(pool):
            pool.memset(onesb[:], 1.0).then_inc(consts, 1)
            pool.iota(iota[:], [[1, EXPERTS]], base=0, channel_multiplier=0,
                      allow_small_or_imprecise_dtypes=True).then_inc(consts, 1)
            pool.wait_ge(consts, 2)
            pool.affine_select(out=tri[:], in_=onesb[:], compare_op=ALU.is_ge, fill=0.0, base=0,
                               pattern=[[1, P]], channel_multiplier=-1).then_inc(consts, 1)
            pool.wait_ge(consts, 3)
            for k in range(TILES):
                pool.wait_ge(slots_ready, k // 4 + 1)
                pool.indirect_dma_start(rows_in, bass.IndirectOffsetOnAxis(slotu[:, k:k + 1], 0), x3[:, k, :], None,
                                        bounds_check=S - 1, oob_is_err=False).then_inc(scattered, 16)
            for e in range(EXPERTS):
                pool.wait_ge(down_done, e + 1)
                pool.indirect_dma_start(rows_out, bass.IndirectOffsetOnAxis(xe[:, e, D:D + 1].bitcast(U32), 0),
                                        ye[e % YE][:], None, bounds_check=S - 1, oob_is_err=False)\
                    .then_inc(y_sent[e % YE], 16)

        @block.scalar
        def _(act):
            act.wait_ge(lm_ready, GROUPS)
            act.activation(ex[:], lm[:], ACT.Exp).then_inc(exp_done, 1)
            act.wait_ge(b1_turned, 1)
            act.activation(b1[:].rearrange("p e f -> p f e"), m.psum[:, 7, 0:FT * EXPERTS].rearrange("p (f e) -> p f e", e=EXPERTS),
                           ACT.Copy).then_inc(b1_placed, 1)
            for b in range(4):
                act.wait_ge(xe_turned, b + 1)
                act.activation(xet[:, b * G:(b + 1) * G], m.psum[:, b, :], ACT.Copy).then_inc(xe_placed, 1)
            act.wait_ge(b1_placed, 1)
            for e in range(EXPERTS):
                act.wait_ge(up_full, e + 1)
                if e > 1:
                    act.wait_ge(down_full, e - 1)
                for f in range(FT):
                    last = act.activation(h[e % 2][:, f, :], m.psum[:, 4 + e % 2, f * P:(f + 1) * P], ACT.Relu,
                                          bias=b1[:, e, f:f + 1])
                last.then_inc(up_done, 1)
            for g in range(GROUPS):
                act.wait_ge(last_asked, g + 1)
                act.activation(dev[:, tiles(g)], var[:, tiles(g)], ACT.Sqrt).then_inc(last_dev, 1)
                act.wait_ge(last_scale, g + 1)
                for k in range(4 * g, 4 * g + 4):
                    last = act.activation(r[:, k, :], r[:, k, :], ACT.Identity, scale=rstd[:, k:k + 1],
                                          bias=shift[:, k:k + 1])
                last.then_inc(out_ready, 1)

        @block.tensor
        def _(pe):
            def count(g):
                pe.wait_ge(hot_ready, g + 1)
                out = count_bank[g % 2]
                pe.matmul(out, tri[:], hot[:, tiles(g), :].rearrange("p a n -> p (a n)"), start=True, stop=False)
                for k in range(4 * g + 3):
                    first = max(0, k + 1 - 4 * g)
                    last = pe.matmul(out[:, first * EXPERTS:], onesb[:],
                                     hot[:, k:k + 1, :].broadcast_to([P, 4 - first, EXPERTS]),
                                     start=False, stop=(k == 4 * g + 2))
                last.then_inc(counted, 1)

            pe.wait_ge(consts, 3)
            for g in range(GROUPS):
                count(g)
            pe.wait_ge(loaded, 16)
            for f in range(FT):
                last = pe.transpose(m.psum[:, 7, f * EXPERTS:(f + 1) * EXPERTS], b1r[:, f * P:(f + 1) * P],
                                    m.ident[0:EXPERTS, 0:EXPERTS])
            last.then_inc(b1_turned, 1)
            for b in range(4):
                pe.wait_ge(xe_loaded[b], 16)
                for k in range(4):
                    last = pe.transpose(m.psum[:, b, k * P:(k + 1) * P], xe[:, 4 * b + k, 0:D], m.ident[:])
                last.then_inc(xe_turned, 1)
            pe.wait_ge(slots_ready, GROUPS)

            def up(e):
                if e > 1:
                    pe.wait_ge(up_done, e - 1)
                if e % 4 == 0:
                    pe.wait_ge(xe_placed, e // 4 + 1)
                pe.wait_ge(w_loaded[e % SLOTS], 32 * (e // SLOTS + 1))
                for f in range(FT):
                    last = pe.matmul(m.psum[:, 4 + e % 2, f * P:(f + 1) * P], w1[e % SLOTS][:, f * P:(f + 1) * P],
                                     xet[:, e * P:(e + 1) * P], start=True, stop=True)
                last.then_inc(up_full, 1)

            def down(e):
                pe.wait_ge(up_done, e + 1)
                if e > 1:
                    pe.wait_ge(down_done, e - 1)
                for f in range(FT):
                    last = pe.matmul(m.psum[:, 6 + e % 2, 0:D], h[e % 2][:, f, :], w2[e % SLOTS][:, f, :],
                                     start=(f == 0), stop=(f == FT - 1))
                last.then_inc(down_full, 1)

            up(0)
            for e in range(1, EXPERTS):
                up(e)
                down(e - 1)
            down(EXPERTS - 1)

        @block.vector
        def _(dve):
            c = Chain(dve, chain)

            def choose(g):
                s = tiles(g)
                c.step(dve.tensor_tensor(logit[:, s, :], m.psum[:, 5, 4 * g * EXPERTS:(4 * g + 4) * EXPERTS].rearrange("p (a n) -> p a n", n=EXPERTS),
                                         t.bg_b[:].unsqueeze(1).broadcast_to([P, 4, EXPERTS]), ALU.add))
                for k in range(4 * g, 4 * g + 4):
                    c.mark(dve.max(top[:, k, :], logit[:, k, :]))
                c.wait()
                for k in range(4 * g, 4 * g + 4):
                    c.mark(dve.max_index(topi[:, k, :], top[:, k, :], logit[:, k, :]))
                dve.tensor_tensor(lm[:, s, :], logit[:, s, :], top[:, s, 0:1].broadcast_to([P, 4, EXPERTS]),
                                  ALU.subtract).then_inc(lm_ready, 1)
                c.wait()
                c.step(dve.tensor_copy(idx[:, s], topi[:, s, 0]))
                dve.tensor_tensor(hot[:, s, :], iota[:].unsqueeze(1).broadcast_to([P, 4, EXPERTS]),
                                  idx[:, s].unsqueeze(2).broadcast_to([P, 4, EXPERTS]), ALU.is_equal)\
                    .then_inc(hot_ready, 1)

            def place(g):
                s = tiles(g)
                dve.wait_ge(counted, g + 1)
                dve.wait_ge(hot_ready, g + 1)
                c.step(dve.tensor_tensor(cnt[:, s, :], count_bank[g % 2].rearrange("p (a n) -> p a n", n=EXPERTS), hot[:, s, :], ALU.mult))
                c.step(dve.tensor_reduce(pos[:, s], cnt[:, s, :], AX, ALU.add))
                c.mark(dve.tensor_scalar(keep[:, s], pos[:, s], float(CAP), None, ALU.is_le))
                c.step(dve.tensor_scalar(slot[:, s], idx[:, s], float(CAP), 2.0 * S - 1.0, ALU.mult, ALU.add))
                c.step(dve.tensor_tensor(slot[:, s], slot[:, s], pos[:, s], ALU.add))
                c.step(dve.scalar_tensor_tensor(slot[:, s], keep[:, s], -2.0 * S, slot[:, s], ALU.mult, ALU.add))
                dve.tensor_copy(slotu[:, s], slot[:, s]).then_inc(slots_ready, 1)

            dve.wait_ge(consts, 3)
            choose(0)
            for g in range(GROUPS):
                if g + 1 < GROUPS:
                    choose(g + 1)
                place(g)
            dve.wait_ge(exp_done, 1)
            c.step(dve.tensor_reduce(gate[:], ex[:], AX, ALU.add))
            c.step(dve.reciprocal(gate[:], gate[:]))
            c.step(dve.tensor_tensor(gate[:], gate[:], keep[:], ALU.mult))
            for e in range(EXPERTS):
                dve.wait_ge(down_full, e + 1)
                if e >= YE:
                    dve.wait_ge(y_sent[e % YE], 16 * (e // YE))
                dve.tensor_tensor(ye[e % YE][:], m.psum[:, 6 + e % 2, 0:D], t.eb2[:, e, :], ALU.add).then_inc(down_done, 1)

            def last_norm(g):
                dve.wait_ge(back_loaded[g], 16)
                for k in range(4 * g, 4 * g + 4):
                    c.mark(dve.scalar_tensor_tensor(r[:, k, :], back[:, k, :], gate[:, k:k + 1], x3[:, k, 0:D],
                                                    ALU.mult, ALU.add))
                c.wait()
                for k in range(4 * g, 4 * g + 4):
                    c.mark(dve.bn_stats(stats[:, k, :], r[:, k, :]))
                c.wait()
                moments(dve, c, stats[:, tiles(g), :], mv[:, tiles(g), :])
                dve.tensor_scalar(var[:, tiles(g)], mv[:, tiles(g), 1], EPS, None, ALU.add).then_inc(last_asked, 1)

            def finish(g):
                dve.wait_ge(last_dev, g + 1)
                c.step(dve.reciprocal(rstd[:, tiles(g)], dev[:, tiles(g)]))
                dve.scalar_tensor_tensor(shift[:, tiles(g)], mv[:, tiles(g), 0], -1.0, rstd[:, tiles(g)], ALU.mult,
                                         ALU.mult).then_inc(last_scale, 1)

            for g in range(GROUPS):
                last_norm(g)
                finish(g)


INPUTS = ["L0_attn_x", "L0_attn_Wq", "L0_attn_Wk", "L0_attn_Wv", "L0_attn_Wo", "L0_attn_bo",
          "L0_ffn_W1", "L0_ffn_b1", "L0_ffn_W2", "L0_ffn_b2",
          "L1_attn_qkv_w", "L1_attn_qkv_alpha", "L1_attn_bias_q", "L1_attn_bias_k", "L1_attn_q_alpha",
          "L1_attn_q_zp", "L1_attn_k_alpha", "L1_attn_k_zp", "L1_attn_v_alpha", "L1_attn_v_zp",
          "L1_attn_attn_alpha", "L1_attn_attn_zp", "L1_attn_proj_w", "L1_attn_proj_b", "L1_attn_proj_alpha",
          "L1_ffn_Wg", "L1_ffn_bg", "L1_ffn_W1", "L1_ffn_b1", "L1_ffn_W2", "L1_ffn_b2"]


def build(nc, ins, out):
    with ExitStack() as kept:
        def sem(name):
            return kept.enter_context(nc.semaphore(name))

        with ExitStack() as ctx:
            m = Memory(nc, kept, ctx)
            early = sem("early")
            setup(nc, m, ins, early, sem)
            attention(nc, m, sem)
        t = Tail(nc, m, kept)
        t.w_loaded = [sem(f"w_loaded{i}") for i in range(SLOTS)]
        for phase in (lambda c: layer0_rest(nc, m, t, ins, early, sem), lambda c: attention1_check(nc, m, t, sem),
                      lambda c: attention1_general(nc, m, t, sem), lambda c: experts(nc, m, t, ins, out, sem)):
            with ExitStack() as ctx:
                t.scope(ctx)
                phase(ctx)


def kernel(**inputs):
    import concourse.bacc as bacc
    from concourse.bass_utils import run_bass_kernel_spmd

    nc = bacc.Bacc("TRN2", target_bir_lowering=False, num_devices=1)
    arrays, ins = {}, {}
    for name in INPUTS:
        a = np.ascontiguousarray(inputs[name])
        arrays[f"in_{name}"] = a
        ins[name] = nc.dram_tensor(f"in_{name}", a.shape, mybir.dt.from_np(a.dtype), kind="ExternalInput").ap()
    out = nc.dram_tensor("out_x", (1, S, D), F32, kind="ExternalOutput").ap()
    build(nc, ins, out)
    r = run_bass_kernel_spmd(nc, [arrays], core_ids=[0])
    return r.results[0]["out_x"]
```
